# Optimizing a Trainium2 kernel written in Bass

```python
import numpy as np
import jax
import jax.numpy as jnp

def _softmax(x, axis=-1):
    return jax.nn.softmax(x, axis=axis)

def _gelu(x):
    return jax.nn.gelu(x, approximate=True)

def _silu(x):
    return jax.nn.silu(x)

def _sigmoid(x):
    return jax.nn.sigmoid(x)

def _layernorm(x, axis=-1, eps=1e-05):
    m = jnp.mean(x, axis=axis, keepdims=True)
    v = jnp.var(x, axis=axis, keepdims=True)
    return (x - m) / jnp.sqrt(v + eps)

def _scatter_add(tgt, idx, src, axis=0):
    return tgt.at[idx].add(src)

def _segment_sum(src, seg, n):
    return jax.ops.segment_sum(src, seg, n)
kernel_name = 'mk_macaron_d1_jaxref_r4_27bbfe'

def setup_inputs(seed: int=0):
    np.random.seed(seed)
    _w = jnp.asarray

    def _L0_attn_setup():
        import jax, jax.numpy as jnp
        import numpy as np
        B, T, D = (1, 512, 512)
        H, DK, DV, M = (16, 64, 128, 64)
        KEY_DIM, VALUE_DIM = (H * DK, H * DV)
        EPS = 1e-05
        CLAMP_MIN, CLAMP_MAX = (-32.0, 32.0)
        XAVIER_GAIN = 2.0 ** (-2.5)

        def _chunk_abc(q, k, v, s):
            scale = q.shape[-1] ** (-0.5)
            z = jax.lax.cumlogsumexp(s, axis=2)
            g = jnp.exp(jnp.concatenate([z[:, :, :1], z[:, :, :-1]], axis=2) - z)
            p = jnp.exp(s - z)
            tfirst = lambda x: jnp.moveaxis(x, 2, 0)
            qT, kT, vT, pT, gT = map(tfirst, (q * scale, k, v, p, g))
            b, h = (q.shape[0], q.shape[1])
            hk0 = jnp.zeros((b, h, q.shape[-1], s.shape[-1]), q.dtype)

            def step_k(hk, x):
                q_t, k_t, p_t, g_t = x
                hk = hk * g_t[:, :, None, :] + k_t[..., None] * p_t[:, :, None, :]
                return (hk, jnp.einsum('bhk,bhkm->bhm', q_t, hk))
            _, okT = jax.lax.scan(step_k, hk0, (qT, kT, pT, gT))
            pvT = jax.nn.softmax(okT, axis=-1)
            hv0 = jnp.zeros((b, h, s.shape[-1], v.shape[-1]), q.dtype)

            def step_v(hv, x):
                pv_t, v_t, p_t, g_t = x
                hv = hv * g_t[..., None] + p_t[..., None] * v_t[:, :, None, :]
                return (hv, jnp.einsum('bhm,bhmv->bhv', pv_t, hv))
            _, ovT = jax.lax.scan(step_v, hv0, (pvT, vT, pT, gT))
            return jnp.moveaxis(ovT, 0, 2)
        key = jax.random.key(seed)
        ks = jax.random.split(key, 8)

        def w(k, fan_in, fan_out):
            std = XAVIER_GAIN * np.sqrt(2.0 / (fan_in + fan_out))
            return jax.random.normal(k, (fan_in, fan_out), jnp.float32) * std
        return {'hidden_states': jax.random.normal(ks[0], (B, T, D), jnp.float32), 'Wq': w(ks[1], D, KEY_DIM), 'Wk': w(ks[2], D, KEY_DIM), 'Wv': w(ks[3], D, VALUE_DIM), 'Wg': w(ks[4], D, VALUE_DIM), 'Ws': w(ks[5], D, H * M), 'Wo': w(ks[6], VALUE_DIM, D), 'g_norm_weight': jnp.ones((DV,), jnp.float32)}
    _L0_attn_in = _L0_attn_setup()

    def _L0_ffn_setup():
        import jax, jax.numpy as jnp
        import numpy as np
        DIM = 512
        HIDDEN = 2048
        NUM_EXPERTS = 2
        BATCH, SEQ = (4, 256)
        key = jax.random.key(seed)
        k1, k2, k3, k4 = jax.random.split(key, 4)
        x = jax.random.normal(k1, (BATCH, SEQ, DIM), dtype=jnp.float32)
        w_router = jax.random.normal(k2, (NUM_EXPERTS, DIM), dtype=jnp.float32) * (1.0 / np.sqrt(DIM))
        w_fc = jax.random.normal(k3, (NUM_EXPERTS, HIDDEN, DIM), dtype=jnp.float32) * (1.0 / np.sqrt(DIM))
        w_proj = jax.random.normal(k4, (NUM_EXPERTS, DIM, HIDDEN), dtype=jnp.float32) * (1.0 / np.sqrt(HIDDEN))
        return {'x': x, 'w_router': w_router, 'w_fc': w_fc, 'w_proj': w_proj}
    _L0_ffn_in = _L0_ffn_setup()
    _d = {'L0_attn_hidden_states': _L0_attn_in['hidden_states'], 'L0_attn_Wq': _L0_attn_in['Wq'], 'L0_attn_Wk': _L0_attn_in['Wk'], 'L0_attn_Wv': _L0_attn_in['Wv'], 'L0_attn_Wg': _L0_attn_in['Wg'], 'L0_attn_Ws': _L0_attn_in['Ws'], 'L0_attn_Wo': _L0_attn_in['Wo'], 'L0_attn_g_norm_weight': _L0_attn_in['g_norm_weight'], 'L0_ffn_w_router': _L0_ffn_in['w_router'], 'L0_ffn_w_fc': _L0_ffn_in['w_fc'], 'L0_ffn_w_proj': _L0_ffn_in['w_proj']}
    _x0 = _d['L0_attn_hidden_states']
    _d['L0_attn_hidden_states'] = jax.random.normal(jax.random.fold_in(jax.random.key(seed), 1), (2, 1024, 512), dtype=_x0.dtype)
    del _x0
    return _d

def reference(L0_attn_hidden_states, L0_attn_Wq, L0_attn_Wk, L0_attn_Wv, L0_attn_Wg, L0_attn_Ws, L0_attn_Wo, L0_attn_g_norm_weight, L0_ffn_w_router, L0_ffn_w_fc, L0_ffn_w_proj):

    def _L0_attn_ref(hidden_states, Wq, Wk, Wv, Wg, Ws, Wo, g_norm_weight):
        import jax, jax.numpy as jnp
        import numpy as np
        B, T, D = (1, 512, 512)
        H, DK, DV, M = (16, 64, 128, 64)
        KEY_DIM, VALUE_DIM = (H * DK, H * DV)
        EPS = 1e-05
        CLAMP_MIN, CLAMP_MAX = (-32.0, 32.0)
        XAVIER_GAIN = 2.0 ** (-2.5)

        def _chunk_abc(q, k, v, s):
            scale = q.shape[-1] ** (-0.5)
            z = jax.lax.cumlogsumexp(s, axis=2)
            g = jnp.exp(jnp.concatenate([z[:, :, :1], z[:, :, :-1]], axis=2) - z)
            p = jnp.exp(s - z)
            tfirst = lambda x: jnp.moveaxis(x, 2, 0)
            qT, kT, vT, pT, gT = map(tfirst, (q * scale, k, v, p, g))
            b, h = (q.shape[0], q.shape[1])
            hk0 = jnp.zeros((b, h, q.shape[-1], s.shape[-1]), q.dtype)

            def step_k(hk, x):
                q_t, k_t, p_t, g_t = x
                hk = hk * g_t[:, :, None, :] + k_t[..., None] * p_t[:, :, None, :]
                return (hk, jnp.einsum('bhk,bhkm->bhm', q_t, hk))
            _, okT = jax.lax.scan(step_k, hk0, (qT, kT, pT, gT))
            pvT = jax.nn.softmax(okT, axis=-1)
            hv0 = jnp.zeros((b, h, s.shape[-1], v.shape[-1]), q.dtype)

            def step_v(hv, x):
                pv_t, v_t, p_t, g_t = x
                hv = hv * g_t[..., None] + p_t[..., None] * v_t[:, :, None, :]
                return (hv, jnp.einsum('bhm,bhmv->bhv', pv_t, hv))
            _, ovT = jax.lax.scan(step_v, hv0, (pvT, vT, pT, gT))
            return jnp.moveaxis(ovT, 0, 2)
        b, t, _ = hidden_states.shape
        to_heads = lambda x, d: jnp.transpose(x.reshape(b, t, H, d), (0, 2, 1, 3))
        q = to_heads(hidden_states @ Wq, DK)
        k = to_heads(hidden_states @ Wk, DK)
        v = to_heads(hidden_states @ Wv, DV)
        s = jnp.clip(to_heads(hidden_states @ Ws, M), CLAMP_MIN, CLAMP_MAX)
        o = jnp.transpose(_chunk_abc(q, k, v, s), (0, 2, 1, 3))
        g = (hidden_states @ Wg).reshape(b, t, H, DV)
        o = o * jax.lax.rsqrt(jnp.mean(jnp.square(o), axis=-1, keepdims=True) + EPS) * g_norm_weight
        o = o * (g * jax.nn.sigmoid(g))
        return o.reshape(b, t, VALUE_DIM) @ Wo

    def _L0_ffn_ref(x, w_router, w_fc, w_proj):
        import jax, jax.numpy as jnp
        import numpy as np
        DIM = 512
        HIDDEN = 2048
        NUM_EXPERTS = 2
        BATCH, SEQ = (4, 256)
        bsz, seq, dim = x.shape
        num_experts = w_router.shape[0]
        x_flat = x.reshape(-1, dim)
        logits = x_flat @ w_router.T
        probs = jax.nn.softmax(logits, axis=-1)
        top_idx = jnp.argmax(probs, axis=-1)
        top_weight = jnp.take_along_axis(probs, top_idx[:, None], axis=1)[:, 0]
        h = jnp.einsum('nd,ehd->enh', x_flat, w_fc)
        a = jnp.square(jnp.where(h >= 0, h, 0.5 * h))
        expert_out = jnp.einsum('enh,edh->end', a, w_proj)
        mask = (top_idx[None, :] == jnp.arange(num_experts)[:, None]).astype(x.dtype)
        out = jnp.einsum('end,en->nd', expert_out, mask * top_weight[None, :])
        return out.reshape(bsz, seq, dim)
    x = L0_attn_hidden_states
    x = x + 0.5 * _L0_ffn_ref(_layernorm(x, axis=-1), L0_ffn_w_router, L0_ffn_w_fc, L0_ffn_w_proj)
    x = x + _L0_attn_ref(_layernorm(x, axis=-1), L0_attn_Wq, L0_attn_Wk, L0_attn_Wv, L0_attn_Wg, L0_attn_Ws, L0_attn_Wo, L0_attn_g_norm_weight)
    x = x + 0.5 * _L0_ffn_ref(_layernorm(x, axis=-1), L0_ffn_w_router, L0_ffn_w_fc, L0_ffn_w_proj)
    return x

_drawn_inputs = setup_inputs


def setup_inputs(seed=0):
    import zlib

    import numpy as np

    out = dict(_drawn_inputs(seed))
    spreads = {'L0_attn_g_norm_weight': (1.0, 0.6)}
    factors = {'L0_attn_Wq': 64.0,
     'L0_attn_Wk': 64.0,
     'L0_attn_Wv': 2.853,
     'L0_attn_Wg': 2.726,
     'L0_attn_Ws': 33.692}
    for name, (base, spread) in spreads.items():
        noise = np.random.default_rng([zlib.crc32(name.encode()), seed]).standard_normal(out[name].shape)
        drawn = base * np.exp(spread * noise) if base else spread * noise
        out[name] = jnp.asarray(drawn.astype(out[name].dtype))
    for name, factor in factors.items():
        out[name] = (out[name] * factor).astype(out[name].dtype)
    return out
```

```python
from contextlib import ExitStack

import concourse.bass as bass
from concourse import mybir

F32 = mybir.dt.float32
F32R = mybir.dt.float32r
I32 = mybir.dt.int32
ALU = mybir.AluOpType
ACT = mybir.ActivationFunctionType
AX = mybir.AxisListType

P = 128
BATCH, SEQ, D = 2, 1024, 512
TOK = BATCH * SEQ
TILES = TOK // P
KC = D // P
EPS = 1e-5

EXPERTS, HIDDEN = 2, 2048
HT = HIDDEN // P
GROUP = 512
GROUPS = TOK // GROUP
SLOTS = GROUPS + 1
GT = GROUP // P
RING = 4
GATHERS = 6
AHEAD = 2
assert HT % RING == 0

HEADS, DK, DV, M = 16, 64, 128, 64
PAIRS = HEADS // 2
CHUNK = P
UNIT = 512
UC = UNIT // CHUNK
UNITS = TOK // UNIT
HALVES = SEQ // UNIT
CLAMP = 32.0


def phase_constants(nc, top):
    c = {}
    c["ident"] = top.enter_context(nc.sbuf_tensor("ident", [P, P], F32))
    c["causal"] = top.enter_context(nc.sbuf_tensor("causal", [P, P], F32))
    c["ones"] = top.enter_context(nc.sbuf_tensor("ones", [P, P], F32))
    c["minus_half"] = top.enter_context(nc.sbuf_tensor("minus_half", [P, TILES], F32))
    const_set = top.enter_context(nc.semaphore("const_set"))
    const_done = top.enter_context(nc.semaphore("const_done"))
    with nc.Block() as block:
        @block.gpsimd
        def _(pool):
            pool.memset(c["ident"][:], 0.0).then_inc(const_set, 1)
            pool.memset(c["causal"][:], 1.0).then_inc(const_set, 1)
            pool.memset(c["ones"][:], 1.0)
            pool.memset(c["minus_half"][:], -0.5)
            pool.wait_ge(const_set, 2)
            pool.affine_select(out=c["ident"][:], in_=c["ident"][:], compare_op=ALU.not_equal, fill=1.0,
                               base=0, pattern=[[-1, P]], channel_multiplier=1).then_inc(const_done, 1)
            pool.affine_select(out=c["causal"][:], in_=c["causal"][:], compare_op=ALU.is_ge, fill=0.0,
                               base=0, pattern=[[1, P]], channel_multiplier=-1).then_inc(const_done, 1)
            pool.wait_ge(const_done, 2)
    return c


def phase_route(nc, top, tag, c, x_in, router, xres, half_weight, gather_row, slot_table, sorted_rows):
    with ExitStack() as ctx:
        sb = lambda n, s, d=F32: ctx.enter_context(nc.sbuf_tensor(tag + n, s, d))
        sem = lambda n: top.enter_context(nc.semaphore(tag + n))
        xn = sb("rt_xn", [P, TILES, D])
        rows = sb("rt_router", [P, EXPERTS, D])
        wdiff = sb("rt_wdiff", [P, D])
        prod = sb("rt_prod", [P, D])
        stats = sb("rt_stats", [P, TILES, 6])
        mv = sb("rt_mv", [P, TILES, 2])
        vare = sb("rt_vare", [P, TILES])
        rstd = sb("rt_rstd", [P, TILES])
        shift = sb("rt_shift", [P, TILES])
        gap = sb("rt_gap", [P, TILES])
        is1 = sb("rt_is1", [P, TILES])
        mag = sb("rt_mag", [P, TILES])
        em = sb("rt_em", [P, TILES])
        total = sb("rt_total", [P, TILES])
        cum = sb("rt_cum", [P, TILES])
        seen = sb("rt_seen", [P, TILES])
        zero = sb("rt_zero", [P, TILES])
        tok_i = sb("rt_tok_i", [P, TILES], I32)
        tok = sb("rt_tok", [P, TILES])
        pos0 = sb("rt_pos0", [P, TILES])
        pos = sb("rt_pos", [P, TILES])
        row_i = sb("rt_row_i", [P, TILES], I32)
        slot_i = sb("rt_slot_i", [P, 8], I32)
        slot = sb("rt_slot", [P, 8])
        border = sb("rt_border", [P, 4])
        table = sb("rt_table", [P, 2, 8])
        ps = ctx.enter_context(nc.psum_tensor(tag + "rt_ps", [P, 512], F32))
        x_loaded = [sem(f"rt_x_loaded{i}") for i in range(4)]
        r_loaded = sem("rt_r_loaded")
        iota_done = sem("rt_iota")
        var_ready = sem("rt_var_ready")
        rstd_done = sem("rt_rstd_done")
        shift_done = sem("rt_shift_done")
        xn_done = sem("rt_xn_done")
        mag_done = sem("rt_mag_done")
        em_done = sem("rt_em_done")
        is1_done = sem("rt_is1_done")
        rank_mm = sem("rt_rank_mm")
        rows_ready = sem("rt_rows_ready")
        scattered = sem("rt_scattered")
        dve_step = sem("rt_dve_step")
        block = ctx.enter_context(nc.Block())
        q = TILES // 4

        @block.sync
        def _(sp):
            if x_in is not None:
                for i in range(4):
                    sp.dma_start(xres[:, i * q:(i + 1) * q, :],
                                 x_in.rearrange("(i p) d -> p i d", p=P)[:, i * q:(i + 1) * q, :]).then_inc(x_loaded[i], 16)
            sp.dma_start(rows[:, :, :], router.rearrange("e d -> (e d)").partition_broadcast(P).rearrange("p (e d) -> p e d", e=EXPERTS)).then_inc(r_loaded, 16)

        @block.vector
        def _(dve):
            n = [0]

            def step(ins):
                n[0] += 1
                ins.then_inc(dve_step, 1)
                dve.wait_ge(dve_step, n[0])
            dve.memset(zero[:], 0.0)
            for i in range(TILES):
                if x_in is not None and i % q == 0:
                    dve.wait_ge(x_loaded[i // q], 16)
                step(dve.bn_stats(stats[:, i, :], xres[:, i, :]))
                last = dve.bn_aggr(mv[:, i, :], stats[:, i, :])
            step(last)
            dve.tensor_scalar(vare[:], mv[:, :, 1], EPS, None, ALU.add).then_inc(var_ready, 1)
            dve.wait_ge(r_loaded, 16)
            step(dve.tensor_tensor(wdiff[:], rows[:, 0, :], rows[:, 1, :], ALU.subtract))
            dve.wait_ge(rstd_done, 1)
            dve.scalar_tensor_tensor(out=shift[:], in0=mv[:, :, 0], scalar=-1.0, in1=rstd[:],
                                     op0=ALU.mult, op1=ALU.mult).then_inc(shift_done, 1)
            for i in range(TILES):
                dve.wait_ge(xn_done, i + 1)
                step(dve.tensor_tensor_reduce(out=prod[:], in0=xn[:, i, :], in1=wdiff[:], scale=1.0, scalar=0.0,
                                              op0=ALU.mult, op1=ALU.add, accum_out=gap[:, i:i + 1]))
            dve.tensor_scalar(is1[:], gap[:], 0.0, None, ALU.is_lt).then_inc(is1_done, 1)
            step(dve.tensor_scalar(mag[:], gap[:], -1.0, None, ALU.mult))
            dve.tensor_tensor(mag[:], mag[:], gap[:], ALU.max).then_inc(mag_done, 1)
            dve.wait_ge(iota_done, 2)
            dve.tensor_copy(slot[:], slot_i[:])
            step(dve.tensor_copy(tok[:], tok_i[:]))
            dve.wait_ge(em_done, 1)
            step(dve.tensor_scalar(em[:], em[:], 1.0, None, ALU.add))
            step(dve.reciprocal(half_weight[:], em[:]))
            step(dve.tensor_scalar(half_weight[:], half_weight[:], 0.5, None, ALU.mult))
            dve.wait_ge(rank_mm, 2)
            step(dve.tensor_copy(total[:], ps[:, TILES:2 * TILES]))
            step(dve.tensor_tensor_scan(out=cum[:], data0=total[:], data1=zero[:], initial=0.0, op0=ALU.add, op1=ALU.add))
            step(dve.tensor_tensor(seen[:], cum[:], total[:], ALU.subtract))
            step(dve.tensor_tensor(seen[:], ps[:, 0:TILES], seen[:], ALU.add))
            step(dve.tensor_tensor(pos0[:], tok[:], seen[:], ALU.subtract))
            step(dve.tensor_scalar(pos[:], seen[:], cum[:, TILES - 1:TILES], float(TOK - 1), ALU.subtract, ALU.add))
            step(dve.tensor_tensor(pos[:], pos[:], pos0[:], ALU.subtract))
            step(dve.tensor_tensor(pos[:], pos[:], is1[:], ALU.mult))
            step(dve.tensor_tensor(pos[:], pos[:], pos0[:], ALU.add))
            dve.tensor_copy(row_i[:], pos[:]).then_inc(rows_ready, 1)
            step(dve.scalar_tensor_tensor(out=pos[:], in0=is1[:], scalar=float(GROUP), in1=pos[:], op0=ALU.mult, op1=ALU.add))
            dve.tensor_copy(gather_row[:], pos[:])
            step(dve.tensor_scalar(border[:, 0:1], cum[:, TILES - 1:TILES], -1.0, float(TOK), ALU.mult, ALU.add))
            step(dve.tensor_scalar(border[:, 1:2], border[:, 0:1], float(GROUP), None, ALU.is_ge))
            for g in range(2, GROUPS):
                step(dve.tensor_scalar(border[:, 2:3], border[:, 0:1], float(g * GROUP), None, ALU.is_ge))
                step(dve.tensor_tensor(border[:, 1:2], border[:, 1:2], border[:, 2:3], ALU.add))
            step(dve.tensor_scalar(table[:, 0, :], slot[:], border[:, 1:2], None, ALU.is_gt))
            step(dve.tensor_tensor(table[:, 1, :], slot[:], table[:, 0, :], ALU.subtract))
            step(dve.tensor_scalar(table[:, 1, :], table[:, 1, :], float(GROUPS - 1), float(GROUP), ALU.min, ALU.mult))
            step(dve.tensor_scalar(table[:, 0, :], table[:, 0, :], float(HT), None, ALU.mult))
            step(dve.tensor_copy(slot_table[:], table[:]))

        @block.gpsimd
        def _(pool):
            pool.iota(tok_i[:], pattern=[[P, TILES]], base=0, channel_multiplier=1).then_inc(iota_done, 1)
            pool.iota(slot_i[:], pattern=[[1, 8]], base=0, channel_multiplier=0).then_inc(iota_done, 1)
            pool.wait_ge(var_ready, 1)
            pool.tensor_tensor(rstd[:], vare[:], c["minus_half"][:], ALU.pow).then_inc(rstd_done, 1)
            pool.wait_ge(rows_ready, 1)
            for i in range(TILES):
                pool.indirect_dma_start(out=sorted_rows, out_offset=bass.IndirectOffsetOnAxis(ap=row_i[:, i:i + 1], axis=0),
                                        in_=xn[:, i, :], in_offset=None).then_inc(scattered, 16)
            pool.wait_ge(scattered, 16 * TILES)

        @block.scalar
        def _(act):
            act.wait_ge(shift_done, 1)
            for i in range(TILES):
                act.activation(xn[:, i, :], xres[:, i, :], ACT.Identity, bias=shift[:, i:i + 1],
                               scale=rstd[:, i:i + 1]).then_inc(xn_done, 1)
            act.wait_ge(mag_done, 1)
            act.activation(em[:], mag[:], ACT.Exp, scale=-1.0).then_inc(em_done, 1)

        @block.tensor
        def _(pe):
            pe.wait_ge(is1_done, 1)
            pe.matmul(ps[:, 0:TILES], c["causal"][:], is1[:], start=True, stop=True).then_inc(rank_mm, 1)
            pe.matmul(ps[:, TILES:2 * TILES], c["ones"][:], is1[:], start=True, stop=True).then_inc(rank_mm, 1)


def phase_experts(nc, top, tag, c, wff, slot_table, sorted_rows, slot_rows):
    with ExitStack() as ctx:
        sb = lambda n, s, d=F32: ctx.enter_context(nc.sbuf_tensor(tag + n, s, d))
        sem = lambda n: top.enter_context(nc.semaphore(tag + n))
        stage = sb("ff_stage", [P, RING, 2 * D])
        w_hi = sb("ff_w_hi", [P, RING, 2 * D], F32R)
        w_lo = sb("ff_w_lo", [P, RING, 2 * D], F32R)
        xg = sb("ff_xg", [P, GT, D])
        xT_hi = sb("ff_xT_hi", [P, KC, GROUP], F32R)
        xT_lo = sb("ff_xT_lo", [P, KC, GROUP], F32R)
        square = sb("ff_square", [P, RING, GROUP])
        factor = sb("ff_factor", [P, RING, GROUP])
        a = sb("ff_a", [P, RING, GROUP])
        a_hi = sb("ff_a_hi", [P, RING, GROUP], F32R)
        a_lo = sb("ff_a_lo", [P, RING, GROUP], F32R)
        y = sb("ff_y", [P, GT, D])
        ps_y = [ctx.enter_context(nc.psum_tensor(f"{tag}ff_ps_y{t}", [P, D], F32)) for t in range(GT)]
        ps_h = [ctx.enter_context(nc.psum_tensor(f"{tag}ff_ps_h{t}", [P, GROUP], F32)) for t in range(2)]
        ps_x = [ctx.enter_context(nc.psum_tensor(f"{tag}ff_ps_x{t}", [P, GROUP], F32)) for t in range(2)]
        w_loaded = [sem(f"ff_w_loaded{r}") for r in range(RING)]
        x_loaded = sem("ff_x_loaded")
        w_hi_done = sem("ff_w_hi_done")
        w_lo_done = sem("ff_w_lo_done")
        x_turned = sem("ff_x_turned")
        x_hi_done = sem("ff_x_hi_done")
        x_lo_done = sem("ff_x_lo_done")
        up_done = sem("ff_up_done")
        square_done = sem("ff_square_done")
        factor_done = sem("ff_factor_done")
        a_done = sem("ff_a_done")
        a_hi_done = sem("ff_a_hi_done")
        a_lo_done = sem("ff_a_lo_done")
        down_done = sem("ff_down_done")
        y_act = sem("ff_y_act")
        y_dve = sem("ff_y_dve")
        y_stored = sem("ff_y_stored")
        y_free = sem("ff_y_free")
        block = ctx.enter_context(nc.Block())

        @block.sync
        def _(sp):
            def load_group(s):
                row = sp.value_load(slot_table[0:1, 1, bass.ds(s, 1)], min_val=0, max_val=TOK - GROUP)
                sp.dma_start(xg[:, :, :], sorted_rows[bass.ds(row, GROUP), :].rearrange("(i p) d -> p i d", p=P)).then_inc(x_loaded, 16)
            load_group(0)
            with sp.Fori(0, SLOTS) as j:
                sp.wait_ge(x_turned, j * KC + KC)
                load_group(j + 1)
                tile0 = sp.value_load(slot_table[0:1, 0, bass.ds(j, 1)], min_val=0, max_val=HT)
                for t in range(HT):
                    sp.wait_ge(w_hi_done, j * HT + t + 1)
                    sp.wait_ge(w_lo_done, j * HT + t + 1)
                    sp.dma_start(stage[:, t % RING, :], wff[bass.ds(tile0 + t, 1), :, :].rearrange("a p n -> (a p) n")).then_inc(w_loaded[t % RING], 16)

        @block.gpsimd
        def _(pool):
            pool.sem_inc(y_free, 1)
            with pool.Fori(0, SLOTS) as j:
                pool.wait_ge(y_act, j * 2 + 3)
                pool.wait_ge(y_dve, j * 2 + 3)
                pool.dma_start(slot_rows[bass.ds(j * GROUP, GROUP), :].rearrange("(i p) d -> p i d", p=P), y[:, :, :]).then_inc(y_stored, 16)
                pool.wait_ge(y_stored, j * 16 + 16)
                pool.sem_inc(y_free, 1)

        @block.scalar
        def _(act):
            def split_x(g):
                for k in range(KC):
                    act.wait_ge(x_turned, g * KC + k + 1)
                    act.activation(xT_hi[:, k, :], ps_x[k % 2][:, :], ACT.Copy).then_inc(x_hi_done, 1)
            act.sem_inc(w_hi_done, RING)
            act.sem_inc(y_act, 1)
            act.sem_inc(square_done, 2)
            split_x(0)
            with act.Fori(0, SLOTS) as j:
                def split_w(t):
                    act.wait_ge(w_loaded[t % RING], (j * (HT // RING) + t // RING + 1) * 16)
                    act.wait_ge(down_done, j * HT + t + 1)
                    act.activation(w_hi[:, t % RING, :], stage[:, t % RING, :], ACT.Copy).then_inc(w_hi_done, 1)
                for t in range(AHEAD):
                    split_w(t)
                for t in range(HT):
                    r = t % RING
                    if t + AHEAD < HT:
                        split_w(t + AHEAD)
                    act.wait_ge(up_done, j * HT + t + 1)
                    act.activation(square[:, r, :], ps_h[t % 2][:, :], ACT.Square).then_inc(square_done, 1)
                    act.wait_ge(a_done, j * HT + t + 1)
                    act.activation(a_hi[:, r, :], a[:, r, :], ACT.Copy).then_inc(a_hi_done, 1)
                split_x(j + 1)
                act.wait_ge(y_free, j + 1)
                act.wait_ge(down_done, j * HT + HT + RING)
                for i in range(0, GT, 2):
                    act.activation(y[:, i, :], ps_y[i][:, :], ACT.Copy).then_inc(y_act, 1)

        @block.vector
        def _(dve):
            def split_x(g):
                for k in range(KC):
                    dve.wait_ge(x_hi_done, g * KC + k + 1)
                    dve.tensor_tensor(xT_lo[:, k, :], ps_x[k % 2][:, :], xT_hi[:, k, :].bitcast(F32), ALU.subtract).then_inc(x_lo_done, 1)
            dve.sem_inc(w_lo_done, RING)
            dve.sem_inc(y_dve, 1)
            dve.sem_inc(factor_done, 2)
            split_x(0)
            with dve.Fori(0, SLOTS) as j:
                def split_w(t):
                    dve.wait_ge(w_hi_done, j * HT + t + 1 + RING)
                    dve.tensor_tensor(w_lo[:, t % RING, :], stage[:, t % RING, :], w_hi[:, t % RING, :].bitcast(F32),
                                      ALU.subtract).then_inc(w_lo_done, 1)
                for t in range(AHEAD):
                    split_w(t)
                for t in range(HT):
                    r = t % RING
                    if t + AHEAD < HT:
                        split_w(t + AHEAD)
                    dve.wait_ge(square_done, j * HT + t + 3)
                    dve.tensor_scalar(factor[:, r, :], ps_h[t % 2][:, :], 0.0, 0.25, ALU.is_ge, ALU.max).then_inc(factor_done, 1)
                    dve.wait_ge(factor_done, j * HT + t + 3)
                    dve.tensor_tensor(a[:, r, :], square[:, r, :], factor[:, r, :], ALU.mult).then_inc(a_done, 1)
                    dve.wait_ge(a_hi_done, j * HT + t + 1)
                    dve.tensor_tensor(a_lo[:, r, :], a[:, r, :], a_hi[:, r, :].bitcast(F32), ALU.subtract).then_inc(a_lo_done, 1)
                split_x(j + 1)
                dve.wait_ge(y_free, j + 1)
                dve.wait_ge(down_done, j * HT + HT + RING)
                for i in range(1, GT, 2):
                    dve.tensor_copy(y[:, i, :], ps_y[i][:, :]).then_inc(y_dve, 1)

        @block.tensor
        def _(pe):
            def turn_x(g, waited, k0, k1):
                if k0 == 0:
                    pe.wait_ge(x_loaded, g * 16 + 16)
                for k in range(k0, k1):
                    if waited:
                        pe.wait_ge(x_lo_done, g * KC + k - 1)
                    elif k >= 2:
                        pe.wait_ge(x_lo_done, k - 1)
                    for i in range(GT):
                        last = pe.transpose(ps_x[k % 2][:, i * P:(i + 1) * P], xg[:, i, k * P:(k + 1) * P], c["ident"][:])
                    last.then_inc(x_turned, 1)
            pe.sem_inc(down_done, RING)
            turn_x(0, False, 0, KC)
            with pe.Fori(0, SLOTS) as j:
                def up(t):
                    r = t % RING
                    if t == 0:
                        pe.wait_ge(x_lo_done, j * KC + KC)
                    pe.wait_ge(w_lo_done, j * HT + t + 1 + RING)
                    pe.wait_ge(square_done, j * HT + t + 1)
                    pe.wait_ge(factor_done, j * HT + t + 1)
                    parts = ((w_lo, xT_hi), (w_hi, xT_lo), (w_hi, xT_hi))
                    for k in range(KC):
                        for n, (w, x) in enumerate(parts):
                            last = pe.matmul(ps_h[t % 2][:, :], w[:, r, k * P:(k + 1) * P], x[:, k, :],
                                             start=(k == 0 and n == 0), stop=(k == KC - 1 and n == 2))
                    last.then_inc(up_done, 1)

                def down(t):
                    r = t % RING
                    pe.wait_ge(a_lo_done, j * HT + t + 1)
                    if t == 0:
                        pe.wait_ge(y_act, j * 2 + 1)
                        pe.wait_ge(y_dve, j * 2 + 1)
                    for i in range(GT):
                        for n, (x, w) in enumerate(((a_lo, w_hi), (a_hi, w_lo), (a_hi, w_hi))):
                            last = pe.matmul(ps_y[i][:, :], x[:, r, i * P:(i + 1) * P], w[:, r, D:2 * D],
                                             start=(t == 0 and n == 0), stop=(t == HT - 1 and n == 2))
                    last.then_inc(down_done, 1)
                for t in range(AHEAD):
                    up(t)
                for t in range(HT):
                    if t + AHEAD < HT:
                        up(t + AHEAD)
                    if t == HT - 2:
                        turn_x(j + 1, True, 0, 2)
                    if t == HT - 1:
                        turn_x(j + 1, True, 2, KC)
                    down(t)


def phase_gather(nc, top, tag, slot_rows, gather_row, half_weight, xres, y_out):
    with ExitStack() as ctx:
        sem = lambda n: top.enter_context(nc.semaphore(tag + n))
        rows = ctx.enter_context(nc.sbuf_tensor(tag + "ga_rows", [P, TILES, D], F32))
        loaded = [sem(f"ga_loaded{i}") for i in range(GATHERS)]
        added = sem("ga_added")
        stored = sem("ga_stored")
        block = ctx.enter_context(nc.Block())

        @block.gpsimd
        def _(pool):
            for i in range(TILES):
                if i >= GATHERS:
                    pool.wait_ge(added, i - GATHERS + 1)
                pool.indirect_dma_start(out=rows[:, i, :], out_offset=None, in_=slot_rows,
                                        in_offset=bass.IndirectOffsetOnAxis(ap=gather_row[:, i:i + 1], axis=0)).then_inc(loaded[i % GATHERS], 16)

        @block.vector
        def _(dve):
            for i in range(TILES):
                dve.wait_ge(loaded[i % GATHERS], 16 * (i // GATHERS + 1))
                dve.scalar_tensor_tensor(out=xres[:, i, :], in0=rows[:, i, :], scalar=half_weight[:, i:i + 1],
                                         in1=xres[:, i, :], op0=ALU.mult, op1=ALU.add).then_inc(added, 1)

        @block.sync
        def _(sp):
            if y_out is None:
                return
            for i in range(TILES):
                sp.wait_ge(added, i + 1)
                sp.dma_start(y_out[i * P:(i + 1) * P, :], xres[:, i, :]).then_inc(stored, 16)
            sp.wait_ge(stored, 16 * TILES)


def phase_turn(nc, top, c, xres, xT_hi, xT_lo):
    with ExitStack() as ctx:
        sb = lambda n, s, d=F32: ctx.enter_context(nc.sbuf_tensor(n, s, d))
        sem = lambda n: top.enter_context(nc.semaphore(n))
        xn = sb("tu_xn", [P, GT, D])
        stats = sb("tu_stats", [P, TILES, 6])
        mv = sb("tu_mv", [P, TILES, 2])
        vare = sb("tu_vare", [P, TILES])
        rstd = sb("tu_rstd", [P, TILES])
        shift = sb("tu_shift", [P, TILES])
        ps = [ctx.enter_context(nc.psum_tensor(f"tu_ps{k}", [P, UNIT], F32)) for k in range(8)]
        dve_step = sem("tu_dve_step")
        var_ready = sem("tu_var_ready")
        rstd_done = sem("tu_rstd_done")
        shift_done = sem("tu_shift_done")
        xn_done = sem("tu_xn_done")
        turned = sem("tu_turned")
        hi_done = sem("tu_hi_done")
        lo_done = sem("tu_lo_done")
        block = ctx.enter_context(nc.Block())

        @block.gpsimd
        def _(pool):
            pool.wait_ge(var_ready, 1)
            pool.tensor_tensor(rstd[:], vare[:], c["minus_half"][:], ALU.pow).then_inc(rstd_done, 1)

        @block.vector
        def _(dve):
            n = 0
            for i in range(TILES):
                dve.bn_stats(stats[:, i, :], xres[:, i, :]).then_inc(dve_step, 1)
                n += 1
                dve.wait_ge(dve_step, n)
                last = dve.bn_aggr(mv[:, i, :], stats[:, i, :])
            last.then_inc(dve_step, 1)
            dve.wait_ge(dve_step, n + 1)
            dve.tensor_scalar(vare[:], mv[:, :, 1], EPS, None, ALU.add).then_inc(var_ready, 1)
            dve.wait_ge(rstd_done, 1)
            dve.scalar_tensor_tensor(out=shift[:], in0=mv[:, :, 0], scalar=-1.0, in1=rstd[:],
                                     op0=ALU.mult, op1=ALU.mult).then_inc(shift_done, 1)
            for u in range(UNITS):
                for k in range(KC):
                    dve.wait_ge(hi_done, u * KC + k + 1)
                    dve.tensor_tensor(xT_lo[:, k, u * UNIT:(u + 1) * UNIT], ps[(u * KC + k) % 8][:, :],
                                      xT_hi[:, k, u * UNIT:(u + 1) * UNIT].bitcast(F32), ALU.subtract).then_inc(lo_done, 1)

        @block.scalar
        def _(act):
            act.wait_ge(shift_done, 1)
            for u in range(UNITS):
                if u > 0:
                    act.wait_ge(turned, u * KC)
                for i in range(UC):
                    t = u * UC + i
                    act.activation(xn[:, i, :], xres[:, t, :], ACT.Identity, bias=shift[:, t:t + 1],
                                   scale=rstd[:, t:t + 1]).then_inc(xn_done, 1)
                for k in range(KC):
                    act.wait_ge(turned, u * KC + k + 1)
                    act.activation(xT_hi[:, k, u * UNIT:(u + 1) * UNIT], ps[(u * KC + k) % 8][:, :], ACT.Copy).then_inc(hi_done, 1)

        @block.tensor
        def _(pe):
            for u in range(UNITS):
                pe.wait_ge(xn_done, (u + 1) * UC)
                for k in range(KC):
                    n = u * KC + k
                    if n >= 8:
                        pe.wait_ge(lo_done, n - 7)
                    for i in range(UC):
                        last = pe.transpose(ps[n % 8][:, i * P:(i + 1) * P], xn[:, i, k * P:(k + 1) * P], c["ident"][:])
                    last.then_inc(turned, 1)



QKS = KC * 3 * P
VG = KC * 4 * P
WO = 2 * D
PIECE = 1024
HK_STEPS = [UC if k % HALVES == 0 else UC - 1 for k in range(UNITS)]
HK_AT = [sum(HK_STEPS[:k]) for k in range(UNITS + 1)]
PIECES = [(0, 768), (768, 768), (QKS, PIECE), (QKS + PIECE, PIECE), (QKS + VG, WO)]


def phase_attention(nc, top, c, watt, gnorm, xres):
    with ExitStack() as ctx:
        xT_hi = ctx.enter_context(nc.sbuf_tensor("at_xT_hi", [P, KC, TOK], F32R))
        xT_lo = ctx.enter_context(nc.sbuf_tensor("at_xT_lo", [P, KC, TOK], F32R))
        phase_turn(nc, top, c, xres, xT_hi, xT_lo)
        phase_heads(nc, top, c, watt, gnorm, xres, xT_hi, xT_lo)


def phase_heads(nc, top, c, watt, gnorm, xres, xT_hi, xT_lo):
    with ExitStack() as ctx:
        sb = lambda n, s, d=F32: ctx.enter_context(nc.sbuf_tensor(n, s, d))
        sem = lambda n: top.enter_context(nc.semaphore(n))
        stage = sb("at_stage", [P, PIECE])
        w_hi = sb("at_w_hi", [P, QKS + VG + WO], F32R)
        w_lo = sb("at_w_lo", [P, QKS + VG + WO], F32R)
        gn = sb("at_gn", [DV, 1])
        qT = sb("at_qT", [P, 2, UNIT])
        kT = sb("at_kT", [P, UNIT])
        eT = sb("at_eT", [P, 2, UNIT])
        zT = sb("at_zT", [P, UNIT])
        zlast = sb("at_zlast", [P, 1])
        v = sb("at_v", [P, 2, UC, 2 * DV])
        gate = sb("at_gate", [P, 2, UC, 2 * DV])
        en = sb("at_en", [P, UC, P])
        kn = sb("at_kn", [P, UC, P])
        rz = sb("at_rz", [P, UC, P])
        am = sb("at_am", [P, 2, UC, P])
        hk = sb("at_hk", [P, UC, P])
        hv = sb("at_hv", [P, UC, 2 * DV])
        ok = sb("at_ok", [P, UC, P])
        pv = sb("at_pv", [P, UC, P])
        pT = sb("at_pT", [P, UNIT])
        u = sb("at_u", [P, 2, UC, DV])
        uT_hi = sb("at_uT_hi", [P, 2, 2, 2 * P], F32R)
        uT_lo = sb("at_uT_lo", [P, 2, 2, 2 * P], F32R)
        highest = sb("at_highest", [P, 2 * UC])
        den = sb("at_den", [P, 2 * UC])
        ss = sb("at_ss", [P, 2 * UC])
        ms = sb("at_ms", [P, 2 * UC])
        coef = sb("at_coef", [P, 2 * UC])
        PJ = [ctx.enter_context(nc.psum_tensor(f"at_pj{b}", [P, 512], F32)) for b in range(2)]
        R = [ctx.enter_context(nc.psum_tensor(f"at_r{b}", [P, 512], F32)) for b in range(6)]

        gn_loaded = sem("at_gn_loaded")
        piece_loaded = sem("at_piece_loaded")
        piece_scaled = sem("at_piece_scaled")
        piece_hi = sem("at_piece_hi")
        piece_lo = sem("at_piece_lo")
        q_mm, k_mm, s_mm, vg_mm = sem("at_q_mm"), sem("at_k_mm"), sem("at_s_mm"), sem("at_vg_mm")
        q_out, k_out, s_clipped, e_done, z_done = sem("at_q_out"), sem("at_k_out"), sem("at_s_clipped"), sem("at_e_done"), sem("at_z_done")
        z_kept = sem("at_z_kept")
        v_out, tanh_done, gate_done = sem("at_v_out"), sem("at_tanh_done"), sem("at_gate_done")
        e_tr, k_tr, z_tr = sem("at_e_tr"), sem("at_k_tr"), sem("at_z_tr")
        en_out, kn_out, rz_done = sem("at_en_out"), sem("at_kn_out"), sem("at_rz_done")
        dk_mm, hk_done = sem("at_dk_mm"), sem("at_hk_done")
        a_mm, a_masked = sem("at_a_mm"), sem("at_a_masked")
        ok_mm, ok_scaled, highest_done, ok_shifted = sem("at_ok_mm"), sem("at_ok_scaled"), sem("at_highest_done"), sem("at_ok_shifted")
        pv_done, den_done, pz_done = sem("at_pv_done"), sem("at_den_done"), sem("at_pz_done")
        p_tr, p_out = sem("at_p_tr"), sem("at_p_out")
        b_mm, b_masked = sem("at_b_mm"), sem("at_b_masked")
        dv_mm, hv_done = sem("at_dv_mm"), sem("at_hv_done")
        o_mm, squared, ss_done, eps_done, ms_done, coef_done, u_done = (
            sem("at_o_mm"), sem("at_squared"), sem("at_ss_done"), sem("at_eps_done"), sem("at_ms_done"), sem("at_coef_done"), sem("at_u_done"))
        u_tr, u_hi, u_lo = sem("at_u_tr"), sem("at_u_hi"), sem("at_u_lo")
        wo_mm, added = sem("at_wo_mm"), sem("at_added")
        block = ctx.enter_context(nc.Block())
        NP = len(PIECES)

        wq = lambda w, k, part: w[:, k * 3 * P + part * P:k * 3 * P + (part + 1) * P]
        wvg = lambda w, k: w[:, QKS + k * 4 * P:QKS + (k + 1) * 4 * P]
        wo = lambda w, h: w[:, QKS + VG + h * D:QKS + VG + (h + 1) * D]

        def count(i, k, per, done):
            return i * (UNITS * per) + (k * per + done + 1)

        @block.sync
        def _(sp):
            sp.dma_start(gn[:, :], gnorm).then_inc(gn_loaded, 16)
            for n in range(4):
                if n > 0:
                    sp.wait_ge(piece_lo, n + 1)
                sp.dma_start(stage[:, 0:PIECES[n][1]], watt[0, :, PIECES[n][0]:PIECES[n][0] + PIECES[n][1]]).then_inc(piece_loaded, 16)

            def load(i, n, pair, piece):
                col, width = PIECES[piece]
                sp.wait_ge(piece_lo, i * NP + n + 4 + 1)
                sp.dma_start(stage[:, 0:width], watt[bass.ds(pair, 1), :, col:col + width].rearrange("a p n -> (a p) n")).then_inc(piece_loaded, 16)
            with sp.Fori(0, PAIRS - 1) as i:
                load(i, 0, i, 4)
                for n in range(4):
                    load(i, n + 1, i + 1, n)
            load(PAIRS - 1, 0, PAIRS - 1, 4)

        @block.gpsimd
        def _(pool):
            pool.sem_inc(piece_lo, 1)
            pool.sem_inc(coef_done, 1)

            def lo_piece(n, piece):
                col, width = PIECES[piece]
                pool.wait_ge(piece_hi, n + 1)
                pool.tensor_tensor(w_lo[:, col:col + width], stage[:, 0:width], w_hi[:, col:col + width].bitcast(F32),
                                   ALU.subtract).then_inc(piece_lo, 1)
            pool.wait_ge(gn_loaded, 16)
            for n in range(4):
                lo_piece(n, n)

            def pair(i, last):
                def norm(k):
                    pool.wait_ge(ms_done, count(i, k, 2, 2))
                    pool.tensor_tensor(coef[:, :], ms[:, :], c["minus_half"][:, 0:2 * UC], ALU.pow).then_inc(coef_done, 1)
                pool.wait_ge(piece_loaded, i * (NP * 16) + 5 * 16)
                pool.tensor_tensor(stage[:, 0:WO], stage[:, 0:WO], gn[:, 0:1].to_broadcast([P, WO]), ALU.mult).then_inc(piece_scaled, 1)
                lo_piece(i * NP + 4, 4)
                norm(0)
                norm(1)
                if not last:
                    lo_piece(i * NP + 5, 0)
                norm(2)
                if not last:
                    for n in range(1, 4):
                        lo_piece(i * NP + 5 + n, n)
                norm(3)
            with pool.Fori(0, PAIRS - 1) as i:
                pair(i, False)
            pair(PAIRS - 1, True)

        @block.scalar
        def _(act):
            for s in (q_out, e_done, v_out, tanh_done, en_out, pv_done, p_out, squared, u_hi):
                act.sem_inc(s, 1)

            def hi_piece(n, piece):
                col, width = PIECES[piece]
                act.wait_ge(piece_scaled if piece == 4 else piece_loaded, n)
                act.activation(w_hi[:, col:col + width], stage[:, 0:width], ACT.Copy).then_inc(piece_hi, 1)

            def q_scale(i, k):
                act.wait_ge(q_mm, count(i, k, 1, 0))
                act.activation(qT[:, k % 2, :], PJ[(7 * k) % 2][:, :], ACT.Copy, scale=float(DK) ** -0.5).then_inc(q_out, 1)

            def e_exp(i, k):
                act.wait_ge(s_clipped, count(i, k, 1, 1))
                act.activation(eT[:, k % 2, :], eT[:, k % 2, :], ACT.Exp).then_inc(e_done, 1)

            def vg_read(i, k, t):
                bank = PJ[(7 * k + 3 + t) % 2]
                act.wait_ge(vg_mm, count(i, k, UC, t))
                act.activation(v[:, k % 2, t, :], bank[:, 0:2 * DV], ACT.Copy).then_inc(v_out, 1)
                act.activation(gate[:, k % 2, t, :], bank[:, 2 * DV:4 * DV], ACT.Tanh, scale=0.5).then_inc(tanh_done, 1)
            for n in range(4):
                hi_piece((n + 1) * 16, n)
            q_scale(0, 0)
            e_exp(0, 0)
            for t in range(UC):
                vg_read(0, 0, t)

            def pair(i, last):
                for k in range(UNITS):
                    more = not last or k < UNITS - 1
                    act.wait_ge(e_tr, count(i, k, 1, 0))
                    act.activation(en[:, :, :], R[0][:, :].rearrange("p (a b) -> p a b", a=UC), ACT.Copy).then_inc(en_out, 1)
                    if more:
                        q_scale(i, k + 1)
                    if k == 0:
                        act.wait_ge(wo_mm, count(i, k, UC, 0))
                        hi_piece(i + 1, 4)
                    if k == UNITS - 1 and more:
                        hi_piece(i * (NP * 16) + 9 * 16, 3)
                    act.wait_ge(ok_shifted, count(i, k, 1, 1))
                    act.activation(pv[:, :, :], ok[:, :, :], ACT.Exp).then_inc(pv_done, 1)
                    if more:
                        e_exp(i, k + 1)
                        vg_read(i, k + 1, 0)
                    act.wait_ge(p_tr, count(i, k, 1, 0))
                    act.activation(pT[:, :], R[3][:, :], ACT.Copy).then_inc(p_out, 1)
                    if more:
                        vg_read(i, k + 1, 1)
                    if k == UNITS - 2 and not last:
                        act.wait_ge(s_mm, count(i, k + 1, 1, 0))
                        hi_piece(i * (NP * 16) + 6 * 16, 0)
                    for b in range(2):
                        act.wait_ge(o_mm, count(i, k, 2, b))
                        act.activation(u[:, b, :, :].rearrange("p a d -> p (a d)"), R[b][:, :], ACT.Square).then_inc(squared, 1)
                    if more:
                        vg_read(i, k + 1, 2)
                    if k == UNITS - 2 and not last:
                        hi_piece(i * (NP * 16) + 7 * 16, 1)
                    if more:
                        vg_read(i, k + 1, 3)
                    for b in range(2):
                        act.wait_ge(u_tr, count(i, k, 2, b))
                        act.activation(uT_hi[:, b, :, :].rearrange("p h t -> p (h t)"), R[2 + b][:, :], ACT.Copy).then_inc(u_hi, 1)
                    if k == UNITS - 2 and not last:
                        hi_piece(i * (NP * 16) + 8 * 16, 2)
            with act.Fori(0, PAIRS - 1) as i:
                pair(i, False)
            pair(PAIRS - 1, True)

        @block.vector
        def _(dve):
            for s in (k_out, s_clipped, z_done, gate_done, kn_out, rz_done, hk_done, a_masked, ok_scaled, highest_done, ok_shifted,
                      den_done, pz_done, b_masked, hv_done, ss_done, eps_done, ms_done, u_done, u_lo, added):
                dve.sem_inc(s, 1)
            dve.memset(hk[:, :, :], 0.0)

            def k_copy(i, k):
                dve.wait_ge(k_mm, count(i, k, 1, 0))
                dve.tensor_copy(kT[:, :], PJ[(7 * k + 1) % 2][:, :]).then_inc(k_out, 1)

            def s_clip(i, k):
                dve.wait_ge(s_mm, count(i, k, 1, 0))
                dve.tensor_scalar(eT[:, k % 2, :], PJ[(7 * k + 2) % 2][:, :], CLAMP, -CLAMP, ALU.min, ALU.max).then_inc(s_clipped, 1)

            def z_scan(i, k):
                dve.wait_ge(e_done, count(i, k, 1, 1))
                first = k % HALVES == 0
                if not first:
                    dve.wait_ge(z_kept, i * (UNITS // HALVES) + k // HALVES + 1)
                dve.tensor_tensor_scan(out=zT[:, :], data0=eT[:, k % 2, :], data1=eT[:, k % 2, :],
                                       initial=0.0 if first else zlast[:, 0:1], op0=ALU.add, op1=ALU.bypass).then_inc(z_done, 1)
                if first:
                    dve.wait_ge(z_done, count(i, k, 1, 1))
                    dve.tensor_copy(zlast[:, :], zT[:, UNIT - 1:UNIT]).then_inc(z_kept, 1)

            def gate_make(i, k, t):
                dve.wait_ge(tanh_done, count(i, k, UC, t + 1))
                dve.scalar_tensor_tensor(out=gate[:, k % 2, t, :], in0=gate[:, k % 2, t, :], scalar=1.0,
                                         in1=PJ[(7 * k + 3 + t) % 2][:, 2 * DV:4 * DV], op0=ALU.add, op1=ALU.mult).then_inc(gate_done, 1)
            k_copy(0, 0)
            s_clip(0, 0)
            z_scan(0, 0)
            for t in range(UC):
                gate_make(0, 0, t)

            def pair(i, last_pair):
                for k in range(UNITS):
                    more = not last_pair or k < UNITS - 1
                    first = k % HALVES == 0
                    dve.wait_ge(k_tr, count(i, k, 1, 0))
                    dve.tensor_copy(kn[:, :, :], R[1][:, :].rearrange("p (a b) -> p a b", a=UC)).then_inc(kn_out, 1)
                    dve.wait_ge(z_tr, count(i, k, 1, 0))
                    dve.reciprocal(rz[:, :, :], R[2][:, :].rearrange("p (a b) -> p a b", a=UC)).then_inc(rz_done, 1)
                    dve.wait_ge(dk_mm, count(i, k, 1, 0))
                    for cc in range(UC if first else UC - 1):
                        to = (cc + 1) % UC
                        for h in range(2):
                            rows, cols = slice(64 * h, 64 * h + 64), slice(64 * h, 64 * h + 64)
                            part = R[5][rows, cc * P + 64 * h:cc * P + 64 * h + 64]
                            if first and cc == 0:
                                last = dve.tensor_copy(hk[rows, to, cols], part)
                            else:
                                last = dve.tensor_tensor(hk[rows, to, cols], part, hk[rows, cc, cols], ALU.add)
                        last.then_inc(hk_done, 1)
                        dve.wait_ge(hk_done, i * HK_AT[UNITS] + HK_AT[k] + cc + 2)
                    for b in range(2):
                        dve.wait_ge(a_mm, count(i, k, 2, b))
                        dve.tensor_tensor(am[:, b, :, :],
                                          R[3 + b][:, :].rearrange("p (a t) -> p a t", a=4),
                                          c["causal"][:, :].rearrange("p (a t) -> p a t", a=1).to_broadcast([P, 4, P]), ALU.mult).then_inc(a_masked, 1)
                    if more:
                        k_copy(i, k + 1)
                    dve.wait_ge(ok_mm, count(i, k, 1, 0))
                    dve.wait_ge(rz_done, count(i, k, 1, 1))
                    dve.tensor_tensor(ok[:, :, :], R[2][:, :].rearrange("p (a b) -> p a b", a=UC), rz[:, :, :], ALU.mult).then_inc(ok_scaled, 1)
                    dve.wait_ge(ok_scaled, count(i, k, 1, 1))
                    by_head = lambda x: x[:, :, :].rearrange("p a (h m) -> p (a h) m", h=2)
                    spread = lambda x: x[:, :].rearrange("p (a b) -> p a b", b=1).to_broadcast([P, 2 * UC, M])
                    dve.tensor_reduce(highest[:, :], by_head(ok), op=ALU.max, axis=AX.X).then_inc(highest_done, 1)
                    dve.wait_ge(highest_done, count(i, k, 1, 1))
                    dve.tensor_tensor(by_head(ok), by_head(ok), spread(highest), ALU.subtract).then_inc(ok_shifted, 1)
                    dve.wait_ge(pv_done, count(i, k, 1, 1))
                    dve.tensor_tensor(ok[:, :, :], pv[:, :, :], rz[:, :, :], ALU.mult).then_inc(pz_done, 1)
                    if more:
                        s_clip(i, k + 1)
                    dve.tensor_reduce(den[:, :], pv[:, :, :].rearrange("p a (h m) -> p h a m", h=2), op=ALU.add, axis=AX.X).then_inc(den_done, 1)
                    if more:
                        gate_make(i, k + 1, 0)
                    dve.wait_ge(den_done, count(i, k, 1, 1))
                    dve.scalar_tensor_tensor(out=ms[:, :], in0=den[:, :], scalar=4.0 * EPS, in1=den[:, :], op0=ALU.mult, op1=ALU.mult).then_inc(eps_done, 1)
                    for b in range(2):
                        dve.wait_ge(b_mm, count(i, k, 2, b))
                        dve.tensor_tensor(am[:, b, :, :],
                                          R[4 + b][:, :].rearrange("p (a t) -> p a t", a=4),
                                          c["causal"][:, :].rearrange("p (a t) -> p a t", a=1).to_broadcast([P, 4, P]), ALU.mult).then_inc(b_masked, 1)
                    for cc in range(UC if first else UC - 1):
                        to = (cc + 1) % UC
                        if cc % 2 == 0:
                            dve.wait_ge(dv_mm, count(i, k, 2, cc // 2))
                        part = R[2 + cc // 2][:, (cc % 2) * 2 * DV:(cc % 2 + 1) * 2 * DV]
                        if first and cc == 0:
                            last = dve.tensor_copy(hv[:, to, :], part)
                        else:
                            last = dve.tensor_tensor(hv[:, to, :], part, hv[:, cc, :], ALU.add)
                        last.then_inc(hv_done, 1)
                        dve.wait_ge(hv_done, i * HK_AT[UNITS] + HK_AT[k] + cc + 2)
                    if more:
                        gate_make(i, k + 1, 1)
                        z_scan(i, k + 1)
                    dve.wait_ge(eps_done, count(i, k, 1, 1))
                    for b in range(2):
                        cols = slice(4 * b, 4 * b + 4)
                        dve.wait_ge(squared, count(i, k, 2, b + 1))
                        dve.tensor_reduce(ss[:, cols], u[:, b, :, :], op=ALU.add, axis=AX.X).then_inc(ss_done, 1)
                        dve.wait_ge(ss_done, count(i, k, 2, b + 1))
                        dve.scalar_tensor_tensor(out=ms[:, cols], in0=ss[:, cols], scalar=4.0 / DV, in1=ms[:, cols], op0=ALU.mult, op1=ALU.add).then_inc(ms_done, 1)
                    dve.wait_ge(coef_done, count(i, k, 1, 1))
                    for b in range(2):
                        for cc, h in ((2 * b, 0), (2 * b, 1), (2 * b + 1, 0), (2 * b + 1, 1)):
                            last = dve.scalar_tensor_tensor(out=u[:, h, cc, :], in0=R[h][:, cc * P:(cc + 1) * P], scalar=coef[:, 4 * h + cc:4 * h + cc + 1],
                                                            in1=gate[:, k % 2, cc, h * DV:(h + 1) * DV], op0=ALU.mult, op1=ALU.mult)
                        last.then_inc(u_done, 1)
                    if more:
                        gate_make(i, k + 1, 2)
                    for b in range(2):
                        dve.wait_ge(u_hi, count(i, k, 2, b + 1))
                        dve.tensor_tensor(uT_lo[:, b, :, :].rearrange("p h t -> p (h t)"), R[2 + b][:, :],
                                          uT_hi[:, b, :, :].rearrange("p h t -> p (h t)").bitcast(F32), ALU.subtract).then_inc(u_lo, 1)
                    if more:
                        gate_make(i, k + 1, 3)
                    for cc in range(UC):
                        dve.wait_ge(wo_mm, count(i, k, UC, cc + 1))
                        dve.tensor_tensor(xres[:, k * UC + cc, :], R[4 + cc % 2][:, :], xres[:, k * UC + cc, :], ALU.add).then_inc(added, 1)
            with dve.Fori(0, PAIRS - 1) as i:
                pair(i, False)
            pair(PAIRS - 1, True)

        @block.tensor
        def _(pe):
            parts = ((w_lo, xT_hi), (w_hi, xT_lo), (w_hi, xT_hi))

            def turned(i, k, part, done):
                tok = slice((k % UNITS) * UNIT, (k % UNITS + 1) * UNIT)
                for kk in range(KC):
                    for n, (w, x) in enumerate(parts):
                        last = pe.matmul(PJ[(7 * k + part) % 2][:, :], wq(w, kk, part), x[:, kk, tok],
                                         start=(kk == 0 and n == 0), stop=(kk == KC - 1 and n == 2))
                last.then_inc(done, 1)

            def project_q(i, k):
                pe.wait_ge(gate_done, count(i, k, UC, -1))
                turned(i, k, 0, q_mm)

            def project_k(i, k):
                pe.wait_ge(gate_done, count(i, k, UC, 0))
                turned(i, k, 1, k_mm)

            def project_s(i, k):
                pe.wait_ge(q_out, count(i, k, 1, 1))
                turned(i, k, 2, s_mm)

            def project_vg(i, k, t):
                if t == 0:
                    pe.wait_ge(k_out, count(i, k, 1, 1))
                elif t == 1:
                    pe.wait_ge(s_clipped, count(i, k, 1, 1))
                else:
                    pe.wait_ge(gate_done, count(i, k, UC, t - 1))
                tok = slice((k % UNITS) * UNIT + t * P, (k % UNITS) * UNIT + (t + 1) * P)
                for kk in range(KC):
                    for n, (w, x) in enumerate(parts):
                        last = pe.matmul(PJ[(7 * k + 3 + t) % 2][:, :], x[:, kk, tok], wvg(w, kk),
                                         start=(kk == 0 and n == 0), stop=(kk == KC - 1 and n == 2))
                last.then_inc(vg_mm, 1)
            pe.sem_inc(wo_mm, 1)
            pe.wait_ge(piece_lo, 1 + 2)
            turned(0, 0, 0, q_mm)
            turned(0, 0, 1, k_mm)
            project_s(0, 0)
            pe.wait_ge(piece_lo, 1 + 4)
            for t in range(UC):
                project_vg(0, 0, t)

            chunk = lambda cc: slice(cc * P, (cc + 1) * P)
            half = lambda h: slice(64 * h, 64 * h + 64)

            def turn_ek(i, k):
                pe.wait_ge(e_done, count(i, k, 1, 1))
                for cc in range(UC):
                    last = pe.transpose(R[0][:, chunk(cc)], eT[:, k % 2, chunk(cc)], c["ident"][:])
                last.then_inc(e_tr, 1)
                pe.wait_ge(k_out, count(i, k, 1, 1))
                for cc in range(UC):
                    last = pe.transpose(R[1][:, chunk(cc)], kT[:, chunk(cc)], c["ident"][:])
                last.then_inc(k_tr, 1)
            turn_ek(0, 0)

            def pair(i, last_pair):
                for k in range(UNITS):
                    more = not last_pair or k < UNITS - 1
                    first = k % HALVES == 0
                    b2 = k % 2
                    pe.wait_ge(z_done, count(i, k, 1, 1))
                    pe.wait_ge(u_lo, count(i, k, 2, 0))
                    for cc in range(UC):
                        last = pe.transpose(R[2][:, chunk(cc)], zT[:, chunk(cc)], c["ident"][:])
                    last.then_inc(z_tr, 1)
                    if k == UNITS - 1 and more:
                        pe.wait_ge(piece_lo, i * NP + 1 + 7)
                    if more:
                        project_q(i, k + 1)
                    pe.wait_ge(en_out, count(i, k, 1, 1))
                    pe.wait_ge(kn_out, count(i, k, 1, 1))
                    pe.wait_ge(added, count(i, k, UC, 0))
                    for cc in range(UC):
                        last = pe.matmul(R[5][:, chunk(cc)], kn[:, cc, :], en[:, cc, :], start=True, stop=True)
                    last.then_inc(dk_mm, 1)
                    pe.wait_ge(q_out, count(i, k, 1, 1))
                    for cc in range(UC):
                        for h in range(2):
                            last = pe.matmul(R[3 + h][:, chunk(cc)], kT[half(h), chunk(cc)], qT[half(h), b2, chunk(cc)], start=True, stop=True)
                            if cc == UC - 1:
                                last.then_inc(a_mm, 1)
                    if more:
                        project_k(i, k + 1)
                    pe.wait_ge(rz_done, count(i, k, 1, 1))
                    pe.wait_ge(hk_done, i * HK_AT[UNITS] + HK_AT[k + 1] + 1)
                    pe.wait_ge(a_masked, count(i, k, 2, 2))
                    for cc in range(UC):
                        state = not (first and cc == 0)
                        if state:
                            pe.matmul(R[2][:, chunk(cc)], qT[:, b2, chunk(cc)], hk[:, cc, :], start=True, stop=False, skip_group_check=True)
                        for h in range(2):
                            last = pe.matmul(R[2][:, cc * P + 64 * h:cc * P + 64 * h + 64], am[:, h, cc, :], en[:, cc, half(h)],
                                             start=not state, stop=True, skip_group_check=True)
                    last.then_inc(ok_mm, 1)
                    if more:
                        project_s(i, k + 1)
                    if k == UNITS - 1 and more:
                        pe.wait_ge(piece_lo, i * NP + 1 + 9)
                    if more:
                        project_vg(i, k + 1, 0)
                    pe.wait_ge(pz_done, count(i, k, 1, 1))
                    for cc in range(UC):
                        last = pe.transpose(R[3][:, chunk(cc)], ok[:, cc, :], c["ident"][:])
                    last.then_inc(p_tr, 1)
                    if more:
                        project_vg(i, k + 1, 1)
                    pe.wait_ge(p_out, count(i, k, 1, 1))
                    for cc in range(UC):
                        for h in range(2):
                            last = pe.matmul(R[4 + h][:, chunk(cc)], eT[half(h), b2, chunk(cc)], pT[half(h), chunk(cc)], start=True, stop=True)
                            if cc == UC - 1:
                                last.then_inc(b_mm, 1)
                    pe.wait_ge(v_out, count(i, k, UC, UC))
                    for b in range(2):
                        for a in range(2):
                            cc = 2 * b + a
                            last = pe.matmul(R[2 + b][:, a * 2 * DV:(a + 1) * 2 * DV], en[:, cc, :], v[:, b2, cc, :], start=True, stop=True)
                        last.then_inc(dv_mm, 1)
                    for h in range(2):
                        pe.wait_ge(b_masked, count(i, k, 2, h + 1))
                        for cc in range(UC):
                            last = pe.matmul(R[h][:, chunk(cc)], am[:, h, cc, :], v[:, b2, cc, h * DV:(h + 1) * DV],
                                             start=(cc == 0), stop=(first and cc == 0), skip_group_check=True)
                    pe.wait_ge(hv_done, i * HK_AT[UNITS] + HK_AT[k + 1] + 1)
                    for h in range(2):
                        for cc in range(1 if first else 0, UC):
                            last = pe.matmul(R[h][:, chunk(cc)], pT[half(h), chunk(cc)], hv[half(h), cc, h * DV:(h + 1) * DV],
                                             start=False, stop=True, skip_group_check=True)
                        last.then_inc(o_mm, 1)
                    if more:
                        project_vg(i, k + 1, 2)
                        project_vg(i, k + 1, 3)
                    for b in range(2):
                        pe.wait_ge(u_done, count(i, k, 2, b + 1))
                        for h in range(2):
                            for a in range(2):
                                last = pe.transpose(R[2 + b][:, (2 * h + a) * P:(2 * h + a + 1) * P], u[:, h, 2 * b + a, :], c["ident"][:])
                        last.then_inc(u_tr, 1)
                    if more:
                        turn_ek(i, k + 1)
                    if k == 0:
                        pe.wait_ge(piece_lo, i * NP + 1 + 5)
                    for cc in range(UC):
                        if cc % 2 == 0:
                            pe.wait_ge(u_lo, count(i, k, 2, cc // 2 + 1))
                        if cc >= 2:
                            pe.wait_ge(added, count(i, k, UC, cc - 1))
                        for h in range(2):
                            for n, (x, w) in enumerate(((uT_lo, w_hi), (uT_hi, w_lo), (uT_hi, w_hi))):
                                last = pe.matmul(R[4 + cc % 2][:, :], x[:, cc // 2, h, (cc % 2) * P:(cc % 2 + 1) * P], wo(w, h),
                                                 start=(h == 0 and n == 0), stop=(h == 1 and n == 2))
                        last.then_inc(wo_mm, 1)
            with pe.Fori(0, PAIRS - 1) as i:
                pair(i, False)
            pair(PAIRS - 1, True)


def macaron(nc, x, wff, router, watt, gnorm, out):
    sorted_rows = nc.dram_tensor("sorted_rows", [TOK, D], F32, kind="Internal").ap()
    slot_rows = nc.dram_tensor("slot_rows", [SLOTS * GROUP, D], F32, kind="Internal").ap()
    with ExitStack() as top:
        sb = lambda n, s, d=F32: top.enter_context(nc.sbuf_tensor(n, s, d))
        c = phase_constants(nc, top)
        xres = sb("xres", [P, TILES, D])
        half_weight = sb("half_weight", [P, TILES])
        gather_row = sb("gather_row", [P, TILES], I32)
        slot_table = sb("slot_table", [P, 2, 8], I32)

        def feed_forward(tag, x_in, y_out):
            phase_route(nc, top, tag, c, x_in, router, xres, half_weight, gather_row, slot_table, sorted_rows)
            phase_experts(nc, top, tag, c, wff, slot_table, sorted_rows, slot_rows)
            phase_gather(nc, top, tag, slot_rows, gather_row, half_weight, xres, y_out)
        feed_forward("first_", x, None)
        phase_attention(nc, top, c, watt, gnorm, xres)
        feed_forward("last_", None, out)


def kernel(**inputs):
    import numpy as np
    import concourse.bacc as bacc
    from concourse.bass_utils import run_bass_kernel_spmd

    get = lambda name: np.asarray(inputs[name])
    x = get("L0_attn_hidden_states")
    up = get("L0_ffn_w_fc").reshape(EXPERTS, HT, P, KC, P).transpose(0, 1, 4, 3, 2).reshape(EXPERTS * HT, P, D)
    down = get("L0_ffn_w_proj").reshape(EXPERTS, D, HT, P).transpose(0, 2, 3, 1).reshape(EXPERTS * HT, P, D)

    def pair_columns(w, width):
        return w.reshape(KC, P, PAIRS, 2 * width).transpose(2, 1, 0, 3)
    qks = np.concatenate([pair_columns(get("L0_attn_" + n), d) for n, d in (("Wq", DK), ("Wk", DK), ("Ws", M))], axis=3)
    vg = np.concatenate([pair_columns(get("L0_attn_" + n), DV) for n in ("Wv", "Wg")], axis=3)
    wo = get("L0_attn_Wo").reshape(PAIRS, 2, DV, D).transpose(0, 2, 1, 3)
    arrays = {
        "x": x.reshape(TOK, D),
        "wff": np.concatenate([up, down], axis=2),
        "router": get("L0_ffn_w_router"),
        "watt": np.concatenate([a.reshape(PAIRS, P, -1) for a in (qks, vg, wo)], axis=2),
        "gnorm": get("L0_attn_g_norm_weight").reshape(DV, 1),
    }
    arrays = {n: np.ascontiguousarray(a) for n, a in arrays.items()}
    nc = bacc.Bacc("TRN2", target_bir_lowering=False, num_devices=1)
    args = [nc.dram_tensor(n, a.shape, mybir.dt.from_np(a.dtype), kind="ExternalInput").ap() for n, a in arrays.items()]
    out = nc.dram_tensor("out", [TOK, D], F32, kind="ExternalOutput").ap()
    macaron(nc, *args, out)
    result = run_bass_kernel_spmd(nc, [arrays], core_ids=[0])
    return result.results[0]["out"].reshape(x.shape)
```

```python
from contextlib import ExitStack

import concourse.bass as bass
from concourse import mybir

F32 = mybir.dt.float32
F32R = mybir.dt.float32r
I32 = mybir.dt.int32
ALU = mybir.AluOpType
ACT = mybir.ActivationFunctionType
AX = mybir.AxisListType

P = 128
BATCH, SEQ, D = 2, 1024, 512
TOK = BATCH * SEQ
TILES = TOK // P
KC = D // P
EPS = 1e-5

EXPERTS, HIDDEN = 2, 2048
HT = HIDDEN // P
GROUP = 512
GROUPS = TOK // GROUP
SLOTS = GROUPS + 1
BLOCK = GROUP // 2
BLOCKS = TOK // BLOCK
GT = GROUP // P
RT = 4
RING = 4
GATHERS = 6
AHEAD = 2
assert HT % RING == 0

HEADS, DK, DV, M = 16, 64, 128, 64
PAIRS = HEADS // 2
CHUNK = P
UNIT = 512
UC = UNIT // CHUNK
UNITS = TOK // UNIT
HALVES = SEQ // UNIT
CLAMP = 32.0

QKS = KC * 3 * P
VG = KC * 4 * P
WO = 2 * D
PIECE = 1024
PIECES = [(0, QKS // 2), (QKS // 2, QKS // 2), (QKS, PIECE), (QKS + PIECE, PIECE), (QKS + VG, WO)]


def phase_constants(nc, top):
    c = {}
    c["ident"] = top.enter_context(nc.sbuf_tensor("ident", [P, P], F32))
    c["causal"] = top.enter_context(nc.sbuf_tensor("causal", [P, P], F32))
    c["ones"] = top.enter_context(nc.sbuf_tensor("ones", [P, P], F32))
    c["later"] = top.enter_context(nc.sbuf_tensor("later", [P, P], F32))
    c["minus_half"] = top.enter_context(nc.sbuf_tensor("minus_half", [P, TILES], F32))
    const_set = top.enter_context(nc.semaphore("const_set"))
    const_done = top.enter_context(nc.semaphore("const_done"))
    with nc.Block() as block:
        @block.gpsimd
        def _(pool):
            pool.memset(c["ident"][:], 0.0).then_inc(const_set, 1)
            pool.memset(c["causal"][:], 1.0).then_inc(const_set, 1)
            pool.memset(c["later"][:], 1.0).then_inc(const_set, 1)
            pool.memset(c["ones"][:], 1.0)
            pool.memset(c["minus_half"][:], -0.5)
            pool.wait_ge(const_set, 3)
            pool.affine_select(out=c["ident"][:], in_=c["ident"][:], compare_op=ALU.not_equal, fill=1.0,
                               base=0, pattern=[[-1, P]], channel_multiplier=1).then_inc(const_done, 1)
            pool.affine_select(out=c["causal"][:], in_=c["causal"][:], compare_op=ALU.is_ge, fill=0.0,
                               base=0, pattern=[[1, P]], channel_multiplier=-1).then_inc(const_done, 1)
            pool.affine_select(out=c["later"][:], in_=c["later"][:], compare_op=ALU.is_gt, fill=0.0,
                               base=0, pattern=[[-1, P]], channel_multiplier=1).then_inc(const_done, 1)
            pool.wait_ge(const_done, 3)
    return c


def phase_feed_forward(nc, top, tag, c, x_in, router, wff, watt, xres, mv, aw, half_weight, gather_row, slot_table, sorted_rows, slot_rows):
    with ExitStack() as ctx:
        sb = lambda n, s, d=F32: ctx.enter_context(nc.sbuf_tensor(tag + n, s, d))
        sem = lambda n: top.enter_context(nc.semaphore(tag + n))
        rows = sb("rt_router", [P, EXPERTS, D])
        wdiff = sb("rt_wdiff", [P, D])
        stats = sb("rt_stats", [P, TILES, 6])
        vare = sb("rt_vare", [P, TILES])
        nmean = sb("rt_nmean", [P, TILES])
        rstd = sb("rt_rstd", [P, TILES])
        shift = sb("rt_shift", [P, TILES])
        gap = sb("rt_gap", [P, TILES])
        is1 = sb("rt_is1", [P, TILES])
        mag = sb("rt_mag", [P, TILES])
        em = sb("rt_em", [P, TILES])
        cum = sb("rt_cum", [P, TILES])
        zero = sb("rt_zero", [P, TILES])
        tok_i = sb("rt_tok_i", [P, TILES], I32)
        tok = sb("rt_tok", [P, TILES])
        rest = sb("rt_rest", [P, TILES])
        base = sb("rt_base", [P, TILES])
        behind = sb("rt_behind", [P, TILES])
        pos = sb("rt_pos", [P, TILES])
        row_i = sb("rt_row_i", [P, TILES], I32)
        slot_i = sb("rt_slot_i", [P, BLOCKS], I32)
        slot = sb("rt_slot", [P, BLOCKS])
        blocks = sb("rt_blocks", [P, BLOCKS])
        border = sb("rt_border", [P, 6])
        inside = sb("rt_inside", [P, TILES])
        table = sb("rt_table", [P, 2, 8])
        in_loaded = [sem(f"rt_in_loaded{i}") for i in range(TILES // RT)] if x_in is not None else []
        r_loaded = sem("rt_r_loaded")
        iota_done = sem("rt_iota")
        var_ready = sem("rt_var_ready")
        rstd_done = sem("rt_rstd_done")
        shift_done = sem("rt_shift_done")
        xn_done = sem("rt_xn_done")
        mag_done = sem("rt_mag_done")
        em_done = sem("rt_em_done")
        is1_done = sem("rt_is1_done")
        rank_mm = sem("rt_rank_mm")
        rows_ready = sem("rt_rows_ready")
        scattered = sem("rt_scattered")
        table_ready = sem("rt_table_ready")
        dve_step = sem("rt_dve_step")
        stage = sb("ff_stage", [P, RING, 2 * D])
        w_hi = sb("ff_w_hi", [P, RING, 2 * D], F32R)
        w_lo = sb("ff_w_lo", [P, RING, 2 * D], F32R)
        xg = sb("ff_xg", [P, GT, D])
        xT_hi = sb("ff_xT_hi", [P, KC, GROUP], F32R)
        xT_lo = sb("ff_xT_lo", [P, KC, GROUP], F32R)
        square = sb("ff_square", [P, 2, GROUP])
        factor = sb("ff_factor", [P, 2, GROUP])
        a = sb("ff_a", [P, 2, GROUP])
        a_hi = sb("ff_a_hi", [P, RING, GROUP], F32R)
        a_lo = sb("ff_a_lo", [P, RING, GROUP], F32R)
        y = sb("ff_y", [P, GT, D])
        xn_rest = sb("ff_xn_rest", [P, TILES - 2 * GT - 2, D])
        ps_y = [ctx.enter_context(nc.psum_tensor(f"{tag}ff_ps_y{t}", [P, D], F32)) for t in range(GT)]
        ps_h = [ctx.enter_context(nc.psum_tensor(f"{tag}ff_ps_h{t}", [P, GROUP], F32)) for t in range(2)]
        ps_x = [ctx.enter_context(nc.psum_tensor(f"{tag}ff_ps_x{t}", [P, GROUP], F32)) for t in range(2)]
        ps_later, ps_total = ps_y[0][:, 0:TILES], ps_y[0][:, TILES:2 * TILES]
        w_loaded = [sem(f"ff_w_loaded{r}") for r in range(RING)]
        x_loaded = sem("ff_x_loaded")
        w_hi_done = sem("ff_w_hi_done")
        w_lo_done = sem("ff_w_lo_done")
        x_turned = sem("ff_x_turned")
        x_hi_done = sem("ff_x_hi_done")
        x_lo_done = sem("ff_x_lo_done")
        up_done = sem("ff_up_done")
        square_done = sem("ff_square_done")
        factor_done = sem("ff_factor_done")
        a_done = sem("ff_a_done")
        a_hi_done = sem("ff_a_hi_done")
        a_lo_done = sem("ff_a_lo_done")
        down_done = sem("ff_down_done")
        y_act = sem("ff_y_act")
        y_dve = sem("ff_y_dve")
        y_stored = sem("ff_y_stored")
        y_free = sem("ff_y_free")
        block = ctx.enter_context(nc.Block())
        steps = range(TILES // RT)
        tiles = lambda g: slice(g * RT, (g + 1) * RT)
        piece_step = HT // (len(PIECES) - 1)
        takes_piece = lambda j, t: x_in is not None and isinstance(j, int) and j == GROUPS - 1 and t % piece_step == 0

        def normed(i):
            for room in (xg, y, a):
                if i < room.shape[1]:
                    return room[:, i, :]
                i -= room.shape[1]
            return xn_rest[:, i, :]

        def all_slots(engine, slot_body):
            with engine.Fori(0, GROUPS - 1) as j:
                slot_body(j, GROUP, GROUP)
            slot_body(GROUPS - 1, GROUP, BLOCK)
            slot_body(GROUPS, BLOCK, 0)

        @block.sync
        def _(sp):
            if x_in is not None:
                for g in steps:
                    sp.dma_start(xres[:, tiles(g), :], x_in.rearrange("(i p) d -> p i d", p=P)[:, tiles(g), :]).then_inc(in_loaded[g], 16)
                    if g == 0:
                        sp.dma_start(rows[:, :, :], router.rearrange("e d -> (e d)").partition_broadcast(P).rearrange("p (e d) -> p e d", e=EXPERTS)).then_inc(r_loaded, 16)
            else:
                sp.dma_start(rows[:, :, :], router.rearrange("e d -> (e d)").partition_broadcast(P).rearrange("p (e d) -> p e d", e=EXPERTS)).then_inc(r_loaded, 16)

            def load_w(tile0, t):
                sp.dma_start(stage[:, t % RING, :], wff[bass.ds(tile0 + t % HT, 1), :, :].rearrange("a p n -> (a p) n")).then_inc(w_loaded[t % RING], 16)
            sp.wait_ge(table_ready, 1)
            first = sp.value_load(slot_table[0:1, 0, 0:1], min_val=0, max_val=HT)
            for t in range(AHEAD):
                load_w(first, t)
            sp.wait_ge(scattered, 16 * TILES)
            sp.dma_start(xg[:, :, :], sorted_rows[0:GROUP, :].rearrange("(i p) d -> p i d", p=P)).then_inc(x_loaded, 16)
            for t in range(AHEAD, RING):
                load_w(first, t)

            def slot_body(j, width, after):
                tile0 = sp.value_load(slot_table[0:1, 0, bass.ds(j, 1)], min_val=0, max_val=HT)
                if after:
                    tile0_next = sp.value_load(slot_table[0:1, 0, bass.ds(j + 1, 1)], min_val=0, max_val=HT)
                for t in range(RING, HT + RING):
                    if after and t == 2 * RING:
                        sp.wait_ge(x_turned, j * KC + KC)
                        if after == GROUP:
                            row = (j + 1) * GROUP
                        else:
                            row = sp.value_load(slot_table[0:1, 1, GROUPS:SLOTS], min_val=0, max_val=TOK - BLOCK)
                        sp.dma_start(xg[:, 0:after // P, :], sorted_rows[bass.ds(row, after), :].rearrange("(i p) d -> p i d", p=P)).then_inc(x_loaded, 16)
                    if takes_piece(j, t):
                        piece = t // piece_step - 1
                        col, width_p = PIECES[piece]
                        if piece > 0:
                            sp.wait_ge(aw["piece_lo"], piece + 1)
                        sp.dma_start(aw["stage"][:, 0:width_p], watt[0, :, col:col + width_p]).then_inc(aw["piece_loaded"], 16)
                    if after or t < HT:
                        sp.wait_ge(w_hi_done, j * HT + t + 1)
                        sp.wait_ge(w_lo_done, j * HT + t + 1)
                        load_w(tile0 if t < HT else tile0_next, t)
            all_slots(sp, slot_body)

        @block.gpsimd
        def _(pool):
            pool.iota(tok_i[:], pattern=[[P, TILES]], base=0, channel_multiplier=1).then_inc(iota_done, 1)
            pool.iota(slot_i[:], pattern=[[1, BLOCKS]], base=0, channel_multiplier=0).then_inc(iota_done, 1)

            def norm(g):
                pool.wait_ge(var_ready, g + 1)
                pool.tensor_tensor(rstd[:, tiles(g)], vare[:, tiles(g)], c["minus_half"][:, tiles(g)], ALU.pow).then_inc(rstd_done, 1)
                pool.wait_ge(rstd_done, g + 1)
                pool.tensor_tensor(shift[:, tiles(g)], nmean[:, tiles(g)], rstd[:, tiles(g)], ALU.mult).then_inc(shift_done, 1)

            def scatter(g):
                pool.wait_ge(rows_ready, g + 1)
                for i in range(g * RT, (g + 1) * RT):
                    pool.indirect_dma_start(out=sorted_rows, out_offset=bass.IndirectOffsetOnAxis(ap=row_i[:, i:i + 1], axis=0),
                                            in_=normed(i), in_offset=None).then_inc(scattered, 16)
            norm(0)
            for g in steps:
                if g + 1 in steps:
                    norm(g + 1)
                scatter(g)

            def slot_body(j, width, after):
                for t in range(HT):
                    if takes_piece(j, t):
                        piece = t // piece_step
                        col, width_p = PIECES[piece]
                        pool.wait_ge(aw["piece_hi"], piece + 1)
                        pool.tensor_tensor(aw["lo"][:, col:col + width_p], aw["stage"][:, 0:width_p],
                                           aw["hi"][:, col:col + width_p].bitcast(F32), ALU.subtract).then_inc(aw["piece_lo"], 1)
                pool.wait_ge(y_act, j * 2 + width // P // 2 + 1)
                pool.wait_ge(y_dve, j * 2 + width // P // 2 + 1)
                pool.dma_start(slot_rows[bass.ds(j * GROUP, width), :].rearrange("(i p) d -> p i d", p=P), y[:, 0:width // P, :]).then_inc(y_stored, 16)
                pool.wait_ge(y_stored, j * 16 + 16)
                pool.sem_inc(y_free, 1)
            pool.sem_inc(y_free, 1)
            if x_in is not None:
                pool.sem_inc(aw["piece_lo"], 1)
            all_slots(pool, slot_body)
            pool.wait_ge(scattered, 16 * TILES)

        @block.scalar
        def _(act):
            for g in steps:
                act.wait_ge(shift_done, g + 1)
                for i in range(g * RT, (g + 1) * RT):
                    act.activation(normed(i), xres[:, i, :], ACT.Identity, bias=shift[:, i:i + 1],
                                   scale=rstd[:, i:i + 1]).then_inc(xn_done, 1)
            act.wait_ge(mag_done, 1)
            act.activation(em[:], mag[:], ACT.Exp, scale=-1.0).then_inc(em_done, 1)

            def split_w(j, t):
                act.wait_ge(w_loaded[t % RING], (j * (HT // RING) + t // RING + 1) * 16)
                act.wait_ge(down_done, j * HT + t + 1)
                act.activation(w_hi[:, t % RING, :], stage[:, t % RING, :], ACT.Copy).then_inc(w_hi_done, 1)

            def split_x(j, width, k0, k1):
                for k in range(k0, k1):
                    act.wait_ge(x_turned, j * KC + k + 1)
                    act.activation(xT_hi[:, k, 0:width], ps_x[k % 2][:, 0:width], ACT.Copy).then_inc(x_hi_done, 1)
            act.sem_inc(w_hi_done, RING)
            act.sem_inc(y_act, 1)
            act.sem_inc(square_done, 2)
            act.wait_ge(down_done, RING)
            for t in range(AHEAD):
                split_w(0, t)
            split_x(0, GROUP, 0, KC)

            def slot_body(j, width, after):
                for t in range(HT):
                    if after or t + AHEAD < HT:
                        split_w(j, t + AHEAD)
                    act.wait_ge(up_done, j * HT + t + 1)
                    act.activation(square[:, t % 2, 0:width], ps_h[t % 2][:, 0:width], ACT.Square).then_inc(square_done, 1)
                    if after and t == HT - 1:
                        split_x(j + 1, after, 0, 2)
                    act.wait_ge(a_done, j * HT + t + 1)
                    act.activation(a_hi[:, t % RING, 0:width], a[:, t % 2, 0:width], ACT.Copy).then_inc(a_hi_done, 1)
                    if takes_piece(j, t - piece_step // 2):
                        piece = t // piece_step
                        col, width_p = PIECES[piece]
                        act.wait_ge(aw["piece_loaded"], (piece + 1) * 16)
                        act.activation(aw["hi"][:, col:col + width_p], aw["stage"][:, 0:width_p], ACT.Copy).then_inc(aw["piece_hi"], 1)
                if after:
                    split_x(j + 1, after, 2, KC)
                act.wait_ge(y_free, j + 1)
                act.wait_ge(down_done, j * HT + HT + RING)
                for i in range(0, width // P, 2):
                    act.activation(y[:, i, :], ps_y[i][:, :], ACT.Copy).then_inc(y_act, 1)
            all_slots(act, slot_body)

        @block.vector
        def _(dve):
            n = [0]

            def step(ins):
                n[0] += 1
                ins.then_inc(dve_step, 1)
                dve.wait_ge(dve_step, n[0])

            def statistics(g):
                if x_in is not None:
                    dve.wait_ge(in_loaded[g], 16)
                    for i in range(g * RT, (g + 1) * RT):
                        last = dve.bn_stats(stats[:, i, :], xres[:, i, :])
                    step(last)
                    for i in range(g * RT, (g + 1) * RT):
                        last = dve.bn_aggr(mv[:, i, :], stats[:, i, :])
                    step(last)
                dve.tensor_scalar(nmean[:, tiles(g)], mv[:, tiles(g), 0], -1.0, None, ALU.mult)
                dve.tensor_scalar(vare[:, tiles(g)], mv[:, tiles(g), 1], EPS, None, ALU.add).then_inc(var_ready, 1)

            def route(g):
                for i in range(g * RT, (g + 1) * RT):
                    dve.wait_ge(xn_done, i + 1)
                    last = dve.tensor_tensor_reduce(out=(square, square, factor, factor)[i % RT][:, i % 2, :], in0=normed(i), in1=wdiff[:], scale=1.0, scalar=0.0,
                                                    op0=ALU.mult, op1=ALU.add, accum_out=gap[:, i:i + 1])
                step(last)
                at = tiles(g)
                dve.tensor_scalar(is1[:, at], gap[:, at], 0.0, None, ALU.is_lt).then_inc(is1_done, 1)
                dve.wait_ge(is1_done, g + 1)
                step(dve.tensor_tensor(base[:, at], is1[:, at], rest[:, at], ALU.mult))
                dve.tensor_tensor(base[:, at], base[:, at], tok[:, at], ALU.add)
                dve.wait_ge(rank_mm, 2 * g + 2)
                step(dve.tensor_tensor_scan(out=cum[:, at], data0=ps_total[:, at], data1=zero[:, at],
                                            initial=cum[:, g * RT - 1:g * RT] if g else 0.0, op0=ALU.add, op1=ALU.add))
                step(dve.tensor_tensor(behind[:, at], ps_later[:, at], cum[:, at], ALU.subtract))
                step(dve.tensor_tensor(pos[:, at], base[:, at], behind[:, at], ALU.add))
                dve.tensor_copy(row_i[:, at], pos[:, at]).then_inc(rows_ready, 1)
            dve.memset(zero[:], 0.0)
            dve.wait_ge(iota_done, 2)
            dve.tensor_copy(slot[:], slot_i[:])
            step(dve.tensor_copy(tok[:], tok_i[:]))
            dve.tensor_scalar(rest[:], tok[:], -1.0, float(TOK), ALU.mult, ALU.add)
            statistics(0)
            dve.wait_ge(r_loaded, 16)
            step(dve.tensor_tensor(wdiff[:], rows[:, 0, :], rows[:, 1, :], ALU.subtract))
            for g in steps:
                if g + 1 in steps:
                    statistics(g + 1)
                route(g)
            dve.scalar_tensor_tensor(out=mag[:], in0=gap[:], scalar=-1.0, in1=gap[:], op0=ALU.mult, op1=ALU.max).then_inc(mag_done, 1)
            step(dve.tensor_scalar(border[:, 0:1], cum[:, TILES - 1:TILES], -1.0, float(TOK), ALU.mult, ALU.add))
            dve.tensor_scalar(blocks[:], slot[:], float(BLOCK), border[:, 0:1], ALU.mult, ALU.is_lt)
            step(dve.tensor_scalar(table[:, 1, 0:GROUPS], slot[:, 0:GROUPS], float(GROUP), float(BLOCK), ALU.mult, ALU.add))
            dve.tensor_reduce(border[:, 1:2], blocks[:], op=ALU.add, axis=AX.X)
            step(dve.tensor_scalar(table[:, 0, 0:GROUPS], table[:, 1, 0:GROUPS], border[:, 0:1], None, ALU.is_ge))
            step(dve.tensor_reduce(border[:, 2:3], table[:, 0, 0:GROUPS], op=ALU.add, axis=AX.X))
            step(dve.tensor_scalar(border[:, 2:3], border[:, 2:3], -2.0, float(1 + 2 * GROUPS), ALU.mult, ALU.add))
            step(dve.tensor_tensor(table[:, 0, GROUPS:SLOTS], border[:, 2:3], border[:, 1:2], ALU.subtract))
            dve.tensor_copy(border[:, 5:6], table[:, 0, GROUPS:SLOTS])
            step(dve.tensor_scalar(border[:, 3:4], border[:, 1:2], -1.0, 0.0, ALU.add, ALU.max))
            step(dve.tensor_scalar(table[:, 1, GROUPS:SLOTS], border[:, 3:4], float(BLOCK), None, ALU.mult))
            dve.tensor_copy(slot_table[:, 1, GROUPS:SLOTS], table[:, 1, GROUPS:SLOTS])
            dve.tensor_scalar(slot_table[:, 0, 0:SLOTS], table[:, 0, 0:SLOTS], float(HT), None, ALU.mult).then_inc(table_ready, 1)
            step(dve.tensor_scalar(behind[:], pos[:], table[:, 1, GROUPS:SLOTS], None, ALU.subtract))
            step(dve.tensor_scalar(inside[:], behind[:], 0.0, None, ALU.is_ge))
            step(dve.scalar_tensor_tensor(out=inside[:], in0=behind[:], scalar=float(BLOCK), in1=inside[:], op0=ALU.is_lt, op1=ALU.mult))
            step(dve.scalar_tensor_tensor(out=inside[:], in0=is1[:], scalar=border[:, 5:6], in1=inside[:], op0=ALU.is_equal, op1=ALU.mult))
            step(dve.tensor_scalar(border[:, 4:5], table[:, 1, GROUPS:SLOTS], -1.0, float(TOK), ALU.mult, ALU.add))
            step(dve.scalar_tensor_tensor(out=pos[:], in0=inside[:], scalar=border[:, 4:5], in1=pos[:], op0=ALU.mult, op1=ALU.add))
            dve.tensor_copy(gather_row[:], pos[:])
            dve.wait_ge(em_done, 1)
            step(dve.tensor_scalar(em[:], em[:], 1.0, None, ALU.add))
            step(dve.reciprocal(half_weight[:], em[:]))
            step(dve.tensor_scalar(half_weight[:], half_weight[:], 0.5, None, ALU.mult))

            def split_w(j, t):
                dve.wait_ge(w_hi_done, j * HT + t + 1 + RING)
                dve.tensor_tensor(w_lo[:, t % RING, :], stage[:, t % RING, :], w_hi[:, t % RING, :].bitcast(F32),
                                  ALU.subtract).then_inc(w_lo_done, 1)

            def split_x(j, width, k0, k1):
                for k in range(k0, k1):
                    dve.wait_ge(x_hi_done, j * KC + k + 1)
                    dve.tensor_tensor(xT_lo[:, k, 0:width], ps_x[k % 2][:, 0:width], xT_hi[:, k, 0:width].bitcast(F32),
                                      ALU.subtract).then_inc(x_lo_done, 1)
            dve.sem_inc(w_lo_done, RING)
            dve.sem_inc(y_dve, 1)
            dve.sem_inc(factor_done, 2)
            for t in range(AHEAD):
                split_w(0, t)
            split_x(0, GROUP, 0, KC)

            def slot_body(j, width, after):
                for t in range(HT):
                    if after or t + AHEAD < HT:
                        split_w(j, t + AHEAD)
                    dve.wait_ge(square_done, j * HT + t + 3)
                    dve.tensor_scalar(factor[:, t % 2, 0:width], ps_h[t % 2][:, 0:width], 0.0, 0.25, ALU.is_ge, ALU.max).then_inc(factor_done, 1)
                    dve.wait_ge(factor_done, j * HT + t + 3)
                    dve.tensor_tensor(a[:, t % 2, 0:width], square[:, t % 2, 0:width], factor[:, t % 2, 0:width], ALU.mult).then_inc(a_done, 1)
                    if after and t == HT - 1:
                        split_x(j + 1, after, 0, 2)
                    dve.wait_ge(a_hi_done, j * HT + t + 1)
                    dve.tensor_tensor(a_lo[:, t % RING, 0:width], a[:, t % 2, 0:width], a_hi[:, t % RING, 0:width].bitcast(F32),
                                      ALU.subtract).then_inc(a_lo_done, 1)
                if after:
                    split_x(j + 1, after, 2, KC)
                dve.wait_ge(y_free, j + 1)
                dve.wait_ge(down_done, j * HT + HT + RING)
                for i in range(1, width // P, 2):
                    dve.tensor_copy(y[:, i, :], ps_y[i][:, :]).then_inc(y_dve, 1)
            all_slots(dve, slot_body)

        @block.tensor
        def _(pe):
            for g in steps:
                pe.wait_ge(is1_done, g + 1)
                pe.matmul(ps_later[:, tiles(g)], c["later"][:], is1[:, tiles(g)], start=True, stop=True).then_inc(rank_mm, 1)
                pe.matmul(ps_total[:, tiles(g)], c["ones"][:], is1[:, tiles(g)], start=True, stop=True).then_inc(rank_mm, 1)

            def turn_x(j, width, k0, k1, first=False):
                if k0 == 0:
                    pe.wait_ge(x_loaded, j * 16 + 16)
                for k in range(k0, k1):
                    if not first or k >= 2:
                        pe.wait_ge(x_lo_done, j * KC + k - 1)
                    for i in range(width // P):
                        last = pe.transpose(ps_x[k % 2][:, i * P:(i + 1) * P], xg[:, i, k * P:(k + 1) * P], c["ident"][:])
                    last.then_inc(x_turned, 1)
            pe.sem_inc(down_done, RING)
            turn_x(0, GROUP, 0, KC, first=True)

            def slot_body(j, width, after):
                def up(t):
                    r = t % RING
                    if t == 0:
                        pe.wait_ge(x_lo_done, j * KC + KC)
                    pe.wait_ge(w_lo_done, j * HT + t + 1 + RING)
                    pe.wait_ge(square_done, j * HT + t + 1)
                    pe.wait_ge(factor_done, j * HT + t + 1)
                    parts = ((w_lo, xT_hi), (w_hi, xT_lo), (w_hi, xT_hi))
                    for k in range(KC):
                        for n, (w, x) in enumerate(parts):
                            last = pe.matmul(ps_h[t % 2][:, 0:width], w[:, r, k * P:(k + 1) * P], x[:, k, 0:width],
                                             start=(k == 0 and n == 0), stop=(k == KC - 1 and n == 2))
                    last.then_inc(up_done, 1)

                def down(t):
                    r = t % RING
                    pe.wait_ge(a_lo_done, j * HT + t + 1)
                    if t == 0:
                        pe.wait_ge(y_act, j * 2 + 1)
                        pe.wait_ge(y_dve, j * 2 + 1)
                    for i in range(width // P):
                        for n, (x, w) in enumerate(((a_lo, w_hi), (a_hi, w_lo), (a_hi, w_hi))):
                            last = pe.matmul(ps_y[i][:, :], x[:, r, i * P:(i + 1) * P], w[:, r, D:2 * D],
                                             start=(t == 0 and n == 0), stop=(t == HT - 1 and n == 2))
                    last.then_inc(down_done, 1)
                for t in range(AHEAD):
                    up(t)
                for t in range(HT):
                    if t + AHEAD < HT:
                        up(t + AHEAD)
                    if after and t == HT - 4:
                        turn_x(j + 1, after, 0, 2)
                    if after and t == HT - 1:
                        turn_x(j + 1, after, 2, KC)
                    down(t)
            all_slots(pe, slot_body)


def phase_gather(nc, top, slot_rows, gather_row, half_weight, xres, y_out):
    with ExitStack() as ctx:
        sem = lambda n: top.enter_context(nc.semaphore(n))
        rows = ctx.enter_context(nc.sbuf_tensor("ga_rows", [P, TILES, D], F32))
        loaded = [sem(f"ga_loaded{i}") for i in range(GATHERS)]
        added = sem("ga_added")
        stored = sem("ga_stored")
        block = ctx.enter_context(nc.Block())

        @block.gpsimd
        def _(pool):
            for i in range(TILES):
                if i >= GATHERS:
                    pool.wait_ge(added, i - GATHERS + 1)
                pool.indirect_dma_start(out=rows[:, i, :], out_offset=None, in_=slot_rows,
                                        in_offset=bass.IndirectOffsetOnAxis(ap=gather_row[:, i:i + 1], axis=0)).then_inc(loaded[i % GATHERS], 16)

        @block.vector
        def _(dve):
            for i in range(TILES):
                dve.wait_ge(loaded[i % GATHERS], 16 * (i // GATHERS + 1))
                dve.scalar_tensor_tensor(out=xres[:, i, :], in0=rows[:, i, :], scalar=half_weight[:, i:i + 1],
                                         in1=xres[:, i, :], op0=ALU.mult, op1=ALU.add).then_inc(added, 1)

        @block.sync
        def _(sp):
            for i in range(TILES):
                sp.wait_ge(added, i + 1)
                sp.dma_start(y_out[i * P:(i + 1) * P, :], xres[:, i, :]).then_inc(stored, 16)
            sp.wait_ge(stored, 16 * TILES)


def phase_turn(nc, top, c, slot_rows, gather_row, half_weight, xres, xT_hi, xT_lo):
    with ExitStack() as ctx:
        sb = lambda n, s, d=F32: ctx.enter_context(nc.sbuf_tensor(n, s, d))
        sem = lambda n: top.enter_context(nc.semaphore(n))
        rows = sb("tu_rows", [P, TILES, D])
        xn = sb("tu_xn", [P, UC, D])
        stats = sb("tu_stats", [P, TILES, 6])
        mv = sb("tu_mv", [P, TILES, 2])
        vare = sb("tu_vare", [P, TILES])
        nmean = sb("tu_nmean", [P, TILES])
        rstd = sb("tu_rstd", [P, TILES])
        shift = sb("tu_shift", [P, TILES])
        ps = [ctx.enter_context(nc.psum_tensor(f"tu_ps{k}", [P, UNIT], F32)) for k in range(8)]
        loaded = [sem(f"tu_loaded{i}") for i in range(GATHERS)]
        added = sem("tu_added")
        stats_done = sem("tu_stats_done")
        mv_done = sem("tu_mv_done")
        var_ready = sem("tu_var_ready")
        rstd_done = sem("tu_rstd_done")
        shift_done = sem("tu_shift_done")
        xn_done = sem("tu_xn_done")
        turned = sem("tu_turned")
        hi_done = sem("tu_hi_done")
        lo_done = sem("tu_lo_done")
        block = ctx.enter_context(nc.Block())
        tiles = lambda u: slice(u * UC, (u + 1) * UC)

        @block.gpsimd
        def _(pool):
            def gather(u):
                for i in range(u * UC, (u + 1) * UC):
                    if i >= GATHERS:
                        pool.wait_ge(added, i - GATHERS + 1)
                    pool.indirect_dma_start(out=rows[:, i, :], out_offset=None, in_=slot_rows,
                                            in_offset=bass.IndirectOffsetOnAxis(ap=gather_row[:, i:i + 1], axis=0)).then_inc(loaded[i % GATHERS], 16)
            gather(0)
            for u in range(UNITS):
                if u + 1 < UNITS:
                    gather(u + 1)
                pool.wait_ge(var_ready, u + 1)
                pool.tensor_tensor(rstd[:, tiles(u)], vare[:, tiles(u)], c["minus_half"][:, tiles(u)], ALU.pow).then_inc(rstd_done, 1)
                pool.wait_ge(rstd_done, u + 1)
                pool.tensor_tensor(shift[:, tiles(u)], nmean[:, tiles(u)], rstd[:, tiles(u)], ALU.mult).then_inc(shift_done, 1)

        @block.vector
        def _(dve):
            def add(u):
                for i in range(u * UC, (u + 1) * UC):
                    dve.wait_ge(loaded[i % GATHERS], 16 * (i // GATHERS + 1))
                    dve.scalar_tensor_tensor(out=xres[:, i, :], in0=rows[:, i, :], scalar=half_weight[:, i:i + 1],
                                             in1=xres[:, i, :], op0=ALU.mult, op1=ALU.add).then_inc(added, 1)
                for i in range(u * UC, (u + 1) * UC):
                    dve.wait_ge(added, i + 1)
                    last = dve.bn_stats(stats[:, i, :], xres[:, i, :])
                last.then_inc(stats_done, 1)
                dve.wait_ge(stats_done, u + 1)
                for i in range(u * UC, (u + 1) * UC):
                    last = dve.bn_aggr(mv[:, i, :], stats[:, i, :])
                last.then_inc(mv_done, 1)
                dve.wait_ge(mv_done, u + 1)
                dve.tensor_scalar(nmean[:, tiles(u)], mv[:, tiles(u), 0], -1.0, None, ALU.mult)
                dve.tensor_scalar(vare[:, tiles(u)], mv[:, tiles(u), 1], EPS, None, ALU.add).then_inc(var_ready, 1)
            add(0)
            for u in range(UNITS):
                if u + 1 < UNITS:
                    add(u + 1)
                for k in range(KC):
                    dve.wait_ge(hi_done, u * KC + k + 1)
                    dve.tensor_tensor(xT_lo[:, k, u * UNIT:(u + 1) * UNIT], ps[(u * KC + k) % 8][:, :],
                                      xT_hi[:, k, u * UNIT:(u + 1) * UNIT].bitcast(F32), ALU.subtract).then_inc(lo_done, 1)

        @block.scalar
        def _(act):
            for u in range(UNITS):
                act.wait_ge(shift_done, u + 1)
                if u > 0:
                    act.wait_ge(turned, u * KC)
                for i in range(UC):
                    t = u * UC + i
                    act.activation(xn[:, i, :], xres[:, t, :], ACT.Identity, bias=shift[:, t:t + 1],
                                   scale=rstd[:, t:t + 1]).then_inc(xn_done, 1)
                for k in range(KC):
                    act.wait_ge(turned, u * KC + k + 1)
                    act.activation(xT_hi[:, k, u * UNIT:(u + 1) * UNIT], ps[(u * KC + k) % 8][:, :], ACT.Copy).then_inc(hi_done, 1)

        @block.tensor
        def _(pe):
            for u in range(UNITS):
                pe.wait_ge(xn_done, (u + 1) * UC)
                for k in range(KC):
                    n = u * KC + k
                    if n >= 8:
                        pe.wait_ge(lo_done, n - 7)
                    for i in range(UC):
                        last = pe.transpose(ps[n % 8][:, i * P:(i + 1) * P], xn[:, i, k * P:(k + 1) * P], c["ident"][:])
                    last.then_inc(turned, 1)


HK_STEPS = [UC if k % HALVES == 0 else UC - 1 for k in range(UNITS)]
HK_AT = [sum(HK_STEPS[:k]) for k in range(UNITS + 1)]


def phase_attention(nc, top, c, watt, gnorm, slot_rows, gather_row, half_weight, xres, mv, aw):
    with ExitStack() as ctx:
        xT_hi = ctx.enter_context(nc.sbuf_tensor("at_xT_hi", [P, KC, TOK], F32R))
        xT_lo = ctx.enter_context(nc.sbuf_tensor("at_xT_lo", [P, KC, TOK], F32R))
        phase_turn(nc, top, c, slot_rows, gather_row, half_weight, xres, xT_hi, xT_lo)
        phase_heads(nc, top, c, watt, gnorm, xres, mv, aw, xT_hi, xT_lo)


def phase_heads(nc, top, c, watt, gnorm, xres, mv, aw, xT_hi, xT_lo):
    with ExitStack() as ctx:
        sb = lambda n, s, d=F32: ctx.enter_context(nc.sbuf_tensor(n, s, d))
        sem = lambda n: top.enter_context(nc.semaphore(n))
        stage, w_hi, w_lo = aw["stage"], aw["hi"], aw["lo"]
        gn = sb("at_gn", [DV, 1])
        qT = sb("at_qT", [P, 2, UNIT])
        kT = sb("at_kT", [P, UNIT])
        eT = sb("at_eT", [P, 2, UNIT])
        zT = sb("at_zT", [P, UNIT])
        zlast = sb("at_zlast", [P, 1])
        v = sb("at_v", [P, 2, UC, 2 * DV])
        gate = sb("at_gate", [P, 2, UC, 2 * DV])
        en = sb("at_en", [P, UC, P])
        kn = sb("at_kn", [P, UC, P])
        rz = sb("at_rz", [P, UC, P])
        am = sb("at_am", [P, 2, UC, P])
        hk = sb("at_hk", [P, UC, P])
        hv = sb("at_hv", [P, UC, 2 * DV])
        ok = sb("at_ok", [P, UC, P])
        pv = sb("at_pv", [P, UC, P])
        pT = sb("at_pT", [P, UNIT])
        u = sb("at_u", [P, 2, UC, DV])
        uT_hi = sb("at_uT_hi", [P, 2, 2, 2 * P], F32R)
        uT_lo = sb("at_uT_lo", [P, 2, 2, 2 * P], F32R)
        highest = sb("at_highest", [P, 2 * UC])
        den = sb("at_den", [P, 2 * UC])
        ss = sb("at_ss", [P, 2 * UC])
        ms = sb("at_ms", [P, 2 * UC])
        coef = sb("at_coef", [P, 2 * UC])
        PJ = [ctx.enter_context(nc.psum_tensor(f"at_pj{b}", [P, 512], F32)) for b in range(2)]
        R = [ctx.enter_context(nc.psum_tensor(f"at_r{b}", [P, 512], F32)) for b in range(6)]

        gn_loaded = sem("at_gn_loaded")
        piece_loaded, piece_hi, piece_lo = aw["piece_loaded"], aw["piece_hi"], aw["piece_lo"]
        piece_scaled = sem("at_piece_scaled")
        bn = sb("at_bn", [P, TILES, 6])
        bn_done = sem("at_bn_done")
        q_mm, k_mm, s_mm, vg_mm = sem("at_q_mm"), sem("at_k_mm"), sem("at_s_mm"), sem("at_vg_mm")
        q_out, k_out, s_clipped, e_done, z_done = sem("at_q_out"), sem("at_k_out"), sem("at_s_clipped"), sem("at_e_done"), sem("at_z_done")
        z_kept = sem("at_z_kept")
        v_out, tanh_done, gate_done = sem("at_v_out"), sem("at_tanh_done"), sem("at_gate_done")
        e_tr, k_tr, z_tr = sem("at_e_tr"), sem("at_k_tr"), sem("at_z_tr")
        en_out, kn_out, rz_done = sem("at_en_out"), sem("at_kn_out"), sem("at_rz_done")
        dk_mm, hk_done = sem("at_dk_mm"), sem("at_hk_done")
        a_mm, a_masked = sem("at_a_mm"), sem("at_a_masked")
        ok_mm, ok_scaled, highest_done, ok_shifted = sem("at_ok_mm"), sem("at_ok_scaled"), sem("at_highest_done"), sem("at_ok_shifted")
        pv_done, den_done, pz_done = sem("at_pv_done"), sem("at_den_done"), sem("at_pz_done")
        p_tr, p_out = sem("at_p_tr"), sem("at_p_out")
        b_mm, b_masked = sem("at_b_mm"), sem("at_b_masked")
        dv_mm, hv_done = sem("at_dv_mm"), sem("at_hv_done")
        o_mm, squared, ss_done, eps_done, ms_done, coef_done, u_done = (
            sem("at_o_mm"), sem("at_squared"), sem("at_ss_done"), sem("at_eps_done"), sem("at_ms_done"), sem("at_coef_done"), sem("at_u_done"))
        u_tr, u_hi, u_lo = sem("at_u_tr"), sem("at_u_hi"), sem("at_u_lo")
        wo_mm, added = sem("at_wo_mm"), sem("at_added")
        block = ctx.enter_context(nc.Block())
        NP = len(PIECES)

        wq = lambda w, k, part: w[:, k * 3 * P + part * P:k * 3 * P + (part + 1) * P]
        wvg = lambda w, k: w[:, QKS + k * 4 * P:QKS + (k + 1) * 4 * P]
        wo = lambda w, h: w[:, QKS + VG + h * D:QKS + VG + (h + 1) * D]

        def count(i, k, per, done):
            return i * (UNITS * per) + (k * per + done + 1)

        @block.sync
        def _(sp):
            sp.dma_start(gn[:, :], gnorm).then_inc(gn_loaded, 16)
            def load(i, n, pair, piece):
                col, width = PIECES[piece]
                sp.wait_ge(piece_lo, i * NP + n + 4 + 1)
                sp.dma_start(stage[:, 0:width], watt[bass.ds(pair, 1), :, col:col + width].rearrange("a p n -> (a p) n")).then_inc(piece_loaded, 16)
            with sp.Fori(0, PAIRS - 1) as i:
                load(i, 0, i, 4)
                for n in range(4):
                    load(i, n + 1, i + 1, n)
            load(PAIRS - 1, 0, PAIRS - 1, 4)

        @block.gpsimd
        def _(pool):
            pool.sem_inc(coef_done, 1)

            def lo_piece(n, piece):
                col, width = PIECES[piece]
                pool.wait_ge(piece_hi, n + 1)
                pool.tensor_tensor(w_lo[:, col:col + width], stage[:, 0:width], w_hi[:, col:col + width].bitcast(F32),
                                   ALU.subtract).then_inc(piece_lo, 1)
            pool.wait_ge(gn_loaded, 16)

            def pair(i, last):
                def norm(k):
                    pool.wait_ge(ms_done, count(i, k, 2, 2))
                    pool.tensor_tensor(coef[:, :], ms[:, :], c["minus_half"][:, 0:2 * UC], ALU.pow).then_inc(coef_done, 1)
                pool.wait_ge(piece_loaded, i * (NP * 16) + 5 * 16)
                pool.tensor_tensor(stage[:, 0:WO], stage[:, 0:WO], gn[:, 0:1].to_broadcast([P, WO]), ALU.mult).then_inc(piece_scaled, 1)
                lo_piece(i * NP + 4, 4)
                norm(0)
                norm(1)
                if not last:
                    lo_piece(i * NP + 5, 0)
                norm(2)
                if not last:
                    for n in range(1, 4):
                        lo_piece(i * NP + 5 + n, n)
                norm(3)
            with pool.Fori(0, PAIRS - 1) as i:
                pair(i, False)
            pair(PAIRS - 1, True)

        @block.scalar
        def _(act):
            for s in (q_out, e_done, v_out, tanh_done, en_out, pv_done, p_out, squared, u_hi):
                act.sem_inc(s, 1)

            def hi_piece(n, piece):
                col, width = PIECES[piece]
                act.wait_ge(piece_scaled if piece == 4 else piece_loaded, n)
                act.activation(w_hi[:, col:col + width], stage[:, 0:width], ACT.Copy).then_inc(piece_hi, 1)

            def q_scale(i, k):
                act.wait_ge(q_mm, count(i, k, 1, 0))
                act.activation(qT[:, k % 2, :], PJ[(7 * k) % 2][:, :], ACT.Copy, scale=float(DK) ** -0.5).then_inc(q_out, 1)

            def e_exp(i, k):
                act.wait_ge(s_clipped, count(i, k, 1, 1))
                act.activation(eT[:, k % 2, :], eT[:, k % 2, :], ACT.Exp).then_inc(e_done, 1)

            def vg_read(i, k, t):
                bank = PJ[(7 * k + 3 + t) % 2]
                act.wait_ge(vg_mm, count(i, k, UC, t))
                act.activation(v[:, k % 2, t, :], bank[:, 0:2 * DV], ACT.Copy).then_inc(v_out, 1)
                act.activation(gate[:, k % 2, t, :], bank[:, 2 * DV:4 * DV], ACT.Tanh, scale=0.5).then_inc(tanh_done, 1)
            q_scale(0, 0)
            e_exp(0, 0)
            for t in range(UC):
                vg_read(0, 0, t)

            def pair(i, last):
                for k in range(UNITS):
                    more = not last or k < UNITS - 1
                    act.wait_ge(e_tr, count(i, k, 1, 0))
                    act.activation(en[:, :, :], R[0][:, :].rearrange("p (a b) -> p a b", a=UC), ACT.Copy).then_inc(en_out, 1)
                    if more:
                        q_scale(i, k + 1)
                    if k == 0:
                        act.wait_ge(wo_mm, count(i, k, UC, 0))
                        hi_piece(i + 1, 4)
                    if k == UNITS - 1 and more:
                        hi_piece(i * (NP * 16) + 9 * 16, 3)
                    act.wait_ge(ok_shifted, count(i, k, 1, 1))
                    act.activation(pv[:, :, :], ok[:, :, :], ACT.Exp).then_inc(pv_done, 1)
                    if more:
                        e_exp(i, k + 1)
                        vg_read(i, k + 1, 0)
                    act.wait_ge(p_tr, count(i, k, 1, 0))
                    act.activation(pT[:, :], R[3][:, :], ACT.Copy).then_inc(p_out, 1)
                    if more:
                        vg_read(i, k + 1, 1)
                    if k == UNITS - 2 and not last:
                        act.wait_ge(s_mm, count(i, k + 1, 1, 0))
                        hi_piece(i * (NP * 16) + 6 * 16, 0)
                    for b in range(2):
                        act.wait_ge(o_mm, count(i, k, 2, b))
                        act.activation(u[:, b, :, :].rearrange("p a d -> p (a d)"), R[b][:, :], ACT.Square).then_inc(squared, 1)
                    if more:
                        vg_read(i, k + 1, 2)
                    if k == UNITS - 2 and not last:
                        hi_piece(i * (NP * 16) + 7 * 16, 1)
                    if more:
                        vg_read(i, k + 1, 3)
                    for b in range(2):
                        act.wait_ge(u_tr, count(i, k, 2, b))
                        act.activation(uT_hi[:, b, :, :].rearrange("p h t -> p (h t)"), R[2 + b][:, :], ACT.Copy).then_inc(u_hi, 1)
                    if k == UNITS - 2 and not last:
                        hi_piece(i * (NP * 16) + 8 * 16, 2)
            with act.Fori(0, PAIRS - 1) as i:
                pair(i, False)
            pair(PAIRS - 1, True)

        @block.vector
        def _(dve):
            for s in (k_out, s_clipped, z_done, gate_done, kn_out, rz_done, hk_done, a_masked, ok_scaled, highest_done, ok_shifted,
                      den_done, pz_done, b_masked, hv_done, ss_done, eps_done, ms_done, u_done, u_lo, added):
                dve.sem_inc(s, 1)
            dve.memset(hk[:, :, :], 0.0)

            def k_copy(i, k):
                dve.wait_ge(k_mm, count(i, k, 1, 0))
                dve.tensor_copy(kT[:, :], PJ[(7 * k + 1) % 2][:, :]).then_inc(k_out, 1)

            def s_clip(i, k):
                dve.wait_ge(s_mm, count(i, k, 1, 0))
                dve.tensor_scalar(eT[:, k % 2, :], PJ[(7 * k + 2) % 2][:, :], CLAMP, -CLAMP, ALU.min, ALU.max).then_inc(s_clipped, 1)

            def z_scan(i, k):
                dve.wait_ge(e_done, count(i, k, 1, 1))
                first = k % HALVES == 0
                if not first:
                    dve.wait_ge(z_kept, i * (UNITS // HALVES) + k // HALVES + 1)
                dve.tensor_tensor_scan(out=zT[:, :], data0=eT[:, k % 2, :], data1=eT[:, k % 2, :],
                                       initial=0.0 if first else zlast[:, 0:1], op0=ALU.add, op1=ALU.bypass).then_inc(z_done, 1)
                if first:
                    dve.wait_ge(z_done, count(i, k, 1, 1))
                    dve.tensor_copy(zlast[:, :], zT[:, UNIT - 1:UNIT]).then_inc(z_kept, 1)

            def gate_make(i, k, t):
                dve.wait_ge(tanh_done, count(i, k, UC, t + 1))
                dve.scalar_tensor_tensor(out=gate[:, k % 2, t, :], in0=gate[:, k % 2, t, :], scalar=1.0,
                                         in1=PJ[(7 * k + 3 + t) % 2][:, 2 * DV:4 * DV], op0=ALU.add, op1=ALU.mult).then_inc(gate_done, 1)
            k_copy(0, 0)
            s_clip(0, 0)
            z_scan(0, 0)
            for t in range(UC):
                gate_make(0, 0, t)

            def pair(i, last_pair):
                for k in range(UNITS):
                    more = not last_pair or k < UNITS - 1
                    first = k % HALVES == 0
                    dve.wait_ge(k_tr, count(i, k, 1, 0))
                    dve.tensor_copy(kn[:, :, :], R[1][:, :].rearrange("p (a b) -> p a b", a=UC)).then_inc(kn_out, 1)
                    dve.wait_ge(z_tr, count(i, k, 1, 0))
                    dve.reciprocal(rz[:, :, :], R[2][:, :].rearrange("p (a b) -> p a b", a=UC)).then_inc(rz_done, 1)
                    dve.wait_ge(dk_mm, count(i, k, 1, 0))
                    for cc in range(UC if first else UC - 1):
                        to = (cc + 1) % UC
                        for h in range(2):
                            rows, cols = slice(64 * h, 64 * h + 64), slice(64 * h, 64 * h + 64)
                            part = R[5][rows, cc * P + 64 * h:cc * P + 64 * h + 64]
                            if first and cc == 0:
                                last = dve.tensor_copy(hk[rows, to, cols], part)
                            else:
                                last = dve.tensor_tensor(hk[rows, to, cols], part, hk[rows, cc, cols], ALU.add)
                        last.then_inc(hk_done, 1)
                        dve.wait_ge(hk_done, i * HK_AT[UNITS] + HK_AT[k] + cc + 2)
                    for b in range(2):
                        dve.wait_ge(a_mm, count(i, k, 2, b))
                        dve.tensor_tensor(am[:, b, :, :],
                                          R[3 + b][:, :].rearrange("p (a t) -> p a t", a=4),
                                          c["causal"][:, :].rearrange("p (a t) -> p a t", a=1).to_broadcast([P, 4, P]), ALU.mult).then_inc(a_masked, 1)
                    if more:
                        k_copy(i, k + 1)
                    dve.wait_ge(ok_mm, count(i, k, 1, 0))
                    dve.wait_ge(rz_done, count(i, k, 1, 1))
                    dve.tensor_tensor(ok[:, :, :], R[2][:, :].rearrange("p (a b) -> p a b", a=UC), rz[:, :, :], ALU.mult).then_inc(ok_scaled, 1)
                    dve.wait_ge(ok_scaled, count(i, k, 1, 1))
                    by_head = lambda x: x[:, :, :].rearrange("p a (h m) -> p (a h) m", h=2)
                    spread = lambda x: x[:, :].rearrange("p (a b) -> p a b", b=1).to_broadcast([P, 2 * UC, M])
                    dve.tensor_reduce(highest[:, :], by_head(ok), op=ALU.max, axis=AX.X).then_inc(highest_done, 1)
                    dve.wait_ge(highest_done, count(i, k, 1, 1))
                    dve.tensor_tensor(by_head(ok), by_head(ok), spread(highest), ALU.subtract).then_inc(ok_shifted, 1)
                    dve.wait_ge(pv_done, count(i, k, 1, 1))
                    dve.tensor_tensor(ok[:, :, :], pv[:, :, :], rz[:, :, :], ALU.mult).then_inc(pz_done, 1)
                    if more:
                        s_clip(i, k + 1)
                    dve.tensor_reduce(den[:, :], pv[:, :, :].rearrange("p a (h m) -> p h a m", h=2), op=ALU.add, axis=AX.X).then_inc(den_done, 1)
                    if more:
                        gate_make(i, k + 1, 0)
                    dve.wait_ge(den_done, count(i, k, 1, 1))
                    dve.scalar_tensor_tensor(out=ms[:, :], in0=den[:, :], scalar=4.0 * EPS, in1=den[:, :], op0=ALU.mult, op1=ALU.mult).then_inc(eps_done, 1)
                    for b in range(2):
                        dve.wait_ge(b_mm, count(i, k, 2, b))
                        dve.tensor_tensor(am[:, b, :, :],
                                          R[4 + b][:, :].rearrange("p (a t) -> p a t", a=4),
                                          c["causal"][:, :].rearrange("p (a t) -> p a t", a=1).to_broadcast([P, 4, P]), ALU.mult).then_inc(b_masked, 1)
                    for cc in range(UC if first else UC - 1):
                        to = (cc + 1) % UC
                        if cc % 2 == 0:
                            dve.wait_ge(dv_mm, count(i, k, 2, cc // 2))
                        part = R[2 + cc // 2][:, (cc % 2) * 2 * DV:(cc % 2 + 1) * 2 * DV]
                        if first and cc == 0:
                            last = dve.tensor_copy(hv[:, to, :], part)
                        else:
                            last = dve.tensor_tensor(hv[:, to, :], part, hv[:, cc, :], ALU.add)
                        last.then_inc(hv_done, 1)
                        dve.wait_ge(hv_done, i * HK_AT[UNITS] + HK_AT[k] + cc + 2)
                    if more:
                        gate_make(i, k + 1, 1)
                        z_scan(i, k + 1)
                    dve.wait_ge(eps_done, count(i, k, 1, 1))
                    for b in range(2):
                        cols = slice(4 * b, 4 * b + 4)
                        dve.wait_ge(squared, count(i, k, 2, b + 1))
                        dve.tensor_reduce(ss[:, cols], u[:, b, :, :], op=ALU.add, axis=AX.X).then_inc(ss_done, 1)
                        dve.wait_ge(ss_done, count(i, k, 2, b + 1))
                        dve.scalar_tensor_tensor(out=ms[:, cols], in0=ss[:, cols], scalar=4.0 / DV, in1=ms[:, cols], op0=ALU.mult, op1=ALU.add).then_inc(ms_done, 1)
                    dve.wait_ge(coef_done, count(i, k, 1, 1))
                    for b in range(2):
                        for cc, h in ((2 * b, 0), (2 * b, 1), (2 * b + 1, 0), (2 * b + 1, 1)):
                            last = dve.scalar_tensor_tensor(out=u[:, h, cc, :], in0=R[h][:, cc * P:(cc + 1) * P], scalar=coef[:, 4 * h + cc:4 * h + cc + 1],
                                                            in1=gate[:, k % 2, cc, h * DV:(h + 1) * DV], op0=ALU.mult, op1=ALU.mult)
                        last.then_inc(u_done, 1)
                    if more:
                        gate_make(i, k + 1, 2)
                    for b in range(2):
                        dve.wait_ge(u_hi, count(i, k, 2, b + 1))
                        dve.tensor_tensor(uT_lo[:, b, :, :].rearrange("p h t -> p (h t)"), R[2 + b][:, :],
                                          uT_hi[:, b, :, :].rearrange("p h t -> p (h t)").bitcast(F32), ALU.subtract).then_inc(u_lo, 1)
                    if more:
                        gate_make(i, k + 1, 3)
                    for cc in range(UC):
                        dve.wait_ge(wo_mm, count(i, k, UC, cc + 1))
                        dve.tensor_tensor(xres[:, k * UC + cc, :], R[4 + cc % 2][:, :], xres[:, k * UC + cc, :], ALU.add).then_inc(added, 1)
                    if last_pair:
                        for cc in range(UC):
                            dve.wait_ge(added, count(i, k, UC, cc + 1))
                            last = dve.bn_stats(bn[:, k * UC + cc, :], xres[:, k * UC + cc, :])
                        last.then_inc(bn_done, 1)
                        dve.wait_ge(bn_done, k + 1)
                        for t in range(k * UC, (k + 1) * UC):
                            dve.bn_aggr(mv[:, t, :], bn[:, t, :])
            with dve.Fori(0, PAIRS - 1) as i:
                pair(i, False)
            pair(PAIRS - 1, True)

        @block.tensor
        def _(pe):
            parts = ((w_lo, xT_hi), (w_hi, xT_lo), (w_hi, xT_hi))

            def turned(i, k, part, done):
                tok = slice((k % UNITS) * UNIT, (k % UNITS + 1) * UNIT)
                for kk in range(KC):
                    for n, (w, x) in enumerate(parts):
                        last = pe.matmul(PJ[(7 * k + part) % 2][:, :], wq(w, kk, part), x[:, kk, tok],
                                         start=(kk == 0 and n == 0), stop=(kk == KC - 1 and n == 2))
                last.then_inc(done, 1)

            def project_q(i, k):
                pe.wait_ge(gate_done, count(i, k, UC, -1))
                turned(i, k, 0, q_mm)

            def project_k(i, k):
                pe.wait_ge(gate_done, count(i, k, UC, 0))
                turned(i, k, 1, k_mm)

            def project_s(i, k):
                pe.wait_ge(q_out, count(i, k, 1, 1))
                turned(i, k, 2, s_mm)

            def project_vg(i, k, t):
                if t == 0:
                    pe.wait_ge(k_out, count(i, k, 1, 1))
                elif t == 1:
                    pe.wait_ge(s_clipped, count(i, k, 1, 1))
                else:
                    pe.wait_ge(gate_done, count(i, k, UC, t - 1))
                tok = slice((k % UNITS) * UNIT + t * P, (k % UNITS) * UNIT + (t + 1) * P)
                for kk in range(KC):
                    for n, (w, x) in enumerate(parts):
                        last = pe.matmul(PJ[(7 * k + 3 + t) % 2][:, :], x[:, kk, tok], wvg(w, kk),
                                         start=(kk == 0 and n == 0), stop=(kk == KC - 1 and n == 2))
                last.then_inc(vg_mm, 1)
            pe.sem_inc(wo_mm, 1)
            turned(0, 0, 0, q_mm)
            turned(0, 0, 1, k_mm)
            project_s(0, 0)
            for t in range(UC):
                project_vg(0, 0, t)

            chunk = lambda cc: slice(cc * P, (cc + 1) * P)
            half = lambda h: slice(64 * h, 64 * h + 64)

            def turn_ek(i, k):
                pe.wait_ge(e_done, count(i, k, 1, 1))
                for cc in range(UC):
                    last = pe.transpose(R[0][:, chunk(cc)], eT[:, k % 2, chunk(cc)], c["ident"][:])
                last.then_inc(e_tr, 1)
                pe.wait_ge(k_out, count(i, k, 1, 1))
                for cc in range(UC):
                    last = pe.transpose(R[1][:, chunk(cc)], kT[:, chunk(cc)], c["ident"][:])
                last.then_inc(k_tr, 1)
            turn_ek(0, 0)

            def pair(i, last_pair):
                for k in range(UNITS):
                    more = not last_pair or k < UNITS - 1
                    first = k % HALVES == 0
                    b2 = k % 2
                    pe.wait_ge(z_done, count(i, k, 1, 1))
                    pe.wait_ge(u_lo, count(i, k, 2, 0))
                    for cc in range(UC):
                        last = pe.transpose(R[2][:, chunk(cc)], zT[:, chunk(cc)], c["ident"][:])
                    last.then_inc(z_tr, 1)
                    if k == UNITS - 1 and more:
                        pe.wait_ge(piece_lo, i * NP + 1 + 7)
                    if more:
                        project_q(i, k + 1)
                    pe.wait_ge(en_out, count(i, k, 1, 1))
                    pe.wait_ge(kn_out, count(i, k, 1, 1))
                    pe.wait_ge(added, count(i, k, UC, 0))
                    for cc in range(UC):
                        last = pe.matmul(R[5][:, chunk(cc)], kn[:, cc, :], en[:, cc, :], start=True, stop=True)
                    last.then_inc(dk_mm, 1)
                    pe.wait_ge(q_out, count(i, k, 1, 1))
                    for cc in range(UC):
                        for h in range(2):
                            last = pe.matmul(R[3 + h][:, chunk(cc)], kT[half(h), chunk(cc)], qT[half(h), b2, chunk(cc)], start=True, stop=True)
                            if cc == UC - 1:
                                last.then_inc(a_mm, 1)
                    if more:
                        project_k(i, k + 1)
                    pe.wait_ge(rz_done, count(i, k, 1, 1))
                    pe.wait_ge(hk_done, i * HK_AT[UNITS] + HK_AT[k + 1] + 1)
                    pe.wait_ge(a_masked, count(i, k, 2, 2))
                    for cc in range(UC):
                        state = not (first and cc == 0)
                        if state:
                            pe.matmul(R[2][:, chunk(cc)], qT[:, b2, chunk(cc)], hk[:, cc, :], start=True, stop=False, skip_group_check=True)
                        for h in range(2):
                            last = pe.matmul(R[2][:, cc * P + 64 * h:cc * P + 64 * h + 64], am[:, h, cc, :], en[:, cc, half(h)],
                                             start=not state, stop=True, skip_group_check=True)
                    last.then_inc(ok_mm, 1)
                    if more:
                        project_s(i, k + 1)
                    if k == UNITS - 1 and more:
                        pe.wait_ge(piece_lo, i * NP + 1 + 9)
                    if more:
                        project_vg(i, k + 1, 0)
                    pe.wait_ge(pz_done, count(i, k, 1, 1))
                    for cc in range(UC):
                        last = pe.transpose(R[3][:, chunk(cc)], ok[:, cc, :], c["ident"][:])
                    last.then_inc(p_tr, 1)
                    if more:
                        project_vg(i, k + 1, 1)
                    pe.wait_ge(p_out, count(i, k, 1, 1))
                    for cc in range(UC):
                        for h in range(2):
                            last = pe.matmul(R[4 + h][:, chunk(cc)], eT[half(h), b2, chunk(cc)], pT[half(h), chunk(cc)], start=True, stop=True)
                            if cc == UC - 1:
                                last.then_inc(b_mm, 1)
                    pe.wait_ge(v_out, count(i, k, UC, UC))
                    for b in range(2):
                        for a in range(2):
                            cc = 2 * b + a
                            last = pe.matmul(R[2 + b][:, a * 2 * DV:(a + 1) * 2 * DV], en[:, cc, :], v[:, b2, cc, :], start=True, stop=True)
                        last.then_inc(dv_mm, 1)
                    for h in range(2):
                        pe.wait_ge(b_masked, count(i, k, 2, h + 1))
                        for cc in range(UC):
                            last = pe.matmul(R[h][:, chunk(cc)], am[:, h, cc, :], v[:, b2, cc, h * DV:(h + 1) * DV],
                                             start=(cc == 0), stop=(first and cc == 0), skip_group_check=True)
                    pe.wait_ge(hv_done, i * HK_AT[UNITS] + HK_AT[k + 1] + 1)
                    for h in range(2):
                        for cc in range(1 if first else 0, UC):
                            last = pe.matmul(R[h][:, chunk(cc)], pT[half(h), chunk(cc)], hv[half(h), cc, h * DV:(h + 1) * DV],
                                             start=False, stop=True, skip_group_check=True)
                        last.then_inc(o_mm, 1)
                    if more:
                        project_vg(i, k + 1, 2)
                        project_vg(i, k + 1, 3)
                    for b in range(2):
                        pe.wait_ge(u_done, count(i, k, 2, b + 1))
                        for h in range(2):
                            for a in range(2):
                                last = pe.transpose(R[2 + b][:, (2 * h + a) * P:(2 * h + a + 1) * P], u[:, h, 2 * b + a, :], c["ident"][:])
                        last.then_inc(u_tr, 1)
                    if more:
                        turn_ek(i, k + 1)
                    if k == 0:
                        pe.wait_ge(piece_lo, i * NP + 1 + 5)
                    for cc in range(UC):
                        if cc % 2 == 0:
                            pe.wait_ge(u_lo, count(i, k, 2, cc // 2 + 1))
                        if cc >= 2:
                            pe.wait_ge(added, count(i, k, UC, cc - 1))
                        for h in range(2):
                            for n, (x, w) in enumerate(((uT_lo, w_hi), (uT_hi, w_lo), (uT_hi, w_hi))):
                                last = pe.matmul(R[4 + cc % 2][:, :], x[:, cc // 2, h, (cc % 2) * P:(cc % 2 + 1) * P], wo(w, h),
                                                 start=(h == 0 and n == 0), stop=(h == 1 and n == 2))
                        last.then_inc(wo_mm, 1)
            with pe.Fori(0, PAIRS - 1) as i:
                pair(i, False)
            pair(PAIRS - 1, True)


def macaron(nc, x, wff, router, watt, gnorm, out):
    sorted_rows = nc.dram_tensor("sorted_rows", [TOK, D], F32, kind="Internal").ap()
    slot_rows = nc.dram_tensor("slot_rows", [TOK + BLOCK, D], F32, kind="Internal").ap()
    with ExitStack() as top:
        sb = lambda n, s, d=F32: top.enter_context(nc.sbuf_tensor(n, s, d))
        c = phase_constants(nc, top)
        xres = sb("xres", [P, TILES, D])
        mv = sb("mv", [P, TILES, 2])
        aw = {"stage": sb("at_stage", [P, PIECE]),
              "hi": sb("at_w_hi", [P, QKS + VG + WO], F32R), "lo": sb("at_w_lo", [P, QKS + VG + WO], F32R)}
        for n in ("piece_loaded", "piece_hi", "piece_lo"):
            aw[n] = top.enter_context(nc.semaphore("at_" + n))
        half_weight = sb("half_weight", [P, TILES])
        gather_row = sb("gather_row", [P, TILES], I32)
        slot_table = sb("slot_table", [P, 2, 8], I32)

        def feed_forward(tag, x_in):
            phase_feed_forward(nc, top, tag, c, x_in, router, wff, watt, xres, mv, aw, half_weight, gather_row, slot_table, sorted_rows, slot_rows)
        feed_forward("first_", x)
        phase_attention(nc, top, c, watt, gnorm, slot_rows, gather_row, half_weight, xres, mv, aw)
        feed_forward("last_", None)
        phase_gather(nc, top, slot_rows, gather_row, half_weight, xres, out)


def kernel(**inputs):
    import numpy as np
    import concourse.bacc as bacc
    from concourse.bass_utils import run_bass_kernel_spmd

    get = lambda name: np.asarray(inputs[name])
    x = get("L0_attn_hidden_states")
    up = get("L0_ffn_w_fc").reshape(EXPERTS, HT, P, KC, P).transpose(0, 1, 4, 3, 2).reshape(EXPERTS * HT, P, D)
    down = get("L0_ffn_w_proj").reshape(EXPERTS, D, HT, P).transpose(0, 2, 3, 1).reshape(EXPERTS * HT, P, D)

    def pair_columns(w, width):
        return w.reshape(KC, P, PAIRS, 2 * width).transpose(2, 1, 0, 3)
    qks = np.concatenate([pair_columns(get("L0_attn_" + n), d) for n, d in (("Wq", DK), ("Wk", DK), ("Ws", M))], axis=3)
    vg = np.concatenate([pair_columns(get("L0_attn_" + n), DV) for n in ("Wv", "Wg")], axis=3)
    wo = get("L0_attn_Wo").reshape(PAIRS, 2, DV, D).transpose(0, 2, 1, 3)
    arrays = {
        "x": x.reshape(TOK, D),
        "wff": np.concatenate([up, down], axis=2),
        "router": get("L0_ffn_w_router"),
        "watt": np.concatenate([a.reshape(PAIRS, P, -1) for a in (qks, vg, wo)], axis=2),
        "gnorm": get("L0_attn_g_norm_weight").reshape(DV, 1),
    }
    arrays = {n: np.ascontiguousarray(a) for n, a in arrays.items()}
    nc = bacc.Bacc("TRN2", target_bir_lowering=False, num_devices=1)
    args = [nc.dram_tensor(n, a.shape, mybir.dt.from_np(a.dtype), kind="ExternalInput").ap() for n, a in arrays.items()]
    out = nc.dram_tensor("out", [TOK, D], F32, kind="ExternalOutput").ap()
    macaron(nc, *args, out)
    result = run_bass_kernel_spmd(nc, [arrays], core_ids=[0])
    return result.results[0]["out"].reshape(x.shape)
```

```python
from contextlib import ExitStack

import concourse.bass as bass
from concourse import mybir

F32 = mybir.dt.float32
F32R = mybir.dt.float32r
I32 = mybir.dt.int32
ALU = mybir.AluOpType
ACT = mybir.ActivationFunctionType
AX = mybir.AxisListType

P = 128
BATCH, SEQ, D = 2, 1024, 512
TOK = BATCH * SEQ
TILES = TOK // P
KC = D // P
EPS = 1e-5

EXPERTS, HIDDEN = 2, 2048
HT = HIDDEN // P
GROUP = 512
GROUPS = TOK // GROUP
SLOTS = GROUPS + 1
BLOCK = GROUP // 2
BLOCKS = TOK // BLOCK
GT = GROUP // P
RT = 4
RING = 4
GATHERS = 6
AHEAD = 2
assert HT % RING == 0 and HT == TILES and TILES == RT * GT

HEADS, DK, DV, M = 16, 64, 128, 64
PAIRS = HEADS // 2
CHUNK = P
UNIT = 512
UC = UNIT // CHUNK
UNITS = TOK // UNIT
HALVES = SEQ // UNIT
CLAMP = 32.0

QKS = KC * 3 * P
VG = KC * 4 * P
WO = 2 * D
PIECE = 1024
PIECES = [(0, QKS // 2), (QKS // 2, QKS // 2), (QKS, PIECE), (QKS + PIECE, PIECE), (QKS + VG, WO)]


def phase_constants(nc, top):
    c = {}
    c["ident"] = top.enter_context(nc.sbuf_tensor("ident", [P, P], F32))
    c["causal"] = top.enter_context(nc.sbuf_tensor("causal", [P, P], F32))
    c["ones"] = top.enter_context(nc.sbuf_tensor("ones", [P, P], F32))
    c["later"] = top.enter_context(nc.sbuf_tensor("later", [P, P], F32))
    c["minus_half"] = top.enter_context(nc.sbuf_tensor("minus_half", [P, TILES], F32))
    const_set = top.enter_context(nc.semaphore("const_set"))
    const_done = top.enter_context(nc.semaphore("const_done"))
    with nc.Block() as block:
        @block.gpsimd
        def _(pool):
            pool.memset(c["ident"][:], 0.0).then_inc(const_set, 1)
            pool.memset(c["causal"][:], 1.0).then_inc(const_set, 1)
            pool.memset(c["later"][:], 1.0).then_inc(const_set, 1)
            pool.memset(c["ones"][:], 1.0)
            pool.memset(c["minus_half"][:], -0.5)
            pool.wait_ge(const_set, 3)
            pool.affine_select(out=c["ident"][:], in_=c["ident"][:], compare_op=ALU.not_equal, fill=1.0,
                               base=0, pattern=[[-1, P]], channel_multiplier=1).then_inc(const_done, 1)
            pool.affine_select(out=c["causal"][:], in_=c["causal"][:], compare_op=ALU.is_ge, fill=0.0,
                               base=0, pattern=[[1, P]], channel_multiplier=-1).then_inc(const_done, 1)
            pool.affine_select(out=c["later"][:], in_=c["later"][:], compare_op=ALU.is_gt, fill=0.0,
                               base=0, pattern=[[-1, P]], channel_multiplier=1).then_inc(const_done, 1)
            pool.wait_ge(const_done, 3)
    return c


def choose(dve, step, r, at, is1_done):
    dve.tensor_scalar(r["is1"][:, at], r["gap"][:, at], 0.0, None, ALU.is_lt).then_inc(is1_done, 1)
    step(dve.scalar_tensor_tensor(out=r["base"][:, at], in0=r["gap"][:, at], scalar=0.0, in1=r["rest"][:, at], op0=ALU.is_lt, op1=ALU.mult))
    step(dve.tensor_tensor(r["base"][:, at], r["base"][:, at], r["tok"][:, at], ALU.add))


def place(dve, step, r, at, later, total, rank_mm, n, rows_ready):
    dve.wait_ge(rank_mm, n)
    step(dve.tensor_tensor_scan(out=r["cum"][:, at], data0=total, data1=r["zero"][:, at],
                                initial=r["cum"][:, at.start - 1:at.start] if at.start else 0.0, op0=ALU.add, op1=ALU.add))
    step(dve.tensor_tensor(r["behind"][:, at], later, r["cum"][:, at], ALU.subtract))
    dve.tensor_tensor(r["row_i"][:, at], r["base"][:, at], r["behind"][:, at], ALU.add).then_inc(rows_ready, 1)
    step(dve.tensor_tensor(r["pos"][:, at], r["base"][:, at], r["behind"][:, at], ALU.add))


def phase_feed_forward(nc, top, tag, c, x_in, router, wff, watt, xres, norms, r, aw, half_weight, gather_row, slot_table, sorted_rows, slot_rows,
                       loaded=None, sorted_marks=None, y_out=None):
    with ExitStack() as ctx:
        sb = lambda n, s, d=F32: ctx.enter_context(nc.sbuf_tensor(tag + n, s, d))
        sem = lambda n: top.enter_context(nc.semaphore(tag + n))
        wdiff = norms["wdiff"]
        rows = sb("rt_router", [P, EXPERTS, D]) if x_in is not None else None
        stats = sb("rt_stats", [P, TILES, 6])
        mv, vare, nmean, rstd, shift = (norms[n] for n in ("mv", "vare", "nmean", "rstd", "shift"))
        gap, is1, cum, zero, tok, rest, behind, pos, row_i, slot = (r[n] for n in (
            "gap", "is1", "cum", "zero", "tok", "rest", "behind", "pos", "row_i", "slot"))
        mag = sb("rt_mag", [P, TILES])
        em = sb("rt_em", [P, TILES])
        if x_in is not None:
            tok_i = sb("rt_tok_i", [P, TILES], I32)
            slot_i = sb("rt_slot_i", [P, BLOCKS], I32)
        blocks = sb("rt_blocks", [P, BLOCKS])
        border = sb("rt_border", [P, 6])
        inside = sb("rt_inside", [P, TILES])
        table = sb("rt_table", [P, 2, 8])
        in_loaded = [sem(f"rt_in_loaded{i}") for i in range(TILES // RT)] if x_in is not None else []
        if x_in is not None:
            iota_done = sem("rt_iota")
            r_loaded, var_ready, rstd_done, shift_done = sem("rt_r_loaded"), sem("rt_var_ready"), sem("rt_rstd_done"), sem("rt_shift_done")
        xn_done = sem("rt_xn_done")
        mag_done = sem("rt_mag_done")
        em_done = sem("rt_em_done")
        is1_done = sem("rt_is1_done")
        rank_mm = sem("rt_rank_mm")
        rows_ready = sem("rt_rows_ready")
        scattered = sem("rt_scattered")
        table_ready = sem("rt_table_ready")
        dve_step = sem("rt_dve_step")
        stage = sb("ff_stage", [P, RING, 2 * D])
        w_hi = sb("ff_w_hi", [P, RING, 2 * D], F32R)
        w_lo = sb("ff_w_lo", [P, RING, 2 * D], F32R)
        xg = sb("ff_xg", [P, GT, D])
        xT_hi = sb("ff_xT_hi", [P, KC, GROUP], F32R)
        xT_lo = sb("ff_xT_lo", [P, KC, GROUP], F32R)
        square = sb("ff_square", [P, 2, GROUP])
        factor = sb("ff_factor", [P, 2, GROUP])
        a = sb("ff_a", [P, 2, GROUP])
        a_hi = sb("ff_a_hi", [P, RING, GROUP], F32R)
        a_lo = sb("ff_a_lo", [P, RING, GROUP], F32R)
        y = sb("ff_y", [P, GT, D])
        xn_rest = sb("ff_xn_rest", [P, TILES - 2 * GT - 2, D])
        ps_y = [ctx.enter_context(nc.psum_tensor(f"{tag}ff_ps_y{t}", [P, D], F32)) for t in range(GT)]
        ps_h = [ctx.enter_context(nc.psum_tensor(f"{tag}ff_ps_h{t}", [P, GROUP], F32)) for t in range(2)]
        ps_x = [ctx.enter_context(nc.psum_tensor(f"{tag}ff_ps_x{t}", [P, GROUP], F32)) for t in range(2)]
        ps_later, ps_total = [b[:, 0:RT] for b in ps_y], [b[:, RT:2 * RT] for b in ps_y]
        w_loaded = [sem(f"ff_w_loaded{r}") for r in range(RING)]
        x_loaded = sem("ff_x_loaded")
        w_hi_done = sem("ff_w_hi_done")
        w_lo_done = sem("ff_w_lo_done")
        x_turned = sem("ff_x_turned")
        x_hi_done = sem("ff_x_hi_done")
        x_lo_done = sem("ff_x_lo_done")
        up_done = sem("ff_up_done")
        square_done = sem("ff_square_done")
        factor_done = sem("ff_factor_done")
        a_done = sem("ff_a_done")
        a_hi_done = sem("ff_a_hi_done")
        a_lo_done = sem("ff_a_lo_done")
        down_done = sem("ff_down_done")
        y_act = sem("ff_y_act")
        y_dve = sem("ff_y_dve")
        y_stored = sem("ff_y_stored")
        y_free = sem("ff_y_free")
        if y_out is not None:
            marks = sb("rt_marks", [P, TILES, 2])
            late = sb("ff_late", [P, BLOCK // P, 2])
            late_i = sb("ff_late_i", [P, BLOCK // P], I32)
            ring = [xn_rest[:, n, :] for n in range(GATHERS)]
            loaded_before = [16 * len(range(n, TILES, GATHERS)) for n in range(GATHERS)]
            marks_ready, marked, late_loaded, late_known = sem("rt_marks_ready"), sem("rt_marked"), sem("ff_late_loaded"), sem("ff_late_known")
            added, stored = sem("ff_added"), sem("ff_stored")
            back_loaded, back_added, back_stored = sem("ff_back_loaded"), sem("ff_back_added"), sem("ff_back_stored")
        block = ctx.enter_context(nc.Block())
        steps = range(0 if x_in is not None else TILES // RT - 1, TILES // RT)
        tiles_here = len(steps) * RT
        tiles = lambda g: slice(g * RT, (g + 1) * RT)
        piece_step = HT // (len(PIECES) - 1)
        takes_piece = lambda j, t: x_in is not None and isinstance(j, int) and j == GROUPS - 1 and t % piece_step == 0

        def normed(i):
            for room in (xg, y, a):
                if i < room.shape[1]:
                    return room[:, i, :]
                i -= room.shape[1]
            return xn_rest[:, i, :]

        def all_slots(engine, slot_body):
            with engine.Fori(0, GROUPS - 1) as j:
                slot_body(j, GROUP, GROUP)
            slot_body(GROUPS - 1, GROUP, BLOCK)
            slot_body(GROUPS, BLOCK, 0)

        @block.sync
        def _(sp):
            if x_in is not None:
                for g in steps:
                    sp.dma_start(xres[:, tiles(g), :], x_in.rearrange("(i p) d -> p i d", p=P)[:, tiles(g), :]).then_inc(in_loaded[g], 16)
                    if g == 0:
                        sp.dma_start(rows[:, :, :], router.rearrange("e d -> (e d)").partition_broadcast(P).rearrange("p (e d) -> p e d", e=EXPERTS)).then_inc(r_loaded, 16)

            def load_w(tile0, t):
                sp.dma_start(stage[:, t % RING, :], wff[bass.ds(tile0 + t % HT, 1), :, :].rearrange("a p n -> (a p) n")).then_inc(w_loaded[t % RING], 16)
            sp.wait_ge(table_ready, 1)
            first = sp.value_load(slot_table[0:1, 0, 0:1], min_val=0, max_val=HT)
            for t in range(AHEAD):
                load_w(first, t)
            sp.wait_ge(scattered, 16 * tiles_here)
            sp.dma_start(xg[:, :, :], sorted_rows[0:GROUP, :].rearrange("(i p) d -> p i d", p=P)).then_inc(x_loaded, 16)
            for t in range(AHEAD, RING):
                load_w(first, t)

            def slot_body(j, width, after):
                tile0 = sp.value_load(slot_table[0:1, 0, bass.ds(j, 1)], min_val=0, max_val=HT)
                if after:
                    tile0_next = sp.value_load(slot_table[0:1, 0, bass.ds(j + 1, 1)], min_val=0, max_val=HT)
                for t in range(RING, HT + RING):
                    if after and t == 2 * RING:
                        sp.wait_ge(x_turned, j * KC + KC)
                        if after == GROUP:
                            row = (j + 1) * GROUP
                        else:
                            row = sp.value_load(slot_table[0:1, 1, GROUPS:SLOTS], min_val=0, max_val=TOK - BLOCK)
                        sp.dma_start(xg[:, 0:after // P, :], sorted_rows[bass.ds(row, after), :].rearrange("(i p) d -> p i d", p=P)).then_inc(x_loaded, 16)
                        if y_out is not None and after == BLOCK:
                            sp.wait_ge(marked, 16 * TILES)
                            sp.dma_start(late[:, :, :], sorted_marks[bass.ds(row, BLOCK), :].rearrange("(i p) c -> p i c", p=P)).then_inc(late_loaded, 16)
                    if takes_piece(j, t):
                        piece = t // piece_step - 1
                        col, width_p = PIECES[piece]
                        if piece > 0:
                            sp.wait_ge(aw["piece_lo"], piece + 1)
                        sp.dma_start(aw["stage"][:, 0:width_p], watt[0, :, col:col + width_p]).then_inc(aw["piece_loaded"], 16)
                    if after or t < HT:
                        sp.wait_ge(w_hi_done, j * HT + t + 1)
                        sp.wait_ge(w_lo_done, j * HT + t + 1)
                        load_w(tile0 if t < HT else tile0_next, t)
            all_slots(sp, slot_body)
            if y_out is not None:
                for i in range(TILES):
                    sp.wait_ge(added, i + 1)
                    sp.dma_start(y_out[i * P:(i + 1) * P, :], xres[:, i, :]).then_inc(stored, 16)
                sp.wait_ge(stored, 16 * TILES)

        @block.gpsimd
        def _(pool):
            if x_in is not None:
                pool.iota(tok_i[:], pattern=[[P, TILES]], base=0, channel_multiplier=1).then_inc(iota_done, 1)
                pool.iota(slot_i[:], pattern=[[1, BLOCKS]], base=0, channel_multiplier=0).then_inc(iota_done, 1)

            def norm(g):
                pool.wait_ge(var_ready, g + 1)
                pool.tensor_tensor(rstd[:, tiles(g)], vare[:, tiles(g)], c["minus_half"][:, tiles(g)], ALU.pow).then_inc(rstd_done, 1)
                pool.wait_ge(rstd_done, g + 1)
                pool.tensor_tensor(shift[:, tiles(g)], nmean[:, tiles(g)], rstd[:, tiles(g)], ALU.mult).then_inc(shift_done, 1)

            def scatter(g):
                pool.wait_ge(rows_ready, g - steps[0] + 1)
                for i in range(g * RT, (g + 1) * RT):
                    pool.indirect_dma_start(out=sorted_rows, out_offset=bass.IndirectOffsetOnAxis(ap=row_i[:, i:i + 1], axis=0),
                                            in_=normed(i), in_offset=None).then_inc(scattered, 16)
            if x_in is not None:
                norm(0)
                norm(1)
            for g in steps:
                if x_in is not None and g + 2 in steps:
                    norm(g + 2)
                scatter(g)

            if y_out is not None:
                pool.wait_ge(marks_ready, 1)
                for i in range(TILES):
                    pool.indirect_dma_start(out=sorted_marks, out_offset=bass.IndirectOffsetOnAxis(ap=row_i[:, i:i + 1], axis=0),
                                            in_=marks[:, i, :], in_offset=None).then_inc(marked, 16)

            def finish():
                pool.wait_ge(scattered, 16 * tiles_here)
                for i in range(TILES):
                    if i >= GATHERS:
                        pool.wait_ge(added, i - GATHERS + 1)
                    pool.indirect_dma_start(out=ring[i % GATHERS], out_offset=None, in_=slot_rows,
                                            in_offset=bass.IndirectOffsetOnAxis(ap=gather_row[:, i:i + 1], axis=0)).then_inc(loaded[i % GATHERS], 16)
                pool.wait_ge(late_known, 1)
                pool.wait_ge(stored, 16 * TILES)
                for i in range(BLOCK // P):
                    pool.indirect_dma_start(out=y[:, i, :], out_offset=None, in_=y_out,
                                            in_offset=bass.IndirectOffsetOnAxis(ap=late_i[:, i:i + 1], axis=0)).then_inc(back_loaded, 16)
                for i in range(BLOCK // P):
                    pool.wait_ge(back_added, i + 1)
                    pool.indirect_dma_start(out=y_out, out_offset=bass.IndirectOffsetOnAxis(ap=late_i[:, i:i + 1], axis=0),
                                            in_=y[:, i, :], in_offset=None).then_inc(back_stored, 16)
                pool.wait_ge(back_stored, 16 * (BLOCK // P))

            def slot_body(j, width, after):
                if y_out is not None and not after:
                    finish()
                    return
                for t in range(HT):
                    if takes_piece(j, t):
                        piece = t // piece_step
                        col, width_p = PIECES[piece]
                        pool.wait_ge(aw["piece_hi"], piece + 1)
                        pool.tensor_tensor(aw["lo"][:, col:col + width_p], aw["stage"][:, 0:width_p],
                                           aw["hi"][:, col:col + width_p].bitcast(F32), ALU.subtract).then_inc(aw["piece_lo"], 1)
                pool.wait_ge(y_act, j * 2 + width // P // 2 + 1)
                pool.wait_ge(y_dve, j * 2 + width // P // 2 + 1)
                pool.dma_start(slot_rows[bass.ds(j * GROUP, width), :].rearrange("(i p) d -> p i d", p=P), y[:, 0:width // P, :]).then_inc(y_stored, 16)
                pool.wait_ge(y_stored, j * 16 + 16)
                pool.sem_inc(y_free, 1)
            pool.sem_inc(y_free, 1)
            if x_in is not None:
                pool.sem_inc(aw["piece_lo"], 1)
            all_slots(pool, slot_body)
            pool.wait_ge(scattered, 16 * tiles_here)

        @block.scalar
        def _(act):
            for g in steps:
                if x_in is not None:
                    act.wait_ge(shift_done, g + 1)
                for i in range(g * RT, (g + 1) * RT):
                    act.activation(normed(i), xres[:, i, :], ACT.Identity, bias=shift[:, i:i + 1],
                                   scale=rstd[:, i:i + 1]).then_inc(xn_done, 1)
            act.wait_ge(mag_done, 1)
            act.activation(em[:], mag[:], ACT.Exp, scale=-1.0).then_inc(em_done, 1)

            def split_w(j, t):
                act.wait_ge(w_loaded[t % RING], (j * (HT // RING) + t // RING + 1) * 16)
                act.wait_ge(down_done, j * HT + t + 1)
                act.activation(w_hi[:, t % RING, :], stage[:, t % RING, :], ACT.Copy).then_inc(w_hi_done, 1)

            def split_x(j, width, k0, k1):
                for k in range(k0, k1):
                    act.wait_ge(x_turned, j * KC + k + 1)
                    act.activation(xT_hi[:, k, 0:width], ps_x[k % 2][:, 0:width], ACT.Copy).then_inc(x_hi_done, 1)
            act.sem_inc(w_hi_done, RING)
            act.sem_inc(y_act, 1)
            act.sem_inc(square_done, 2)
            act.wait_ge(down_done, RING)
            for t in range(AHEAD):
                split_w(0, t)
            split_x(0, GROUP, 0, KC)

            def slot_body(j, width, after):
                for t in range(HT):
                    if t == 0:
                        split_w(j, AHEAD)
                    act.wait_ge(up_done, j * HT + t + 1)
                    act.activation(square[:, t % 2, 0:width], ps_h[t % 2][:, 0:width], ACT.Square).then_inc(square_done, 1)
                    if 0 < t < HT - AHEAD:
                        split_w(j, t + AHEAD)
                    if after and t == HT - 1:
                        split_x(j + 1, after, 0, 2)
                    act.wait_ge(a_done, j * HT + t + 1)
                    act.activation(a_hi[:, t % RING, 0:width], a[:, t % 2, 0:width], ACT.Copy).then_inc(a_hi_done, 1)
                    if after and t + AHEAD >= HT:
                        split_w(j, t + AHEAD)
                    if takes_piece(j, t - piece_step // 2):
                        piece = t // piece_step
                        col, width_p = PIECES[piece]
                        act.wait_ge(aw["piece_loaded"], (piece + 1) * 16)
                        act.activation(aw["hi"][:, col:col + width_p], aw["stage"][:, 0:width_p], ACT.Copy).then_inc(aw["piece_hi"], 1)
                if after:
                    split_x(j + 1, after, 2, KC)
                elif y_out is not None:
                    return
                act.wait_ge(y_free, j + 1)
                act.wait_ge(down_done, j * HT + HT + RING)
                for i in range(0, width // P, 2):
                    act.activation(y[:, i, :], ps_y[i][:, :], ACT.Copy).then_inc(y_act, 1)
            all_slots(act, slot_body)

        @block.vector
        def _(dve):
            n = [0]

            def step(ins):
                n[0] += 1
                ins.then_inc(dve_step, 1)
                dve.wait_ge(dve_step, n[0])

            def statistics(g):
                dve.wait_ge(in_loaded[g], 16)
                for i in range(g * RT, (g + 1) * RT):
                    last = dve.bn_stats(stats[:, i, :], xres[:, i, :])
                step(last)
                for i in range(g * RT, (g + 1) * RT):
                    last = dve.bn_aggr(mv[:, i, :], stats[:, i, :])
                step(last)
                dve.tensor_scalar(nmean[:, tiles(g)], mv[:, tiles(g), 0], -1.0, None, ALU.mult)
                dve.tensor_scalar(vare[:, tiles(g)], mv[:, tiles(g), 1], EPS, None, ALU.add).then_inc(var_ready, 1)

            def covered(g):
                return x_in is not None and g + 2 in steps

            def route(g):
                for i in range(g * RT, (g + 1) * RT):
                    if i == g * RT + RT // 2 and g - 1 in steps and not covered(g - 1):
                        place_step(g - 1)
                    dve.wait_ge(xn_done, i - steps[0] * RT + 1)
                    last = dve.tensor_tensor_reduce(out=(square, square, factor, factor)[i % RT][:, i % 2, :], in0=normed(i), in1=wdiff[:], scale=1.0, scalar=0.0,
                                                    op0=ALU.mult, op1=ALU.add, accum_out=gap[:, i:i + 1])
                step(last)
                choose(dve, step, r, tiles(g), is1_done)

            def place_step(g):
                place(dve, step, r, tiles(g), ps_later[g], ps_total[g], rank_mm, 2 * (g - steps[0]) + 2, rows_ready)
            if x_in is not None:
                dve.memset(zero[:], 0.0)
                dve.wait_ge(iota_done, 2)
                dve.tensor_copy(slot[:], slot_i[:])
                step(dve.tensor_copy(tok[:], tok_i[:]))
                dve.tensor_scalar(rest[:], tok[:], -1.0, float(TOK), ALU.mult, ALU.add)
                statistics(0)
                dve.wait_ge(r_loaded, 16)
                step(dve.tensor_tensor(wdiff[:], rows[:, 0, :], rows[:, 1, :], ALU.subtract))
                statistics(1)
            for g in steps:
                route(g)
                if covered(g):
                    statistics(g + 2)
                    place_step(g)
            place_step(steps[-1])
            dve.scalar_tensor_tensor(out=mag[:], in0=gap[:], scalar=-1.0, in1=gap[:], op0=ALU.mult, op1=ALU.max).then_inc(mag_done, 1)
            step(dve.tensor_scalar(border[:, 0:1], cum[:, TILES - 1:TILES], -1.0, float(TOK), ALU.mult, ALU.add))
            dve.tensor_scalar(blocks[:], slot[:], float(BLOCK), border[:, 0:1], ALU.mult, ALU.is_lt)
            step(dve.tensor_scalar(table[:, 1, 0:GROUPS], slot[:, 0:GROUPS], float(GROUP), float(BLOCK), ALU.mult, ALU.add))
            dve.tensor_reduce(border[:, 1:2], blocks[:], op=ALU.add, axis=AX.X)
            step(dve.tensor_scalar(table[:, 0, 0:GROUPS], table[:, 1, 0:GROUPS], border[:, 0:1], None, ALU.is_ge))
            step(dve.tensor_reduce(border[:, 2:3], table[:, 0, 0:GROUPS], op=ALU.add, axis=AX.X))
            step(dve.tensor_scalar(border[:, 2:3], border[:, 2:3], -2.0, float(1 + 2 * GROUPS), ALU.mult, ALU.add))
            step(dve.tensor_tensor(table[:, 0, GROUPS:SLOTS], border[:, 2:3], border[:, 1:2], ALU.subtract))
            dve.tensor_copy(border[:, 5:6], table[:, 0, GROUPS:SLOTS])
            step(dve.tensor_scalar(border[:, 3:4], border[:, 1:2], -1.0, 0.0, ALU.add, ALU.max))
            step(dve.tensor_scalar(table[:, 1, GROUPS:SLOTS], border[:, 3:4], float(BLOCK), None, ALU.mult))
            dve.tensor_copy(slot_table[:, 1, GROUPS:SLOTS], table[:, 1, GROUPS:SLOTS])
            dve.tensor_scalar(slot_table[:, 0, 0:SLOTS], table[:, 0, 0:SLOTS], float(HT), None, ALU.mult).then_inc(table_ready, 1)
            step(dve.tensor_scalar(behind[:], pos[:], table[:, 1, GROUPS:SLOTS], None, ALU.subtract))
            step(dve.tensor_scalar(inside[:], behind[:], 0.0, None, ALU.is_ge))
            step(dve.scalar_tensor_tensor(out=inside[:], in0=behind[:], scalar=float(BLOCK), in1=inside[:], op0=ALU.is_lt, op1=ALU.mult))
            step(dve.scalar_tensor_tensor(out=inside[:], in0=is1[:], scalar=border[:, 5:6], in1=inside[:], op0=ALU.is_equal, op1=ALU.mult))
            if y_out is None:
                step(dve.tensor_scalar(border[:, 4:5], table[:, 1, GROUPS:SLOTS], -1.0, float(TOK), ALU.mult, ALU.add))
                step(dve.scalar_tensor_tensor(out=pos[:], in0=inside[:], scalar=border[:, 4:5], in1=pos[:], op0=ALU.mult, op1=ALU.add))
            dve.tensor_copy(gather_row[:], pos[:])
            dve.wait_ge(em_done, 1)
            step(dve.tensor_scalar(em[:], em[:], 1.0, None, ALU.add))
            step(dve.reciprocal(half_weight[:], em[:]))
            step(dve.tensor_scalar(half_weight[:], half_weight[:], 0.5, None, ALU.mult))
            if y_out is not None:
                dve.tensor_copy(marks[:, :, 0], tok[:])
                step(dve.tensor_tensor(marks[:, :, 1], half_weight[:], inside[:], ALU.mult))
                dve.tensor_tensor(half_weight[:], half_weight[:], marks[:, :, 1], ALU.subtract).then_inc(marks_ready, 1)

            def split_w(j, t):
                dve.wait_ge(w_hi_done, j * HT + t + 1 + RING)
                dve.tensor_tensor(w_lo[:, t % RING, :], stage[:, t % RING, :], w_hi[:, t % RING, :].bitcast(F32),
                                  ALU.subtract).then_inc(w_lo_done, 1)

            def split_x(j, width, k0, k1):
                for k in range(k0, k1):
                    dve.wait_ge(x_hi_done, j * KC + k + 1)
                    dve.tensor_tensor(xT_lo[:, k, 0:width], ps_x[k % 2][:, 0:width], xT_hi[:, k, 0:width].bitcast(F32),
                                      ALU.subtract).then_inc(x_lo_done, 1)
            dve.sem_inc(w_lo_done, RING)
            dve.sem_inc(y_dve, 1)
            dve.sem_inc(factor_done, 2)
            for t in range(AHEAD):
                split_w(0, t)
            split_x(0, GROUP, 0, KC)

            behind_by = 3

            def add_row(i):
                dve.wait_ge(loaded[i % GATHERS], loaded_before[i % GATHERS] + 16 * (i // GATHERS + 1))
                dve.scalar_tensor_tensor(out=xres[:, i, :], in0=ring[i % GATHERS], scalar=half_weight[:, i:i + 1],
                                         in1=xres[:, i, :], op0=ALU.mult, op1=ALU.add).then_inc(added, 1)

            def slot_body(j, width, after):
                finishes = y_out is not None and not after
                if finishes:
                    dve.wait_ge(late_loaded, 16)
                    dve.tensor_copy(late_i[:, :], late[:, :, 0]).then_inc(late_known, 1)
                for t in range(HT):
                    if t == 0:
                        split_w(j, AHEAD)
                    dve.wait_ge(square_done, j * HT + t + 3)
                    dve.tensor_scalar(factor[:, t % 2, 0:width], ps_h[t % 2][:, 0:width], 0.0, 0.25, ALU.is_ge, ALU.max).then_inc(factor_done, 1)
                    dve.wait_ge(factor_done, j * HT + t + 3)
                    dve.tensor_tensor(a[:, t % 2, 0:width], square[:, t % 2, 0:width], factor[:, t % 2, 0:width], ALU.mult).then_inc(a_done, 1)
                    if finishes and t >= behind_by:
                        late_tiles = t - (HT - behind_by)
                        for i in (t - behind_by,) if late_tiles < 0 else (HT - 2 * behind_by + 2 * late_tiles, HT - 2 * behind_by + 2 * late_tiles + 1):
                            add_row(i)
                    if 0 < t < HT - AHEAD:
                        split_w(j, t + AHEAD)
                    if after and t == HT - 1:
                        split_x(j + 1, after, 0, 2)
                    dve.wait_ge(a_hi_done, j * HT + t + 1)
                    dve.tensor_tensor(a_lo[:, t % RING, 0:width], a[:, t % 2, 0:width], a_hi[:, t % RING, 0:width].bitcast(F32),
                                      ALU.subtract).then_inc(a_lo_done, 1)
                    if after and t + AHEAD >= HT:
                        split_w(j, t + AHEAD)
                if after:
                    split_x(j + 1, after, 2, KC)
                if finishes:
                    dve.wait_ge(back_loaded, 16 * (BLOCK // P))
                    dve.wait_ge(down_done, j * HT + HT + RING)
                    for i in range(BLOCK // P):
                        dve.scalar_tensor_tensor(out=y[:, i, :], in0=ps_y[i][:, :], scalar=late[:, i, 1:2], in1=y[:, i, :],
                                                 op0=ALU.mult, op1=ALU.add).then_inc(back_added, 1)
                    return
                dve.wait_ge(y_free, j + 1)
                dve.wait_ge(down_done, j * HT + HT + RING)
                for i in range(1, width // P, 2):
                    dve.tensor_copy(y[:, i, :], ps_y[i][:, :]).then_inc(y_dve, 1)
            all_slots(dve, slot_body)

        @block.tensor
        def _(pe):
            for g in steps:
                pe.wait_ge(is1_done, g - steps[0] + 1)
                pe.matmul(ps_later[g], c["later"][:], is1[:, tiles(g)], start=True, stop=True).then_inc(rank_mm, 1)
                pe.matmul(ps_total[g], c["ones"][:], is1[:, tiles(g)], start=True, stop=True).then_inc(rank_mm, 1)

            def turn_x(j, width, k0, k1, first=False):
                if k0 == 0:
                    pe.wait_ge(x_loaded, j * 16 + 16)
                for k in range(k0, k1):
                    if not first or k >= 2:
                        pe.wait_ge(x_lo_done, j * KC + k - 1)
                    for i in range(width // P):
                        last = pe.transpose(ps_x[k % 2][:, i * P:(i + 1) * P], xg[:, i, k * P:(k + 1) * P], c["ident"][:])
                    last.then_inc(x_turned, 1)
            pe.sem_inc(down_done, RING)
            turn_x(0, GROUP, 0, KC, first=True)

            def slot_body(j, width, after):
                def up(t):
                    r = t % RING
                    pe.wait_ge(w_lo_done, j * HT + t + 1 + RING)
                    pe.wait_ge(square_done, j * HT + t + 1)
                    pe.wait_ge(factor_done, j * HT + t + 1)
                    parts = ((w_lo, xT_hi), (w_hi, xT_lo), (w_hi, xT_hi))
                    for k in range(KC):
                        if t == 0:
                            pe.wait_ge(x_lo_done, j * KC + k + 1)
                        for n, (w, x) in enumerate(parts):
                            last = pe.matmul(ps_h[t % 2][:, 0:width], w[:, r, k * P:(k + 1) * P], x[:, k, 0:width],
                                             start=(k == 0 and n == 0), stop=(k == KC - 1 and n == 2))
                    last.then_inc(up_done, 1)

                def down(t):
                    r = t % RING
                    pe.wait_ge(a_lo_done, j * HT + t + 1)
                    if t == 0:
                        pe.wait_ge(y_act, j * 2 + 1)
                        pe.wait_ge(y_dve, j * 2 + 1)
                    for i in range(width // P):
                        for n, (x, w) in enumerate(((a_lo, w_hi), (a_hi, w_lo), (a_hi, w_hi))):
                            last = pe.matmul(ps_y[i][:, :], x[:, r, i * P:(i + 1) * P], w[:, r, D:2 * D],
                                             start=(t == 0 and n == 0), stop=(t == HT - 1 and n == 2))
                    last.then_inc(down_done, 1)
                for t in range(AHEAD):
                    up(t)
                for t in range(HT):
                    if t + AHEAD < HT:
                        up(t + AHEAD)
                    if after and t == HT - 4:
                        turn_x(j + 1, after, 0, 2)
                    if after and t == HT - 1:
                        turn_x(j + 1, after, 2, KC)
                    down(t)
            all_slots(pe, slot_body)


HK_STEPS = [UC if k % HALVES == 0 else UC - 1 for k in range(UNITS)]
HK_AT = [sum(HK_STEPS[:k]) for k in range(UNITS + 1)]


def phase_attention(nc, top, c, watt, gnorm, slot_rows, gather_row, half_weight, xres, norms, routing, loaded, sorted_rows, aw):
    with ExitStack() as ctx:
        sb = lambda n, s, d=F32: ctx.enter_context(nc.sbuf_tensor(n, s, d))
        sem = lambda n: top.enter_context(nc.semaphore(n))
        xT_hi = sb("at_xT_hi", [P, KC, TOK], F32R)
        xT_lo = sb("at_xT_lo", [P, KC, TOK], F32R)
        stage, w_hi, w_lo = aw["stage"], aw["hi"], aw["lo"]
        gn = sb("at_gn", [DV, 1])
        qT = sb("at_qT", [P, 2, UNIT])
        kT = sb("at_kT", [P, UNIT])
        eT = sb("at_eT", [P, 2, UNIT])
        zT = sb("at_zT", [P, UNIT])
        zlast = sb("at_zlast", [P, 1])
        v = sb("at_v", [P, 2, UC, 2 * DV])
        gate = sb("at_gate", [P, 2, UC, 2 * DV])
        en = sb("at_en", [P, UC, P])
        kn = sb("at_kn", [P, UC, P])
        rz = sb("at_rz", [P, UC, P])
        am = sb("at_am", [P, 2, UC, P])
        hk = sb("at_hk", [P, UC, P])
        hv = sb("at_hv", [P, UC, 2 * DV])
        ok = sb("at_ok", [P, UC, P])
        pv = sb("at_pv", [P, UC, P])
        pT = sb("at_pT", [P, UNIT])
        u = sb("at_u", [P, 2, UC, DV])
        uT_hi = sb("at_uT_hi", [P, 2, 2, 2 * P], F32R)
        uT_lo = sb("at_uT_lo", [P, 2, 2, 2 * P], F32R)
        highest = sb("at_highest", [P, 2 * UC])
        den = sb("at_den", [P, 2 * UC])
        ss = sb("at_ss", [P, 2 * UC])
        ms = sb("at_ms", [P, 2 * UC])
        coef = sb("at_coef", [P, 2 * UC])
        PJ = [ctx.enter_context(nc.psum_tensor(f"at_pj{b}", [P, 512], F32)) for b in range(2)]
        R = [ctx.enter_context(nc.psum_tensor(f"at_r{b}", [P, 512], F32)) for b in range(6)]

        ring = [x[:, n * D // width:(n + 1) * D // width, :].rearrange("p a b -> p (a b)") for x, width in
                ((am[:, :, :, :].rearrange("p a b c -> p (a b) c"), P), (u[:, :, :, :].rearrange("p a b c -> p (a b) c"), DV), (hv, 2 * DV)) for n in range(2)]
        xn = [x[:, :, :].rearrange("p a b -> p (a b)") for x in (en, kn, ok, pv)]
        row_added, shift_done, xn_done, x_turned = sem("at_row_added"), sem("at_shift_done"), sem("at_xn_done"), sem("at_x_turned")
        x_hi, x_lo = sem("at_x_hi"), sem("at_x_lo")
        assert len(ring) == GATHERS == len(R) and len(xn) == UC

        rt_rows = sb("at_rt_rows", [P, UC // 2, D])
        rt_xn = [rt_rows[:, n, :] for n in range(UC // 2)] + [stage[:, n * D:(n + 1) * D] for n in range(UC // 2)]
        rt_spare = [x[:, :, :].rearrange("p a b -> p (a b)") for x in (pv, rz, ok, kn)]
        rt_later, rt_total = R[4][:, 0:UC], R[4][:, UC:2 * UC]
        rt_step, is1_done, rank_mm, rows_ready, scattered = (
            sem("at_rt_step"), sem("at_is1_done"), sem("at_rank_mm"), sem("at_rows_ready"), sem("at_scattered"))

        gn_loaded = sem("at_gn_loaded")
        piece_loaded, piece_hi, piece_lo = aw["piece_loaded"], aw["piece_hi"], aw["piece_lo"]
        piece_scaled = sem("at_piece_scaled")
        bn = sb("at_bn", [P, UC, 6])
        mv, vare, nmean, rstd, shift = (norms[n] for n in ("mv", "vare", "nmean", "rstd", "shift"))
        bn_done, mv_done, var_ready, rstd_done = sem("at_bn_done"), sem("at_mv_done"), sem("at_var_ready"), sem("at_rstd_done")
        tiles = lambda m: slice(m * UC, (m + 1) * UC)
        q_mm, k_mm, s_mm, vg_mm = sem("at_q_mm"), sem("at_k_mm"), sem("at_s_mm"), sem("at_vg_mm")
        q_out, k_out, s_clipped, e_done, z_done = sem("at_q_out"), sem("at_k_out"), sem("at_s_clipped"), sem("at_e_done"), sem("at_z_done")
        z_kept = sem("at_z_kept")
        v_out, tanh_done, gate_done = sem("at_v_out"), sem("at_tanh_done"), sem("at_gate_done")
        e_tr, k_tr, z_tr = sem("at_e_tr"), sem("at_k_tr"), sem("at_z_tr")
        en_out, kn_out, rz_done = sem("at_en_out"), sem("at_kn_out"), sem("at_rz_done")
        dk_mm, hk_done = sem("at_dk_mm"), sem("at_hk_done")
        a_mm, a_masked = sem("at_a_mm"), sem("at_a_masked")
        ok_mm, ok_scaled, highest_done, ok_shifted = sem("at_ok_mm"), sem("at_ok_scaled"), sem("at_highest_done"), sem("at_ok_shifted")
        pv_done, den_done, pz_done = sem("at_pv_done"), sem("at_den_done"), sem("at_pz_done")
        p_tr, p_out = sem("at_p_tr"), sem("at_p_out")
        b_mm, b_masked = sem("at_b_mm"), sem("at_b_masked")
        dv_mm, hv_done = sem("at_dv_mm"), sem("at_hv_done")
        o_mm, squared, ss_done, eps_done, ms_done, coef_done, u_done = (
            sem("at_o_mm"), sem("at_squared"), sem("at_ss_done"), sem("at_eps_done"), sem("at_ms_done"), sem("at_coef_done"), sem("at_u_done"))
        u_tr, u_hi, u_lo = sem("at_u_tr"), sem("at_u_hi"), sem("at_u_lo")
        wo_mm, added = sem("at_wo_mm"), sem("at_added")
        block = ctx.enter_context(nc.Block())
        NP = len(PIECES)

        wq = lambda w, k, part: w[:, k * 3 * P + part * P:k * 3 * P + (part + 1) * P]
        wvg = lambda w, k: w[:, QKS + k * 4 * P:QKS + (k + 1) * 4 * P]
        wo = lambda w, h: w[:, QKS + VG + h * D:QKS + VG + (h + 1) * D]

        def count(i, k, per, done):
            return i * (UNITS * per) + (k * per + done + 1)

        @block.sync
        def _(sp):
            sp.dma_start(gn[:, :], gnorm).then_inc(gn_loaded, 16)
            def load(i, n, pair, piece):
                col, width = PIECES[piece]
                sp.wait_ge(piece_lo, i * NP + n + 4 + 1)
                sp.dma_start(stage[:, 0:width], watt[bass.ds(pair, 1), :, col:col + width].rearrange("a p n -> (a p) n")).then_inc(piece_loaded, 16)
            with sp.Fori(0, PAIRS - 1) as i:
                load(i, 0, i, 4)
                for n in range(4):
                    load(i, n + 1, i + 1, n)
            load(PAIRS - 1, 0, PAIRS - 1, 4)

        @block.gpsimd
        def _(pool):
            pool.sem_inc(coef_done, 1)

            def lo_piece(n, piece):
                col, width = PIECES[piece]
                pool.wait_ge(piece_hi, n + 1)
                pool.tensor_tensor(w_lo[:, col:col + width], stage[:, 0:width], w_hi[:, col:col + width].bitcast(F32),
                                   ALU.subtract).then_inc(piece_lo, 1)
            def gather(m):
                for t in range(m * UC, (m + 1) * UC):
                    if t >= GATHERS:
                        pool.wait_ge(row_added, t - GATHERS + 1)
                    pool.indirect_dma_start(out=ring[t % GATHERS], out_offset=None, in_=slot_rows,
                                            in_offset=bass.IndirectOffsetOnAxis(ap=gather_row[:, t:t + 1], axis=0)).then_inc(loaded[t % GATHERS], 16)
            gather(0)
            for m in range(UNITS):
                if m + 1 < UNITS:
                    gather(m + 1)
                pool.wait_ge(var_ready, m + 1)
                pool.tensor_tensor(rstd[:, tiles(m)], vare[:, tiles(m)], c["minus_half"][:, tiles(m)], ALU.pow).then_inc(rstd_done, 1)
                pool.wait_ge(rstd_done, m + 1)
                pool.tensor_tensor(shift[:, tiles(m)], nmean[:, tiles(m)], rstd[:, tiles(m)], ALU.mult).then_inc(shift_done, 1)
            pool.wait_ge(gn_loaded, 16)

            def pair(i, last):
                def norm(k):
                    for h in range(2):
                        cols = slice(h * UC, (h + 1) * UC)
                        pool.wait_ge(ms_done, count(i, k, 2, h + 1))
                        pool.tensor_tensor(coef[:, cols], ms[:, cols], c["minus_half"][:, cols], ALU.pow).then_inc(coef_done, 1)
                pool.wait_ge(piece_loaded, i * (NP * 16) + 5 * 16)
                pool.tensor_tensor(stage[:, 0:WO], stage[:, 0:WO], gn[:, 0:1].to_broadcast([P, WO]), ALU.mult).then_inc(piece_scaled, 1)
                lo_piece(i * NP + 4, 4)

                def next_norm(k):
                    pool.wait_ge(var_ready, UNITS + k + 1)
                    pool.tensor_tensor(rstd[:, tiles(k)], vare[:, tiles(k)], c["minus_half"][:, tiles(k)], ALU.pow).then_inc(rstd_done, 1)
                    pool.wait_ge(rstd_done, UNITS + k + 1)
                    pool.tensor_tensor(shift[:, tiles(k)], nmean[:, tiles(k)], rstd[:, tiles(k)], ALU.mult).then_inc(shift_done, 1)
                for k in range(UNITS):
                    if k >= 2 and not last:
                        for n in ((0,), (1, 2, 3))[k - 2]:
                            lo_piece(i * NP + 5 + n, n)
                    if last and k > 0:
                        next_norm(k - 1)
                    norm(k)
                    if last and k > 0:
                        pool.wait_ge(rows_ready, k)
                        for t in range((k - 1) * UC, k * UC):
                            pool.indirect_dma_start(out=sorted_rows, out_offset=bass.IndirectOffsetOnAxis(ap=routing["row_i"][:, t:t + 1], axis=0),
                                                    in_=rt_xn[t % UC], in_offset=None).then_inc(scattered, 16)
                if last:
                    next_norm(UNITS - 1)
                if last:
                    pool.wait_ge(scattered, 16 * UC * (UNITS - 1))
            with pool.Fori(0, PAIRS - 1) as i:
                pair(i, False)
            pair(PAIRS - 1, True)

        @block.scalar
        def _(act):
            for s in (q_out, e_done, v_out, tanh_done, en_out, pv_done, p_out, squared, u_hi):
                act.sem_inc(s, 1)

            def hi_piece(n, piece):
                col, width = PIECES[piece]
                act.wait_ge(piece_scaled if piece == 4 else piece_loaded, n)
                act.activation(w_hi[:, col:col + width], stage[:, 0:width], ACT.Copy).then_inc(piece_hi, 1)

            def q_scale(i, k):
                act.wait_ge(q_mm, count(i, k, 1, 0))
                act.activation(qT[:, k % 2, :], PJ[(7 * k) % 2][:, :], ACT.Copy, scale=float(DK) ** -0.5).then_inc(q_out, 1)

            def e_exp(i, k):
                act.wait_ge(s_clipped, count(i, k, 1, 1))
                act.activation(eT[:, k % 2, :], eT[:, k % 2, :], ACT.Exp).then_inc(e_done, 1)

            def vg_read(i, k, t):
                bank = PJ[(7 * k + 3 + t) % 2]
                act.wait_ge(vg_mm, count(i, k, UC, t))
                act.activation(v[:, k % 2, t, :], bank[:, 0:2 * DV], ACT.Copy).then_inc(v_out, 1)
                act.activation(gate[:, k % 2, t, :], bank[:, 2 * DV:4 * DV], ACT.Tanh, scale=0.5).then_inc(tanh_done, 1)

            def norm_and_split(m):
                act.wait_ge(shift_done, m + 1)
                if m > 0:
                    act.wait_ge(x_turned, m * KC)
                for n in range(UC):
                    t = m * UC + n
                    act.activation(xn[n], xres[:, t, :], ACT.Identity, bias=shift[:, t:t + 1], scale=rstd[:, t:t + 1]).then_inc(xn_done, 1)
                for kk in range(KC):
                    act.wait_ge(x_turned, m * KC + kk + 1)
                    act.activation(xT_hi[:, kk, m * UNIT:(m + 1) * UNIT], R[(m * KC + kk) % GATHERS][:, :], ACT.Copy).then_inc(x_hi, 1)
            norm_and_split(0)
            q_scale(0, 0)
            norm_and_split(1)
            norm_and_split(2)
            e_exp(0, 0)
            vg_read(0, 0, 0)
            vg_read(0, 0, 1)
            norm_and_split(3)
            vg_read(0, 0, 2)
            vg_read(0, 0, 3)

            def pair(i, last):
                for k in range(UNITS):
                    more = not last or k < UNITS - 1
                    act.wait_ge(e_tr, count(i, k, 1, 0))
                    act.activation(en[:, :, :], R[0][:, :].rearrange("p (a b) -> p a b", a=UC), ACT.Copy).then_inc(en_out, 1)
                    if more:
                        q_scale(i, k + 1)
                    if k == 0:
                        act.wait_ge(wo_mm, count(i, k, UC, 0))
                        hi_piece(i + 1, 4)
                    if k == UNITS - 1 and more:
                        hi_piece(i * (NP * 16) + 9 * 16, 3)
                    act.wait_ge(ok_shifted, count(i, k, 1, 1))
                    act.activation(pv[:, :, :], ok[:, :, :], ACT.Exp).then_inc(pv_done, 1)
                    if more:
                        e_exp(i, k + 1)
                        vg_read(i, k + 1, 0)
                    act.wait_ge(p_tr, count(i, k, 1, 0))
                    act.activation(pT[:, :], R[3][:, :], ACT.Copy).then_inc(p_out, 1)
                    if more:
                        vg_read(i, k + 1, 1)
                    if last and k > 0:
                        act.wait_ge(shift_done, UNITS + k)
                        if k > 1:
                            act.wait_ge(scattered, 16 * UC * (k - 1))
                        for t in range((k - 1) * UC, k * UC):
                            act.activation(rt_xn[t % UC], xres[:, t, :], ACT.Identity, bias=shift[:, t:t + 1], scale=rstd[:, t:t + 1]).then_inc(xn_done, 1)
                    if k == UNITS - 2 and not last:
                        act.wait_ge(s_mm, count(i, k + 1, 1, 0))
                        hi_piece(i * (NP * 16) + 6 * 16, 0)
                    for b in range(2):
                        act.wait_ge(o_mm, count(i, k, 2, b))
                        act.activation(u[:, b, :, :].rearrange("p a d -> p (a d)"), R[b][:, :], ACT.Square).then_inc(squared, 1)
                    if more:
                        vg_read(i, k + 1, 2)
                    if k == UNITS - 2 and not last:
                        hi_piece(i * (NP * 16) + 7 * 16, 1)
                    for b in range(2):
                        if more and b == 1:
                            vg_read(i, k + 1, 3)
                        act.wait_ge(u_tr, count(i, k, 2, b))
                        act.activation(uT_hi[:, b, :, :].rearrange("p h t -> p (h t)"), R[2 + b][:, :], ACT.Copy).then_inc(u_hi, 1)
                    if k == UNITS - 2 and not last:
                        hi_piece(i * (NP * 16) + 8 * 16, 2)
            with act.Fori(0, PAIRS - 1) as i:
                pair(i, False)
            pair(PAIRS - 1, True)

        @block.vector
        def _(dve):
            for s in (k_out, s_clipped, z_done, gate_done, kn_out, rz_done, hk_done, a_masked, ok_scaled, highest_done, ok_shifted,
                      den_done, pz_done, b_masked, hv_done, ss_done, eps_done, ms_done, u_done, u_lo, added):
                dve.sem_inc(s, 1)
            dve.memset(hk[:, :, :], 0.0)
            n_steps = [0]

            def step(ins):
                n_steps[0] += 1
                ins.then_inc(rt_step, 1)
                dve.wait_ge(rt_step, n_steps[0])

            def k_copy(i, k):
                dve.wait_ge(k_mm, count(i, k, 1, 0))
                dve.tensor_copy(kT[:, :], PJ[(7 * k + 1) % 2][:, :]).then_inc(k_out, 1)

            def s_clip(i, k):
                dve.wait_ge(s_mm, count(i, k, 1, 0))
                dve.tensor_scalar(eT[:, k % 2, :], PJ[(7 * k + 2) % 2][:, :], CLAMP, -CLAMP, ALU.min, ALU.max).then_inc(s_clipped, 1)

            def z_scan(i, k):
                dve.wait_ge(e_done, count(i, k, 1, 1))
                first = k % HALVES == 0
                if not first:
                    dve.wait_ge(z_kept, i * (UNITS // HALVES) + k // HALVES + 1)
                dve.tensor_tensor_scan(out=zT[:, :], data0=eT[:, k % 2, :], data1=eT[:, k % 2, :],
                                       initial=0.0 if first else zlast[:, 0:1], op0=ALU.add, op1=ALU.bypass).then_inc(z_done, 1)
                if first:
                    dve.wait_ge(z_done, count(i, k, 1, 1))
                    dve.tensor_copy(zlast[:, :], zT[:, UNIT - 1:UNIT]).then_inc(z_kept, 1)

            def gate_make(i, k, t):
                dve.wait_ge(tanh_done, count(i, k, UC, t + 1))
                dve.scalar_tensor_tensor(out=gate[:, k % 2, t, :], in0=gate[:, k % 2, t, :], scalar=1.0,
                                         in1=PJ[(7 * k + 3 + t) % 2][:, 2 * DV:4 * DV], op0=ALU.add, op1=ALU.mult).then_inc(gate_done, 1)

            def kn_copy(i, k):
                dve.wait_ge(k_tr, count(i, k, 1, 0))
                dve.tensor_copy(kn[:, :, :], R[1][:, :].rearrange("p (a b) -> p a b", a=UC)).then_inc(kn_out, 1)

            def add_rows(m):
                for t in range(m * UC, (m + 1) * UC + 1):
                    if t < (m + 1) * UC:
                        dve.wait_ge(loaded[t % GATHERS], 16 * (t // GATHERS + 1))
                        dve.scalar_tensor_tensor(out=xres[:, t, :], in0=ring[t % GATHERS], scalar=half_weight[:, t:t + 1],
                                                 in1=xres[:, t, :], op0=ALU.mult, op1=ALU.add).then_inc(row_added, 1)
                    if t > m * UC:
                        dve.wait_ge(row_added, t)
                        last = dve.bn_stats(bn[:, (t - 1) % UC, :], xres[:, t - 1, :])
                last.then_inc(bn_done, 1)
                dve.wait_ge(bn_done, m + 1)
                for t in range(m * UC, (m + 1) * UC):
                    last = dve.bn_aggr(mv[:, t, :], bn[:, t % UC, :])
                last.then_inc(mv_done, 1)
                dve.wait_ge(mv_done, m + 1)
                dve.tensor_scalar(nmean[:, tiles(m)], mv[:, tiles(m), 0], -1.0, None, ALU.mult)
                dve.tensor_scalar(vare[:, tiles(m)], mv[:, tiles(m), 1], EPS, None, ALU.add).then_inc(var_ready, 1)

            def split_lo(m):
                for kk in range(KC):
                    dve.wait_ge(x_hi, m * KC + kk + 1)
                    dve.tensor_tensor(xT_lo[:, kk, m * UNIT:(m + 1) * UNIT], R[(m * KC + kk) % GATHERS][:, :],
                                      xT_hi[:, kk, m * UNIT:(m + 1) * UNIT].bitcast(F32), ALU.subtract).then_inc(x_lo, 1)
            add_rows(0)
            add_rows(1)
            split_lo(0)
            add_rows(2)
            k_copy(0, 0)
            split_lo(1)
            s_clip(0, 0)
            add_rows(3)
            gate_make(0, 0, 0)
            split_lo(2)
            z_scan(0, 0)
            gate_make(0, 0, 1)
            split_lo(3)
            gate_make(0, 0, 2)
            gate_make(0, 0, 3)
            kn_copy(0, 0)

            def tile_statistics(i, k, cc):
                dve.wait_ge(added, count(i, k, UC, cc + 1))
                last = dve.bn_stats(bn[:, cc, :], xres[:, k * UC + cc, :])
                if cc == UC - 1:
                    last.then_inc(bn_done, 1)

            def unit_statistics(k):
                dve.wait_ge(bn_done, UNITS + k + 1)
                for t in range(k * UC, (k + 1) * UC):
                    last = dve.bn_aggr(mv[:, t, :], bn[:, t % UC, :])
                last.then_inc(mv_done, 1)
                dve.wait_ge(mv_done, UNITS + k + 1)
                dve.tensor_scalar(nmean[:, tiles(k)], mv[:, tiles(k), 0], -1.0, None, ALU.mult)
                dve.tensor_scalar(vare[:, tiles(k)], mv[:, tiles(k), 1], EPS, None, ALU.add).then_inc(var_ready, 1)

            def pair(i, last_pair):
                for k in range(UNITS):
                    more = not last_pair or k < UNITS - 1
                    first = k % HALVES == 0
                    dve.wait_ge(z_tr, count(i, k, 1, 0))
                    dve.reciprocal(rz[:, :, :], R[2][:, :].rearrange("p (a b) -> p a b", a=UC)).then_inc(rz_done, 1)
                    dve.wait_ge(dk_mm, count(i, k, 1, 0))
                    for cc in range(UC if first else UC - 1):
                        to = (cc + 1) % UC
                        for h in range(2):
                            rows, cols = slice(64 * h, 64 * h + 64), slice(64 * h, 64 * h + 64)
                            part = R[5][rows, cc * P + 64 * h:cc * P + 64 * h + 64]
                            if first and cc == 0:
                                last = dve.tensor_copy(hk[rows, to, cols], part)
                            else:
                                last = dve.tensor_tensor(hk[rows, to, cols], part, hk[rows, cc, cols], ALU.add)
                        last.then_inc(hk_done, 1)
                        dve.wait_ge(hk_done, i * HK_AT[UNITS] + HK_AT[k] + cc + 2)
                    for b in range(2):
                        dve.wait_ge(a_mm, count(i, k, 2, b))
                        dve.tensor_tensor(am[:, b, :, :],
                                          R[3 + b][:, :].rearrange("p (a t) -> p a t", a=4),
                                          c["causal"][:, :].rearrange("p (a t) -> p a t", a=1).to_broadcast([P, 4, P]), ALU.mult).then_inc(a_masked, 1)
                    if more:
                        k_copy(i, k + 1)
                    dve.wait_ge(ok_mm, count(i, k, 1, 0))
                    dve.wait_ge(rz_done, count(i, k, 1, 1))
                    dve.tensor_tensor(ok[:, :, :], R[2][:, :].rearrange("p (a b) -> p a b", a=UC), rz[:, :, :], ALU.mult).then_inc(ok_scaled, 1)
                    dve.wait_ge(ok_scaled, count(i, k, 1, 1))
                    by_head = lambda x: x[:, :, :].rearrange("p a (h m) -> p (a h) m", h=2)
                    spread = lambda x: x[:, :].rearrange("p (a b) -> p a b", b=1).to_broadcast([P, 2 * UC, M])
                    dve.tensor_reduce(highest[:, :], by_head(ok), op=ALU.max, axis=AX.X).then_inc(highest_done, 1)
                    dve.wait_ge(highest_done, count(i, k, 1, 1))
                    dve.tensor_tensor(by_head(ok), by_head(ok), spread(highest), ALU.subtract).then_inc(ok_shifted, 1)
                    dve.wait_ge(pv_done, count(i, k, 1, 1))
                    dve.tensor_tensor(ok[:, :, :], pv[:, :, :], rz[:, :, :], ALU.mult).then_inc(pz_done, 1)
                    if more:
                        s_clip(i, k + 1)
                    dve.tensor_reduce(den[:, :], pv[:, :, :].rearrange("p a (h m) -> p h a m", h=2), op=ALU.add, axis=AX.X).then_inc(den_done, 1)
                    if more:
                        gate_make(i, k + 1, 0)
                    dve.wait_ge(den_done, count(i, k, 1, 1))
                    dve.scalar_tensor_tensor(out=ms[:, :], in0=den[:, :], scalar=4.0 * EPS, in1=den[:, :], op0=ALU.mult, op1=ALU.mult).then_inc(eps_done, 1)
                    if last_pair and k > 0:
                        for cc in range(UC):
                            tile_statistics(i, k - 1, cc)
                        unit_statistics(k - 1)
                    for b in range(2):
                        dve.wait_ge(b_mm, count(i, k, 2, b))
                        dve.tensor_tensor(am[:, b, :, :],
                                          R[4 + b][:, :].rearrange("p (a t) -> p a t", a=4),
                                          c["causal"][:, :].rearrange("p (a t) -> p a t", a=1).to_broadcast([P, 4, P]), ALU.mult).then_inc(b_masked, 1)
                    for cc in range(UC if first else UC - 1):
                        to = (cc + 1) % UC
                        if cc % 2 == 0:
                            dve.wait_ge(dv_mm, count(i, k, 2, cc // 2))
                        part = R[2 + cc // 2][:, (cc % 2) * 2 * DV:(cc % 2 + 1) * 2 * DV]
                        if first and cc == 0:
                            last = dve.tensor_copy(hv[:, to, :], part)
                        else:
                            last = dve.tensor_tensor(hv[:, to, :], part, hv[:, cc, :], ALU.add)
                        last.then_inc(hv_done, 1)
                        dve.wait_ge(hv_done, i * HK_AT[UNITS] + HK_AT[k] + cc + 2)
                    if more:
                        gate_make(i, k + 1, 1)
                        z_scan(i, k + 1)
                    if last_pair and k > 0:
                        for t in range((k - 1) * UC, k * UC):
                            dve.wait_ge(xn_done, TOK // P + t + 1)
                            last = dve.tensor_tensor_reduce(out=rt_spare[t % UC], in0=rt_xn[t % UC], in1=norms["wdiff"][:], scale=1.0, scalar=0.0,
                                                            op0=ALU.mult, op1=ALU.add, accum_out=routing["gap"][:, t:t + 1])
                        step(last)
                        choose(dve, step, routing, tiles(k - 1), is1_done)
                    dve.wait_ge(eps_done, count(i, k, 1, 1))
                    for b in range(2):
                        cols = slice(4 * b, 4 * b + 4)
                        dve.wait_ge(squared, count(i, k, 2, b + 1))
                        dve.tensor_reduce(ss[:, cols], u[:, b, :, :], op=ALU.add, axis=AX.X).then_inc(ss_done, 1)
                        dve.wait_ge(ss_done, count(i, k, 2, b + 1))
                        dve.scalar_tensor_tensor(out=ms[:, cols], in0=ss[:, cols], scalar=4.0 / DV, in1=ms[:, cols], op0=ALU.mult, op1=ALU.add).then_inc(ms_done, 1)
                    dve.wait_ge(coef_done, count(i, k, 2, 2))
                    for b in range(2):
                        for cc, h in ((2 * b, 0), (2 * b, 1), (2 * b + 1, 0), (2 * b + 1, 1)):
                            last = dve.scalar_tensor_tensor(out=u[:, h, cc, :], in0=R[h][:, cc * P:(cc + 1) * P], scalar=coef[:, 4 * h + cc:4 * h + cc + 1],
                                                            in1=gate[:, k % 2, cc, h * DV:(h + 1) * DV], op0=ALU.mult, op1=ALU.mult)
                        last.then_inc(u_done, 1)
                    if last_pair and k > 0:
                        place(dve, step, routing, tiles(k - 1), rt_later, rt_total, rank_mm, 2 * k, rows_ready)
                    for b in range(2):
                        if more and b == 1:
                            gate_make(i, k + 1, 2)
                        dve.wait_ge(u_hi, count(i, k, 2, b + 1))
                        dve.tensor_tensor(uT_lo[:, b, :, :].rearrange("p h t -> p (h t)"), R[2 + b][:, :],
                                          uT_hi[:, b, :, :].rearrange("p h t -> p (h t)").bitcast(F32), ALU.subtract).then_inc(u_lo, 1)
                    if more:
                        gate_make(i, k + 1, 3)
                        kn_copy(i, k + 1)
                    for cc in range(UC):
                        dve.wait_ge(wo_mm, count(i, k, UC, cc + 1))
                        dve.tensor_tensor(xres[:, k * UC + cc, :], R[4 + cc % 2][:, :], xres[:, k * UC + cc, :], ALU.add).then_inc(added, 1)
                        if not more:
                            tile_statistics(i, k, cc)
                    if not more:
                        unit_statistics(k)
            with dve.Fori(0, PAIRS - 1) as i:
                pair(i, False)
            pair(PAIRS - 1, True)

        @block.tensor
        def _(pe):
            parts = ((w_lo, xT_hi), (w_hi, xT_lo), (w_hi, xT_hi))

            def turned(i, k, part, done, fresh=False):
                tok = slice((k % UNITS) * UNIT, (k % UNITS + 1) * UNIT)
                for kk in range(KC):
                    if fresh:
                        pe.wait_ge(x_lo, kk + 1)
                    for n, (w, x) in enumerate(parts):
                        last = pe.matmul(PJ[(7 * k + part) % 2][:, :], wq(w, kk, part), x[:, kk, tok],
                                         start=(kk == 0 and n == 0), stop=(kk == KC - 1 and n == 2))
                last.then_inc(done, 1)

            def project_q(i, k):
                pe.wait_ge(gate_done, count(i, k, UC, -1))
                turned(i, k, 0, q_mm)

            def project_k(i, k):
                pe.wait_ge(gate_done, count(i, k, UC, 0))
                turned(i, k, 1, k_mm)

            def project_s(i, k):
                pe.wait_ge(q_out, count(i, k, 1, 1))
                turned(i, k, 2, s_mm)

            def project_vg(i, k, t):
                if t == 0:
                    pe.wait_ge(k_out, count(i, k, 1, 1))
                elif t == 1:
                    pe.wait_ge(s_clipped, count(i, k, 1, 1))
                else:
                    pe.wait_ge(gate_done, count(i, k, UC, t - 1))
                tok = slice((k % UNITS) * UNIT + t * P, (k % UNITS) * UNIT + (t + 1) * P)
                for kk in range(KC):
                    for n, (w, x) in enumerate(parts):
                        last = pe.matmul(PJ[(7 * k + 3 + t) % 2][:, :], x[:, kk, tok], wvg(w, kk),
                                         start=(kk == 0 and n == 0), stop=(kk == KC - 1 and n == 2))
                last.then_inc(vg_mm, 1)
            pe.sem_inc(wo_mm, 1)

            def turn(m):
                for n in range(m * KC, (m + 1) * KC):
                    if n >= GATHERS:
                        pe.wait_ge(x_lo, n - GATHERS + 1)
                for t in range(UC):
                    pe.wait_ge(xn_done, m * UC + t + 1)
                    for kk in range(KC):
                        last = pe.transpose(R[(m * KC + kk) % GATHERS][:, t * P:(t + 1) * P], xn[t][:, kk * P:(kk + 1) * P], c["ident"][:])
                        if t == UC - 1:
                            last.then_inc(x_turned, 1)
            turn(0)
            turned(0, 0, 0, q_mm, fresh=True)
            turned(0, 0, 1, k_mm)
            turn(1)
            project_s(0, 0)
            project_vg(0, 0, 0)
            turn(2)
            project_vg(0, 0, 1)
            turn(3)
            project_vg(0, 0, 2)
            project_vg(0, 0, 3)
            pe.wait_ge(x_lo, UNITS * KC)

            chunk = lambda cc: slice(cc * P, (cc + 1) * P)
            half = lambda h: slice(64 * h, 64 * h + 64)

            def turn_ek(i, k):
                pe.wait_ge(e_done, count(i, k, 1, 1))
                for cc in range(UC):
                    last = pe.transpose(R[0][:, chunk(cc)], eT[:, k % 2, chunk(cc)], c["ident"][:])
                last.then_inc(e_tr, 1)
                pe.wait_ge(k_out, count(i, k, 1, 1))
                for cc in range(UC):
                    last = pe.transpose(R[1][:, chunk(cc)], kT[:, chunk(cc)], c["ident"][:])
                last.then_inc(k_tr, 1)
            turn_ek(0, 0)

            def pair(i, last_pair):
                for k in range(UNITS):
                    more = not last_pair or k < UNITS - 1
                    first = k % HALVES == 0
                    b2 = k % 2
                    pe.wait_ge(z_done, count(i, k, 1, 1))
                    pe.wait_ge(u_lo, count(i, k, 2, 0))
                    for cc in range(UC):
                        last = pe.transpose(R[2][:, chunk(cc)], zT[:, chunk(cc)], c["ident"][:])
                    last.then_inc(z_tr, 1)
                    if k == UNITS - 1 and more:
                        pe.wait_ge(piece_lo, i * NP + 1 + 7)
                    if more:
                        project_q(i, k + 1)
                    pe.wait_ge(en_out, count(i, k, 1, 1))
                    pe.wait_ge(kn_out, count(i, k, 1, 1))
                    pe.wait_ge(added, count(i, k, UC, 0))
                    for cc in range(UC if first else UC - 1):
                        last = pe.matmul(R[5][:, chunk(cc)], kn[:, cc, :], en[:, cc, :], start=True, stop=True)
                    last.then_inc(dk_mm, 1)
                    pe.wait_ge(q_out, count(i, k, 1, 1))
                    for cc in range(UC):
                        for h in range(2):
                            last = pe.matmul(R[3 + h][:, chunk(cc)], kT[half(h), chunk(cc)], qT[half(h), b2, chunk(cc)], start=True, stop=True)
                            if cc == UC - 1:
                                last.then_inc(a_mm, 1)
                    if more:
                        project_k(i, k + 1)
                    pe.wait_ge(rz_done, count(i, k, 1, 1))
                    pe.wait_ge(hk_done, i * HK_AT[UNITS] + HK_AT[k + 1] + 1)
                    pe.wait_ge(a_masked, count(i, k, 2, 2))
                    for cc in range(UC):
                        state = not (first and cc == 0)
                        if state:
                            pe.matmul(R[2][:, chunk(cc)], qT[:, b2, chunk(cc)], hk[:, cc, :], start=True, stop=False, skip_group_check=True)
                        for h in range(2):
                            last = pe.matmul(R[2][:, cc * P + 64 * h:cc * P + 64 * h + 64], am[:, h, cc, :], en[:, cc, half(h)],
                                             start=not state, stop=True, skip_group_check=True)
                    last.then_inc(ok_mm, 1)
                    if more:
                        project_s(i, k + 1)
                    if k == UNITS - 1 and more:
                        pe.wait_ge(piece_lo, i * NP + 1 + 9)
                    if more:
                        project_vg(i, k + 1, 0)
                    pe.wait_ge(pz_done, count(i, k, 1, 1))
                    for cc in range(UC):
                        last = pe.transpose(R[3][:, chunk(cc)], ok[:, cc, :], c["ident"][:])
                    last.then_inc(p_tr, 1)
                    if more:
                        project_vg(i, k + 1, 1)
                    pe.wait_ge(p_out, count(i, k, 1, 1))
                    for cc in range(UC):
                        for h in range(2):
                            last = pe.matmul(R[4 + h][:, chunk(cc)], eT[half(h), b2, chunk(cc)], pT[half(h), chunk(cc)], start=True, stop=True)
                            if cc == UC - 1:
                                last.then_inc(b_mm, 1)
                    pe.wait_ge(v_out, count(i, k, UC, UC))
                    for b in range(2):
                        for a in range(2 if first or b == 0 else 1):
                            cc = 2 * b + a
                            last = pe.matmul(R[2 + b][:, a * 2 * DV:(a + 1) * 2 * DV], en[:, cc, :], v[:, b2, cc, :], start=True, stop=True)
                        last.then_inc(dv_mm, 1)
                    for h in range(2):
                        pe.wait_ge(b_masked, count(i, k, 2, h + 1))
                        for cc in range(UC):
                            last = pe.matmul(R[h][:, chunk(cc)], am[:, h, cc, :], v[:, b2, cc, h * DV:(h + 1) * DV],
                                             start=(cc == 0), stop=(first and cc == 0), skip_group_check=True)
                    pe.wait_ge(hv_done, i * HK_AT[UNITS] + HK_AT[k + 1] + 1)
                    for h in range(2):
                        for cc in range(1 if first else 0, UC):
                            last = pe.matmul(R[h][:, chunk(cc)], pT[half(h), chunk(cc)], hv[half(h), cc, h * DV:(h + 1) * DV],
                                             start=False, stop=True, skip_group_check=True)
                        last.then_inc(o_mm, 1)
                    if more:
                        project_vg(i, k + 1, 2)
                        project_vg(i, k + 1, 3)
                    if last_pair and k > 0:
                        pe.wait_ge(is1_done, k)
                        pe.matmul(rt_later, c["later"][:], routing["is1"][:, tiles(k - 1)], start=True, stop=True).then_inc(rank_mm, 1)
                        pe.matmul(rt_total, c["ones"][:], routing["is1"][:, tiles(k - 1)], start=True, stop=True).then_inc(rank_mm, 1)
                    for b in range(2):
                        pe.wait_ge(u_done, count(i, k, 2, b + 1))
                        for h in range(2):
                            for a in range(2):
                                last = pe.transpose(R[2 + b][:, (2 * h + a) * P:(2 * h + a + 1) * P], u[:, h, 2 * b + a, :], c["ident"][:])
                        last.then_inc(u_tr, 1)
                    if more:
                        turn_ek(i, k + 1)
                    if k == 0:
                        pe.wait_ge(piece_lo, i * NP + 1 + 5)
                    for cc in range(UC):
                        if cc % 2 == 0:
                            pe.wait_ge(u_lo, count(i, k, 2, cc // 2 + 1))
                        if cc >= 2:
                            pe.wait_ge(added, count(i, k, UC, cc - 1))
                        for h in range(2):
                            for n, (x, w) in enumerate(((uT_lo, w_hi), (uT_hi, w_lo), (uT_hi, w_hi))):
                                last = pe.matmul(R[4 + cc % 2][:, :], x[:, cc // 2, h, (cc % 2) * P:(cc % 2 + 1) * P], wo(w, h),
                                                 start=(h == 0 and n == 0), stop=(h == 1 and n == 2))
                        last.then_inc(wo_mm, 1)
            with pe.Fori(0, PAIRS - 1) as i:
                pair(i, False)
            pair(PAIRS - 1, True)


def macaron(nc, x, wff, router, watt, gnorm, out):
    sorted_rows = nc.dram_tensor("sorted_rows", [TOK, D], F32, kind="Internal").ap()
    sorted_marks = nc.dram_tensor("sorted_marks", [TOK, 2], F32, kind="Internal").ap()
    slot_rows = nc.dram_tensor("slot_rows", [TOK + BLOCK, D], F32, kind="Internal").ap()
    with ExitStack() as top:
        sb = lambda n, s, d=F32: top.enter_context(nc.sbuf_tensor(n, s, d))
        c = phase_constants(nc, top)
        xres = sb("xres", [P, TILES, D])
        norms = {"mv": sb("mv", [P, TILES, 2])}
        for n in ("vare", "nmean", "rstd", "shift"):
            norms[n] = sb(n, [P, TILES])
        norms["wdiff"] = sb("wdiff", [P, D])
        routing = {n: sb("rt_" + n, [P, TILES], I32 if n == "row_i" else F32) for n in (
            "gap", "is1", "cum", "zero", "tok", "rest", "base", "behind", "pos", "row_i")}
        routing["slot"] = sb("rt_slot", [P, BLOCKS])
        aw = {"stage": sb("at_stage", [P, PIECE]),
              "hi": sb("at_w_hi", [P, QKS + VG + WO], F32R), "lo": sb("at_w_lo", [P, QKS + VG + WO], F32R)}
        for n in ("piece_loaded", "piece_hi", "piece_lo"):
            aw[n] = top.enter_context(nc.semaphore("at_" + n))
        loaded = [top.enter_context(nc.semaphore(f"loaded{n}")) for n in range(GATHERS)]
        half_weight = sb("half_weight", [P, TILES])
        gather_row = sb("gather_row", [P, TILES], I32)
        slot_table = sb("slot_table", [P, 2, 8], I32)

        def feed_forward(tag, x_in, *to_out):
            phase_feed_forward(nc, top, tag, c, x_in, router, wff, watt, xres, norms, routing, aw, half_weight, gather_row, slot_table,
                               sorted_rows, slot_rows, *to_out)
        feed_forward("first_", x)
        phase_attention(nc, top, c, watt, gnorm, slot_rows, gather_row, half_weight, xres, norms, routing, loaded, sorted_rows, aw)
        feed_forward("last_", None, loaded, sorted_marks, out)


def kernel(**inputs):
    import numpy as np
    import concourse.bacc as bacc
    from concourse.bass_utils import run_bass_kernel_spmd

    get = lambda name: np.asarray(inputs[name])
    x = get("L0_attn_hidden_states")
    up = get("L0_ffn_w_fc").reshape(EXPERTS, HT, P, KC, P).transpose(0, 1, 4, 3, 2).reshape(EXPERTS * HT, P, D)
    down = get("L0_ffn_w_proj").reshape(EXPERTS, D, HT, P).transpose(0, 2, 3, 1).reshape(EXPERTS * HT, P, D)

    def pair_columns(w, width):
        return w.reshape(KC, P, PAIRS, 2 * width).transpose(2, 1, 0, 3)
    qks = np.concatenate([pair_columns(get("L0_attn_" + n), d) for n, d in (("Wq", DK), ("Wk", DK), ("Ws", M))], axis=3)
    vg = np.concatenate([pair_columns(get("L0_attn_" + n), DV) for n in ("Wv", "Wg")], axis=3)
    wo = get("L0_attn_Wo").reshape(PAIRS, 2, DV, D).transpose(0, 2, 1, 3)
    arrays = {
        "x": x.reshape(TOK, D),
        "wff": np.concatenate([up, down], axis=2),
        "router": get("L0_ffn_w_router"),
        "watt": np.concatenate([a.reshape(PAIRS, P, -1) for a in (qks, vg, wo)], axis=2),
        "gnorm": get("L0_attn_g_norm_weight").reshape(DV, 1),
    }
    arrays = {n: np.ascontiguousarray(a) for n, a in arrays.items()}
    nc = bacc.Bacc("TRN2", target_bir_lowering=False, num_devices=1)
    args = [nc.dram_tensor(n, a.shape, mybir.dt.from_np(a.dtype), kind="ExternalInput").ap() for n, a in arrays.items()]
    out = nc.dram_tensor("out", [TOK, D], F32, kind="ExternalOutput").ap()
    macaron(nc, *args, out)
    result = run_bass_kernel_spmd(nc, [arrays], core_ids=[0])
    return result.results[0]["out"].reshape(x.shape)
```
